# Optimizing a Trainium2 kernel written in Bass

```python
import numpy as np
import jax
import jax.numpy as jnp

def _softmax(x, axis=-1):
    return jax.nn.softmax(x, axis=axis)

def _gelu(x):
    return jax.nn.gelu(x, approximate=True)

def _silu(x):
    return jax.nn.silu(x)

def _sigmoid(x):
    return jax.nn.sigmoid(x)

def _layernorm(x, axis=-1, eps=1e-05):
    m = jnp.mean(x, axis=axis, keepdims=True)
    v = jnp.var(x, axis=axis, keepdims=True)
    return (x - m) / jnp.sqrt(v + eps)

def _scatter_add(tgt, idx, src, axis=0):
    return tgt.at[idx].add(src)

def _segment_sum(src, seg, n):
    return jax.ops.segment_sum(src, seg, n)
kernel_name = 'mk_decoder_preln_d1_seqx_r4_6ab490'

def setup_inputs(seed: int=0):
    np.random.seed(seed)
    _w = jnp.asarray

    def _rec_inputs():
        import jax
        import jax.numpy as jnp
        _rk = jax.random.key(seed)
        x = 7.22e-05 + 1 * jax.random.normal(jax.random.fold_in(_rk, 1), (8, 256, 512), jnp.float32)
        _lenS = 256 - jax.random.randint(jax.random.fold_in(_rk, 7), (8,), 0, max(1, 256 // 4) + 1, jnp.int32)
        _lenS2 = 256 - jax.random.randint(jax.random.fold_in(_rk, 8), (8,), 0, max(1, 256 // 4) + 1, jnp.int32)
        _ctx_2048P = jax.random.normal(jax.random.fold_in(_rk, 11), (8, 16, 512), jnp.float32)
        _ctx_2048c = jax.random.dirichlet(jax.random.fold_in(_rk, 511), 0.3 * jnp.ones((16,), jnp.float32), (8, 256))
        _ctx_2048t = jnp.einsum('bsk,bkd->bsd', _ctx_2048c, _ctx_2048P)
        _ctx_2048t = _ctx_2048t * jax.lax.rsqrt(jnp.mean(jnp.square(_ctx_2048t)) + 1e-12) * 0.953939
        ctx_2048 = 4.13588e-05 + 0.999923 * (_ctx_2048t + 0.3 * jax.random.normal(jax.random.fold_in(_rk, 611), (8, 256, 512), jnp.float32))
        return (x, ctx_2048)
    x, ctx_2048 = _rec_inputs()

    def _L0_attn_setup():
        import jax, jax.numpy as jnp
        import numpy as np
        DIM = 512
        HEADS = 16
        HEAD_DIM = DIM // HEADS
        key = jax.random.key(seed)
        k1, k2, k3 = jax.random.split(key, 3)
        x = jax.random.normal(k1, (4, 512, DIM), dtype=jnp.float32)
        w_qkv = jax.random.normal(k2, (3 * DIM, DIM), dtype=jnp.float32) * DIM ** (-0.5)
        w_out = jax.random.normal(k3, (DIM, DIM), dtype=jnp.float32) * DIM ** (-0.5)
        return {'x': x, 'w_qkv': w_qkv, 'w_out': w_out}
    _L0_attn_all = _L0_attn_setup()
    _L0_attn_in = {k: v for k, v in _L0_attn_all.items() if k in ('w_qkv', 'w_out')}
    del _L0_attn_all

    def _L0_xattn_setup():
        import jax, jax.numpy as jnp
        import numpy as np
        B, D, N, H = (4, 256, 512, 16)
        HD = D // H

        def rotate_half(x):
            x1 = x[..., 0::2]
            x2 = x[..., 1::2]
            return jnp.stack((-x2, x1), axis=-1).reshape(x.shape)

        def apply_cached_rotary_emb(freqs, t):
            return t * freqs[0] + rotate_half(t) * freqs[1]
        key = jax.random.key(seed)
        ks = jax.random.split(key, 13)
        s = 1.0 / np.sqrt(D)
        inp = {'query': jax.random.normal(ks[0], (B, D, N), jnp.float32), 'key': jax.random.normal(ks[1], (B, D, N), jnp.float32), 'value': jax.random.normal(ks[2], (B, D, N), jnp.float32), 'encoding': jax.random.normal(ks[3], (2, 1, 1, N, HD), jnp.float32), 'Wq': jax.random.normal(ks[4], (D, D), jnp.float32) * s, 'bq': jax.random.normal(ks[5], (D,), jnp.float32) * s, 'Wk': jax.random.normal(ks[6], (D, D), jnp.float32) * s, 'bk': jax.random.normal(ks[7], (D,), jnp.float32) * s, 'Wv': jax.random.normal(ks[8], (D, D), jnp.float32) * s, 'bv': jax.random.normal(ks[9], (D,), jnp.float32) * s, 'Wm': jax.random.normal(ks[10], (D, D), jnp.float32) * s, 'bm': jax.random.normal(ks[11], (D,), jnp.float32) * s}
        return inp
    _L0_xattn_all = _L0_xattn_setup()
    _L0_xattn_in = {k: v for k, v in _L0_xattn_all.items() if k in ('encoding', 'Wq', 'bq', 'Wk', 'bk', 'Wv', 'bv', 'Wm', 'bm')}
    del _L0_xattn_all

    def _L0_ffn_setup():
        import jax, jax.numpy as jnp
        import numpy as np
        DIM = 512
        INTER = 352
        E = 16
        TOPK = 4
        G = 4
        TOPK_G = 2
        N_SHARED = 2
        SHARED_INTER = N_SHARED * INTER
        ROUTE_SCALE = 1.0

        def _moe_forward(x, Wg, W1, W3, W2, Ws1, Ws3, Ws2):
            B, S, D = x.shape
            xt = x.reshape(-1, D)
            T = xt.shape[0]
            scores = jax.nn.softmax(xt @ Wg.T, axis=-1)
            sg = scores.reshape(T, G, E // G)
            group_scores = sg.max(axis=-1)
            gidx = jax.lax.top_k(group_scores, TOPK_G)[1]
            gmask = jax.nn.one_hot(gidx, G, dtype=jnp.float32).sum(axis=1) > 0
            masked = jnp.where(gmask[:, :, None], sg, -jnp.inf).reshape(T, E)
            topi = jax.lax.top_k(masked, TOPK)[1]
            weights = jnp.take_along_axis(scores, topi, axis=1) * ROUTE_SCALE
            combine = jnp.zeros((T, E), xt.dtype).at[jnp.arange(T)[:, None], topi].add(weights)
            h = jax.nn.silu(jnp.einsum('td,eid->eti', xt, W1)) * jnp.einsum('td,eid->eti', xt, W3)
            expert_out = jnp.einsum('eti,edi->etd', h, W2)
            y = jnp.einsum('etd,te->td', expert_out, combine)
            z = jax.nn.silu(xt @ Ws1.T) * (xt @ Ws3.T) @ Ws2.T
            return (y + z).reshape(B, S, D)
        key = jax.random.key(seed)
        ks = jax.random.split(key, 8)
        s = 0.02
        x = jax.random.normal(ks[0], (1, 512, DIM), dtype=jnp.float32)
        Wg = jax.random.normal(ks[1], (E, DIM), dtype=jnp.float32) * s
        W1 = jax.random.normal(ks[2], (E, INTER, DIM), dtype=jnp.float32) * s
        W3 = jax.random.normal(ks[3], (E, INTER, DIM), dtype=jnp.float32) * s
        W2 = jax.random.normal(ks[4], (E, DIM, INTER), dtype=jnp.float32) * s
        Ws1 = jax.random.normal(ks[5], (SHARED_INTER, DIM), dtype=jnp.float32) * s
        Ws3 = jax.random.normal(ks[6], (SHARED_INTER, DIM), dtype=jnp.float32) * s
        Ws2 = jax.random.normal(ks[7], (DIM, SHARED_INTER), dtype=jnp.float32) * s
        return {'x': x, 'Wg': Wg, 'W1': W1, 'W3': W3, 'W2': W2, 'Ws1': Ws1, 'Ws3': Ws3, 'Ws2': Ws2}
    _L0_ffn_all = _L0_ffn_setup()
    _L0_ffn_in = {k: v for k, v in _L0_ffn_all.items() if k in ('Wg', 'W1', 'W3', 'W2', 'Ws1', 'Ws3', 'Ws2')}
    del _L0_ffn_all
    return {'x': x, 'ctx_2048': ctx_2048, 'L0_attn_w_qkv': _L0_attn_in['w_qkv'], 'L0_attn_w_out': _L0_attn_in['w_out'], 'L0_xattn_encoding': _L0_xattn_in['encoding'], 'L0_xattn_Wq': _L0_xattn_in['Wq'], 'L0_xattn_bq': _L0_xattn_in['bq'], 'L0_xattn_Wk': _L0_xattn_in['Wk'], 'L0_xattn_bk': _L0_xattn_in['bk'], 'L0_xattn_Wv': _L0_xattn_in['Wv'], 'L0_xattn_bv': _L0_xattn_in['bv'], 'L0_xattn_Wm': _L0_xattn_in['Wm'], 'L0_xattn_bm': _L0_xattn_in['bm'], 'L0_ffn_Wg': _L0_ffn_in['Wg'], 'L0_ffn_W1': _L0_ffn_in['W1'], 'L0_ffn_W3': _L0_ffn_in['W3'], 'L0_ffn_W2': _L0_ffn_in['W2'], 'L0_ffn_Ws1': _L0_ffn_in['Ws1'], 'L0_ffn_Ws3': _L0_ffn_in['Ws3'], 'L0_ffn_Ws2': _L0_ffn_in['Ws2']}

def reference(x, ctx_2048, L0_attn_w_qkv, L0_attn_w_out, L0_xattn_encoding, L0_xattn_Wq, L0_xattn_bq, L0_xattn_Wk, L0_xattn_bk, L0_xattn_Wv, L0_xattn_bv, L0_xattn_Wm, L0_xattn_bm, L0_ffn_Wg, L0_ffn_W1, L0_ffn_W3, L0_ffn_W2, L0_ffn_Ws1, L0_ffn_Ws3, L0_ffn_Ws2):
    import jax
    import jax.numpy as jnp

    def _L0_attn_ref(x, w_qkv, w_out):
        import jax, jax.numpy as jnp
        import numpy as np
        DIM = 512
        HEADS = 16
        HEAD_DIM = DIM // HEADS
        b, s, d = x.shape
        qkv = jnp.einsum('bsd,ed->bse', x, w_qkv)
        qkv = qkv.reshape(b, s, 3, HEADS, HEAD_DIM)
        q, k, v = (qkv[:, :, 0], qkv[:, :, 1], qkv[:, :, 2])
        scale = HEAD_DIM ** (-0.5)
        scores = jnp.einsum('bqhd,bkhd->bhqk', q, k) * scale
        causal = jnp.tril(jnp.ones((s, s), dtype=bool))
        scores = jnp.where(causal, scores, -jnp.inf)
        attn = jax.nn.softmax(scores, axis=-1)
        y = jnp.einsum('bhqk,bkhd->bqhd', attn, v).reshape(b, s, d)
        return jnp.einsum('bsd,ed->bse', y, w_out)

    def _L0_xattn_ref(query, key, value, encoding, Wq, bq, Wk, bk, Wv, bv, Wm, bm):
        import jax, jax.numpy as jnp
        import numpy as np
        B, D, N, H = (4, 256, 512, 16)
        HD = D // H

        def rotate_half(x):
            x1 = x[..., 0::2]
            x2 = x[..., 1::2]
            return jnp.stack((-x2, x1), axis=-1).reshape(x.shape)

        def apply_cached_rotary_emb(freqs, t):
            return t * freqs[0] + rotate_half(t) * freqs[1]
        b, d_model, n = query.shape

        def proj(W, bias, x):
            return jnp.einsum('oi,bin->bon', W, x) + bias[None, :, None]
        q = proj(Wq, bq, query).reshape(b, HD, H, n)
        k = proj(Wk, bk, key).reshape(b, HD, H, n)
        v = proj(Wv, bv, value).reshape(b, HD, H, n)
        q = jnp.transpose(apply_cached_rotary_emb(encoding, jnp.transpose(q, (0, 2, 3, 1))), (0, 3, 1, 2))
        k = jnp.transpose(apply_cached_rotary_emb(encoding, jnp.transpose(k, (0, 2, 3, 1))), (0, 3, 1, 2))
        scores = jnp.einsum('bdhn,bdhm->bhnm', q, k) / np.float32(np.sqrt(HD))
        prob = jax.nn.softmax(scores, axis=-1)
        x = jnp.einsum('bhnm,bdhm->bdhn', prob, v)
        out = jnp.einsum('oi,bin->bon', Wm, x.reshape(b, d_model, n)) + bm[None, :, None]
        return out

    def _L0_ffn_ref(x, Wg, W1, W3, W2, Ws1, Ws3, Ws2):
        import jax, jax.numpy as jnp
        import numpy as np
        DIM = 512
        INTER = 352
        E = 16
        TOPK = 4
        G = 4
        TOPK_G = 2
        N_SHARED = 2
        SHARED_INTER = N_SHARED * INTER
        ROUTE_SCALE = 1.0

        def _moe_forward(x, Wg, W1, W3, W2, Ws1, Ws3, Ws2):
            B, S, D = x.shape
            xt = x.reshape(-1, D)
            T = xt.shape[0]
            scores = jax.nn.softmax(xt @ Wg.T, axis=-1)
            sg = scores.reshape(T, G, E // G)
            group_scores = sg.max(axis=-1)
            gidx = jax.lax.top_k(group_scores, TOPK_G)[1]
            gmask = jax.nn.one_hot(gidx, G, dtype=jnp.float32).sum(axis=1) > 0
            masked = jnp.where(gmask[:, :, None], sg, -jnp.inf).reshape(T, E)
            topi = jax.lax.top_k(masked, TOPK)[1]
            weights = jnp.take_along_axis(scores, topi, axis=1) * ROUTE_SCALE
            combine = jnp.zeros((T, E), xt.dtype).at[jnp.arange(T)[:, None], topi].add(weights)
            h = jax.nn.silu(jnp.einsum('td,eid->eti', xt, W1)) * jnp.einsum('td,eid->eti', xt, W3)
            expert_out = jnp.einsum('eti,edi->etd', h, W2)
            y = jnp.einsum('etd,te->td', expert_out, combine)
            z = jax.nn.silu(xt @ Ws1.T) * (xt @ Ws3.T) @ Ws2.T
            return (y + z).reshape(B, S, D)
        return _moe_forward(x, Wg, W1, W3, W2, Ws1, Ws3, Ws2)
    x = x + _L0_attn_ref(_layernorm(x, axis=-1), L0_attn_w_qkv, L0_attn_w_out)
    x = x + _L0_xattn_ref(_layernorm(x, axis=-1), ctx_2048, ctx_2048, L0_xattn_encoding, L0_xattn_Wq, L0_xattn_bq, L0_xattn_Wk, L0_xattn_bk, L0_xattn_Wv, L0_xattn_bv, L0_xattn_Wm, L0_xattn_bm)
    x = x + _L0_ffn_ref(_layernorm(x, axis=-1), L0_ffn_Wg, L0_ffn_W1, L0_ffn_W3, L0_ffn_W2, L0_ffn_Ws1, L0_ffn_Ws3, L0_ffn_Ws2)
    return x

_drawn_inputs = setup_inputs


def setup_inputs(seed=0):
    import zlib

    import numpy as np

    out = dict(_drawn_inputs(seed))
    spreads = {}
    factors = {'L0_ffn_Wg': 8.0,
     'L0_ffn_W1': 7.805,
     'L0_ffn_W3': 7.702,
     'L0_ffn_W2': 7.673,
     'L0_xattn_bv': 36.546,
     'L0_xattn_bm': 38.441,
     'L0_ffn_Ws1': 8.0,
     'L0_ffn_Ws3': 8.0,
     'L0_ffn_Ws2': 8.0}
    for name, (base, spread) in spreads.items():
        noise = np.random.default_rng([zlib.crc32(name.encode()), seed]).standard_normal(out[name].shape)
        drawn = base * np.exp(spread * noise) if base else spread * noise
        out[name] = jnp.asarray(drawn.astype(out[name].dtype))
    for name, factor in factors.items():
        out[name] = (out[name] * factor).astype(out[name].dtype)
    return out
```

```python
import concourse.bass as bass
from concourse import mybir
from contextlib import ExitStack

P = 128
B, S, D = 8, 256, 512
T = B * S
NT = T // P
H = 16
G = 512
DC = D // P
HD = D // H
CH = S
CC = CH // P
XHD = CH // H
E, GR, EG = 16, 4, 4
TOPK, TOPK_G = 4, 2
SH = 2
EA = E + SH
I = 352
IC = (I + P - 1) // P
IP = IC * P
EPS = 1e-5
MASKED = -1e30
M_CLAMP = 60000.0
PRODUCTS = ((0, 0), (0, 1), (1, 0))
QB, PB, PR = 96, 96, 97

F32 = mybir.dt.float32
F16 = mybir.dt.float16
BF16 = mybir.dt.bfloat16
ALU = mybir.AluOpType
ACT = mybir.ActivationFunctionType
AX = mybir.AxisListType


class Chain:

    def __init__(self, engine, sem, per_round=0, turn=0):
        self.engine, self.sem, self.n = engine, sem, 0
        self.base = per_round * turn

    def __call__(self, instruction):
        instruction.then_inc(self.sem, 1)
        self.n += 1
        return self.base + self.n

    def then_wait(self, instruction):
        self.engine.wait_ge(self.sem, self(instruction))


def split_product(nc, out, lhs, rhs, chunks):
    last = None
    for c in range(chunks):
        for n, (a, b) in enumerate(PRODUCTS):
            last = nc.tensor.matmul(out, lhs(a, c), rhs(b, c), start=(c == 0 and n == 0),
                                    stop=(c == chunks - 1 and n == len(PRODUCTS) - 1))
    return last


def layer_norm(nc, name, x_sb, xn, ident, transposed, source=None):
    with ExitStack() as ctx:
        sb = lambda n, s, d: ctx.enter_context(nc.sbuf_tensor(f"{name}_{n}", s, d))
        sem = lambda n: ctx.enter_context(nc.semaphore(f"{name}_{n}"))
        stats = sb("stats", [P, NT, 6], F32)
        moments = sb("moments", [P, NT, 2], F32)
        std = sb("std", [P, NT], F32)
        rstd = sb("rstd", [P, NT], F32)
        norm = sb("norm", [P, 2, D], F32)
        pair = sb("pair", [P, 2, 2, D], F16)
        turned = ctx.enter_context(nc.psum_tensor(f"{name}_turned", [P, 2, 2, DC, P], F16))
        loaded = [sem(f"loaded{q}") for q in range(4)]
        dve_chain, moments_ready, std_ready = sem("dve_chain"), sem("moments_ready"), sem("std_ready")
        norm_ready, high_ready, low_ready = sem("norm_ready"), sem("high_ready"), sem("low_ready")
        turn_ready, stored = sem("turn_ready"), sem("stored")
        block = ctx.enter_context(nc.Block())

        @block.sync
        def _(sp):
            if source is not None:
                for q in range(4):
                    sp.dma_start(x_sb[:, 4 * q:4 * q + 4, :],
                                 source[4 * q:4 * q + 4].rearrange("t p d -> p t d")).then_inc(loaded[q], 16)

        @block.vector
        def _(dve):
            link = Chain(dve, dve_chain)
            for t in range(NT):
                if source is not None and t % 4 == 0:
                    dve.wait_ge(loaded[t // 4], 16)
                link(nc.vector.bn_stats(stats[:, t, :], x_sb[:, t, :]))
            dve.wait_ge(dve_chain, NT)
            for t in range(NT):
                link(nc.vector.bn_aggr(moments[:, t, :], stats[:, t, :]))
            dve.wait_ge(dve_chain, 2 * NT)
            nc.vector.tensor_scalar(std[:, :], moments[:, :, 1], EPS, None, ALU.add).then_inc(moments_ready, 1)
            dve.wait_ge(std_ready, 1)
            link.then_wait(nc.vector.reciprocal(rstd[:, :], std[:, :]))
            with dve.Fori(0, NT // 2) as i:
                for s in range(2):
                    dve.wait_ge(low_ready, 2 * i + s + 1)
                    nc.vector.tensor_scalar(norm[:, s, :], x_sb[:, 2 * i + s, :],
                                            moments[:, 2 * i + s, 0:1], rstd[:, bass.ds(2 * i + s, 1)],
                                            ALU.subtract, ALU.mult).then_inc(norm_ready, 1)
                for s in range(2):
                    dve.wait_ge(high_ready, 2 * i + s + 1)
                    low = xn[:, 1, 2 * i + s, :] if not transposed else pair[:, s, 1, :]
                    nc.vector.tensor_tensor(low, norm[:, s, :],
                                            xn[:, 0, 2 * i + s, :] if not transposed else pair[:, s, 0, :],
                                            ALU.subtract).then_inc(low_ready, 1)

        @block.scalar
        def _(act):
            act.wait_ge(moments_ready, 1)
            nc.scalar.activation(std[:, :], std[:, :], ACT.Sqrt).then_inc(std_ready, 1)
            act.sem_inc(low_ready, 2)
            with act.Fori(0, NT // 2) as i:
                for s in range(2):
                    act.wait_ge(norm_ready, 2 * i + s + 1)
                    high = xn[:, 0, 2 * i + s, :] if not transposed else pair[:, s, 0, :]
                    if transposed:
                        act.wait_ge(turn_ready, 2 * i + s + 1)
                    nc.scalar.activation(high, norm[:, s, :], ACT.Copy).then_inc(high_ready, 1)
                if transposed:
                    for s in range(2):
                        act.wait_ge(turn_ready, 2 * i + s + 3)
                        nc.scalar.activation(
                            xn[:, :, :, bass.ds((2 * i + s) * P, P)].rearrange("p h c n -> p (h c) n"),
                            turned[:, s, :, :, :].rearrange("p h c n -> p (h c) n"),
                            ACT.Copy).then_inc(stored, 1)

        if transposed:
            @block.tensor
            def _(pe):
                pe.sem_inc(turn_ready, 2)
                with pe.Fori(0, NT // 2) as i:
                    for s in range(2):
                        pe.wait_ge(low_ready, 2 * i + s + 3)
                        if s == 0:
                            pe.wait_ge(high_ready, 2 * i + 1)
                        for h in range(2):
                            for c in range(DC):
                                last = nc.tensor.transpose(turned[:, s, h, c, :],
                                                           pair[:, s, h, c * P:(c + 1) * P], ident[:, :])
                        last.then_inc(turn_ready, 1)


def split_weights(nc, name, jobs):
    with ExitStack() as ctx:
        sem = lambda n: ctx.enter_context(nc.semaphore(f"{name}_{n}"))
        loaded = [sem(f"loaded{n}") for n in range(len(jobs))]
        high_ready, low_ready = sem("high_ready"), sem("low_ready")
        block = ctx.enter_context(nc.Block())

        @block.sync
        def _(sp):
            for n, (dram, raw, _pair) in enumerate(jobs):
                sp.dma_start(raw, dram).then_inc(loaded[n], 16)

        @block.scalar
        def _(act):
            for n, (_dram, raw, pair) in enumerate(jobs):
                act.wait_ge(loaded[n], 16)
                nc.scalar.activation(pair[0], raw, ACT.Copy).then_inc(high_ready, 1)

        @block.gpsimd
        def _(pool):
            for n, (_dram, raw, pair) in enumerate(jobs):
                pool.wait_ge(high_ready, n + 1)
                nc.gpsimd.tensor_tensor(pair[1], raw, pair[0], ALU.subtract).then_inc(low_ready, 1)


def self_attention(nc, x_sb, ident, x_dram, wqkv_dram, wout_dram):
    SCALE = float(HD) ** -0.5
    with ExitStack() as ctx:
        sb = lambda n, s, d: ctx.enter_context(nc.sbuf_tensor(f"sa_{n}", s, d))
        pb = lambda n, s, d: ctx.enter_context(nc.psum_tensor(f"sa_{n}", s, d))
        sem = lambda n: ctx.enter_context(nc.semaphore(f"sa_{n}"))
        w = sb("w", [P, 2, DC, 3 * D], F16)
        wo = sb("wo", [P, 2, DC, D], F16)
        xn = sb("xn", [P, 2, DC, T], F16)
        identb = sb("identb", [P, P], BF16)
        mask4 = sb("mask4", [P, 4, P], BF16)
        mask2 = sb("mask2", [P, 2, 2, P], BF16)
        maskt = sb("maskt", [P, 3, P], BF16)
        with ExitStack() as raws:
            raw = raws.enter_context(nc.sbuf_tensor("sa_raw", [P, DC, 3 * D], F32))
            rawo = raws.enter_context(nc.sbuf_tensor("sa_rawo", [P, DC, D], F32))
            jobs = [(wqkv_dram.rearrange("(c p) e -> p c e", p=P)[:, c], raw[:, c, :],
                     (w[:, 0, c, :], w[:, 1, c, :])) for c in range(DC)]
            jobs.append((wout_dram.rearrange("(c p) e -> p c e", p=P), rawo[:, :, :],
                         (wo[:, 0], wo[:, 1])))
            split_weights(nc, "sa_split", jobs)
        layer_norm(nc, "sa_ln", x_sb, xn, ident, True, x_dram)

        qk = sb("qk", [P, 2, 2 * DC, G], F16)
        qs = sb("qs", [P, H, G], F16)
        ks = sb("ks", [P, H, G], F16)
        v = sb("v", [P, 4, D], F32)
        ones = sb("ones", [P, HD], F32)
        mx = sb("mx", [P, 4, H], F32)
        nm = sb("nm", [P, 4, H], F16)
        nmf = sb("nmf", [P, 4, H], F32)
        mt = sb("mt", [H, G], F16)
        pt = sb("pt", [P, 4, 2, G], F32)
        rden = sb("rden", [P, G], F32)
        yf = sb("yf", [P, 2, G], F32)
        yt = sb("yt", [P, 2, DC, G], F16)
        scratch = nc.dram_tensor("sa_scratch", (2, 2 * D, G), F16).ap()
        proj = pb("proj", [P, 2, G], F32)
        sc = pb("sc", [P, 4, G], F32)
        pv = pb("pv", [P, G], F32)
        den = pb("den", [P, G], F32)
        made, made_f = sem("made"), sem("made_f")
        proj_done, proj_free, high_ready = sem("proj_done"), sem("proj_free"), sem("high_ready")
        spilled, stacked, maxed, score_done = sem("spilled"), sem("stacked"), sem("maxed"), sem("score_done")
        neg_ready, mt_done, mt_ready, row_loaded = sem("neg_ready"), sem("mt_done"), sem("mt_ready"), sem("row_loaded")
        st_done, exp_done, pv_done, norm_done = sem("st_done"), sem("exp_done"), sem("pv_done"), sem("norm_done")
        y_high, y_low, dve_chain = sem("y_high"), sem("y_low"), sem("dve_chain")
        UNITS, SCORES, PAIRS = 16, 24, 16
        DVE_LINKS = 5

        with nc.Block() as block:
            @block.gpsimd
            def _(pool):
                nc.gpsimd.memset(mask4[:, :, :], 0.0).then_inc(made, 1)
                nc.gpsimd.memset(mask2[:, :, :, :], 0.0).then_inc(made, 1)
                nc.gpsimd.memset(maskt[:, :, :], 0.0).then_inc(made, 1)
                nc.gpsimd.memset(identb[:, :], 0.0).then_inc(made, 1)
                nc.gpsimd.memset(ones[:, :], 1.0).then_inc(made_f, 1)
                pool.wait_ge(made, 4)
                nc.gpsimd.affine_select(out=mask4[:, :, :], in_=mask4[:, :, :], compare_op=ALU.is_ge, fill=MASKED,
                                        base=0, pattern=[[0, 4], [-1, P]], channel_multiplier=1).then_inc(made_f, 1)
                nc.gpsimd.affine_select(out=mask2[:, :, 1, :], in_=mask2[:, :, 1, :], compare_op=ALU.is_ge, fill=MASKED,
                                        base=0, pattern=[[0, 2], [-1, P]], channel_multiplier=1).then_inc(made_f, 1)
                nc.gpsimd.affine_select(out=maskt[:, 0:3:2, :], in_=maskt[:, 0:3:2, :], compare_op=ALU.is_ge, fill=MASKED,
                                        base=0, pattern=[[0, 2], [1, P]], channel_multiplier=-1).then_inc(made_f, 1)
                nc.gpsimd.affine_select(out=identb[:, :], in_=identb[:, :], compare_op=ALU.not_equal, fill=1.0,
                                        base=0, pattern=[[-1, P]], channel_multiplier=1).then_inc(made_f, 1)

            @block.vector
            def _(dve):
                nc.vector.memset(ks[PB:PR, :, :], 1.0).then_inc(made_f, 1)

        block = ctx.enter_context(nc.Block())

        @block.tensor
        def _(pe):
            with pe.Fori(0, T // G) as g:
                def unit(u, lhs, rhs):
                    pe.wait_ge(proj_free, UNITS * g + u + 1)
                    split_product(nc, proj[:, u % 2, :], lhs, rhs, DC).then_inc(proj_done, 1)

                for u in range(2 * DC):
                    unit(u, lambda a, c: w[:, a, c, u * P:(u + 1) * P], lambda b, c: xn[:, b, c, bass.ds(g * G, G)])
                for t in range(4):
                    unit(2 * DC + t, lambda a, c: xn[:, a, c, bass.ds(g * G + t * P, P)],
                         lambda b, c: w[:, b, c, 2 * D:3 * D])
                pe.wait_ge(stacked, 96 * g + 96)
                n = 0
                for bb in range(2):
                    for hq in range(4):
                        for part in range(3):
                            if n >= 4:
                                pe.wait_ge(maxed, SCORES * g + n - 3)
                            bank = sc[:, n % 4, :]
                            q0 = bb * S + (P if part else 0)
                            keys, heads = (S, 2) if part else (P, 4)
                            mask = mask2[:, :, :, :].rearrange("p a b c -> p (a b c)") if part \
                                else mask4[:, :, :].rearrange("p a c -> p (a c)")
                            nc.tensor.matmul(bank, identb[:, :], mask, start=True, stop=False, skip_group_check=True)
                            for k in range(heads):
                                h = 4 * hq + (2 * (part - 1) if part else 0) + k
                                last = nc.tensor.matmul(bank[:, k * keys:(k + 1) * keys],
                                                        qs[0:QB, h, q0:q0 + P],
                                                        ks[0:QB, h, bb * S:bb * S + keys],
                                                        start=False, stop=(k == heads - 1), skip_group_check=True)
                            last.then_inc(score_done, 1)
                            n += 1
                pe.wait_ge(neg_ready, g + 1)
                pe.wait_ge(norm_done, 4 * g + 1)
                mtp = pv[0:H, 0:G // 2].bitcast(F16)
                for t in range(4):
                    last = nc.tensor.transpose(mtp[:, t * P:(t + 1) * P], nm[:, t, :], ident[:, :])
                last.then_inc(mt_done, 1)

                def transposed_scores(p):
                    hq, bb, jj = p // 4, p // 2 % 2, p % 2
                    if p >= 2:
                        pe.wait_ge(exp_done, PAIRS * g + p - 1)
                    for i in range(2):
                        h, bank = 4 * hq + 2 * jj + i, sc[:, 2 * (p % 2) + i, :]
                        k0 = bb * S
                        nc.tensor.matmul(bank[:, 0:3 * P], identb[:, :], maskt[:, :, :].rearrange("p a c -> p (a c)"),
                                         start=True, stop=False, skip_group_check=True)
                        nc.tensor.matmul(bank[:, 0:S], ks[0:PR, h, k0:k0 + P], qs[0:PR, h, k0:k0 + S],
                                         start=False, stop=False, skip_group_check=True)
                        last = nc.tensor.matmul(bank[:, S:S + P], ks[0:PR, h, k0 + P:k0 + S],
                                                qs[0:PR, h, k0 + P:k0 + S], start=False, stop=True,
                                                skip_group_check=True)
                    last.then_inc(st_done, 1)

                def values(qd):
                    hq, bb = qd // 2, qd % 2
                    pe.wait_ge(exp_done, PAIRS * g + 2 * qd + 2)
                    if bb == 0:
                        pe.wait_ge(norm_done, 4 * g + hq + 1)
                    for out, values_of in ((pv, True), (den, False)):
                        for kt in range(2):
                            for j in range(4):
                                pr = pt[:, (2 * qd + j // 2) % 4, j % 2, :]
                                lhs = v[:, 2 * bb + kt, (4 * hq + j) * HD:(4 * hq + j + 1) * HD] if values_of \
                                    else ones[:, :]
                                cols = slice(bb * S, bb * S + S) if kt == 0 else slice(bb * S + P, bb * S + S)
                                last = nc.tensor.matmul(out[j * HD:(j + 1) * HD, cols], lhs,
                                                        pr[:, 0:S] if kt == 0 else pr[:, S:S + P],
                                                        start=(kt == 0), stop=(kt == 1), skip_group_check=True,
                                                        tile_position=(0, j * HD))
                    last.then_inc(pv_done, 1)

                pe.wait_ge(row_loaded, 16 * g + 16)
                for p in range(2):
                    transposed_scores(p)
                for qd in range(8):
                    for p in (2 * qd + 2, 2 * qd + 3):
                        if p < PAIRS:
                            transposed_scores(p)
                    values(qd)
                pe.wait_ge(y_low, 4 * g + 4)
                for t in range(4):
                    unit(12 + t, lambda a, c: yt[:, a, c, t * P:(t + 1) * P], lambda b, c: wo[:, b, c, :])

        @block.vector
        def _(dve):
            dve.sem_inc(proj_free, 2)
            dve.sem_inc(norm_done, 1)
            with dve.Fori(0, T // G) as g:
                link = Chain(dve, dve_chain, DVE_LINKS, g)
                for u in range(2 * DC):
                    dve.wait_ge(high_ready, 2 * DC * g + u + 1)
                    nc.vector.tensor_tensor(qk[:, 1, u, :], proj[:, u % 2, :], qk[:, 0, u, :],
                                            ALU.subtract).then_inc(proj_free, 1)
                for t in range(4):
                    dve.wait_ge(proj_done, UNITS * g + 2 * DC + t + 1)
                    nc.vector.tensor_copy(v[:, t, :], proj[:, t % 2, :]).then_inc(proj_free, 1)
                n = 0
                for bb in range(2):
                    for hq in range(4):
                        for part in range(3):
                            dve.wait_ge(score_done, SCORES * g + n + 1)
                            if part == 0:
                                out, heads = mx[:, 2 * bb, 4 * hq:4 * hq + 4], 4
                            else:
                                h0 = 4 * hq + 2 * (part - 1)
                                out, heads = mx[:, 2 * bb + 1, h0:h0 + 2], 2
                            nc.vector.reduce_max(out, sc[:, n % 4, :].rearrange("p (h k) -> p h k", h=heads),
                                                 AX.X).then_inc(maxed, 1)
                            n += 1
                dve.wait_ge(maxed, SCORES * g + SCORES)
                link.then_wait(nc.vector.tensor_scalar(nmf[:, :, :], mx[:, :, :], -1.0, M_CLAMP, ALU.mult, ALU.min))
                nc.vector.tensor_scalar(nm[:, :, :], nmf[:, :, :], -M_CLAMP, None, ALU.max).then_inc(neg_ready, 1)
                for hq in range(4):
                    dve.wait_ge(pv_done, 8 * g + 2 * hq + 2)
                    if hq >= 1:
                        dve.wait_ge(norm_done, 4 * g + hq + 1)
                    link.then_wait(nc.vector.reciprocal(rden[:, :], den[:, :]))
                    if hq >= 2:
                        dve.wait_ge(y_low, 4 * g + hq - 1)
                    nc.vector.tensor_tensor(yf[:, hq % 2, :], pv[:, :], rden[:, :], ALU.mult).then_inc(norm_done, 1)
                for t in range(4):
                    dve.wait_ge(proj_done, UNITS * g + 12 + t + 1)
                    nc.vector.tensor_tensor(x_sb[:, 4 * g + t, :], proj[:, t % 2, :], x_sb[:, 4 * g + t, :],
                                            ALU.add).then_inc(proj_free, 1)
                assert link.n == DVE_LINKS

        @block.scalar
        def _(act):
            with act.Fori(0, T // G) as g:
                for u in range(2 * DC):
                    act.wait_ge(proj_done, UNITS * g + u + 1)
                    nc.scalar.activation(qk[:, 0, u, :], proj[:, u % 2, :], ACT.Copy).then_inc(high_ready, 1)
                act.wait_ge(mt_done, g + 1)
                nc.scalar.activation(mt[:, :], pv[0:H, 0:G // 2].bitcast(F16), ACT.Copy).then_inc(mt_ready, 1)

                def high(hq):
                    act.wait_ge(norm_done, 4 * g + hq + 2)
                    nc.scalar.activation(yt[:, 0, hq, :], yf[:, hq % 2, :], ACT.Copy).then_inc(y_high, 1)

                for p in range(PAIRS):
                    act.wait_ge(st_done, PAIRS * g + p + 1)
                    if p >= 4:
                        act.wait_ge(pv_done, 8 * g + p // 2 - 1)
                    nc.scalar.activation(pt[:, p % 4, :, 0:3 * P], sc[:, 2 * (p % 2):2 * (p % 2) + 2, 0:3 * P],
                                         ACT.Exp, scale=SCALE).then_inc(exp_done, 1)
                    if p % 4 == 3 and p > 3:
                        high(p // 4 - 1)
                high(3)

        @block.gpsimd
        def _(pool):
            with pool.Fori(0, T // G) as g:
                for hq in range(4):
                    pool.wait_ge(y_high, 4 * g + hq + 1)
                    nc.gpsimd.tensor_tensor(yt[:, 1, hq, :], yf[:, hq % 2, :], yt[:, 0, hq, :],
                                            ALU.subtract).then_inc(y_low, 1)

        @block.sync
        def _(sp):
            with sp.Fori(0, T // G) as g:
                for side in range(2):
                    sp.wait_ge(proj_free, UNITS * g + 2 + DC * (side + 1))
                    for part in range(2):
                        sp.dma_start(scratch[part, side * D:(side + 1) * D].rearrange("(c p) n -> p c n", p=P),
                                     qk[:, part, side * DC:(side + 1) * DC, :]).then_inc(spilled, 16)
                sp.wait_ge(spilled, 64 * g + 64)
                for side, (tile, parts) in enumerate(((qs, (0, 0, 1)), (ks, (0, 1, 0)))):
                    for r, part in enumerate(parts):
                        sp.dma_start(tile[r * HD:(r + 1) * HD, :, :],
                                     scratch[part, side * D:(side + 1) * D].rearrange("(h d) n -> d h n", d=HD)
                                     ).then_inc(stacked, 16)
                sp.wait_ge(mt_ready, g + 1)
                sp.dma_start(qs[PB:PR, :, :], mt[:, :]).then_inc(row_loaded, 16)


def cross_attention(nc, x_sb, ctx_dram, enc_dram, w_dram, b_dram, bv_dram, wm_dram, bm_dram):
    SCALE = float(XHD) ** -0.5
    with ExitStack() as ctx:
        sb = lambda n, s, d: ctx.enter_context(nc.sbuf_tensor(f"ca_{n}", s, d))
        pb = lambda n, s, d: ctx.enter_context(nc.psum_tensor(f"ca_{n}", s, d))
        sem = lambda n: ctx.enter_context(nc.semaphore(f"ca_{n}"))
        w = sb("w", [P, 2, 3, CC, CH], F16)
        wm = sb("wm", [P, 2, 4, CH], F16)
        xn = sb("xn", [P, 2, NT, G], F16)
        cx = sb("cx", [P, 2, NT, G], F16)
        with ExitStack() as raws:
            raw = raws.enter_context(nc.sbuf_tensor("ca_raw", [P, 3, CC, CH], F32))
            rawm = raws.enter_context(nc.sbuf_tensor("ca_rawm", [P, 4, CH], F32))
            rawc = raws.enter_context(nc.sbuf_tensor("ca_rawc", [P, NT, G], F32))
            jobs = [(w_dram.rearrange("s (c p) e -> p s c e", p=P), raw[:, :, :, :], (w[:, 0], w[:, 1])),
                    (wm_dram.rearrange("q p e -> p q e"), rawm[:, :, :], (wm[:, 0], wm[:, 1]))]
            jobs += [(ctx_dram[4 * q:4 * q + 4].rearrange("t p d -> p t d"), rawc[:, 4 * q:4 * q + 4, :],
                      (cx[:, 0, 4 * q:4 * q + 4, :], cx[:, 1, 4 * q:4 * q + 4, :])) for q in range(4)]
            split_weights(nc, "ca_split", jobs)
        layer_norm(nc, "ca_ln", x_sb, xn, None, False)

        freq = sb("freq", [P, 2, G], F32)
        sign = sb("sign", [P, 1], F32)
        signi = sb("signi", [P, 1], mybir.dt.int32)
        bqk = sb("bqk", [P, 4], F32)
        bm = sb("bm", [P, CC], F32)
        bv = sb("bv", [P, H, XHD], F32)
        tf = sb("tf", [P, 4, G], F32)
        waited = sb("waited", [P, 4], F32)
        rf = sb("rf", [P, 2, G], F32)
        qk = sb("qk", [P, 2, 4, G], F16)
        qs = sb("qs", [P, H, G], F16)
        ks = sb("ks", [P, H, G], F16)
        va = sb("va", [P, 4, H, 2 * XHD], F32)
        identh = sb("identh", [P, P], F16)
        mx = sb("mx", [P, 4, H], F32)
        nm = sb("nm", [P, 4, H], F16)
        nmf = sb("nmf", [P, 4, H], F32)
        mt = sb("mt", [H, G], F16)
        pt = sb("pt", [P, 4, 2, G], F32)
        turned = sb("turned", [P, G // 32, 32], F32)
        rden = sb("rden", [P, G // 32], F32)
        quot = sb("quot", [P, G // 32, 32], F32)
        yf = sb("yf", [P, 2, G], F32)
        yt = sb("yt", [P, 2, 4, G], F16)
        scratch = nc.dram_tensor("ca_scratch", (2, 4, P, G), F16).ap()
        proj = pb("proj", [P, 2, G], F32)
        sc = pb("sc", [P, 4, G], F32)
        pv = pb("pv", [P, 2, G], F32)
        loads, made, signed = sem("loads"), sem("made"), sem("signed")
        proj_done, qk_out, v_out, res_done = sem("proj_done"), sem("qk_out"), sem("v_out"), sem("res_done")
        swapped, rotated, pool_chain, high_ready, low_ready = (
            sem("swapped"), sem("rotated"), sem("pool_chain"), sem("high_ready"), sem("low_ready"))
        spilled, stacked, maxed, score_done = sem("spilled"), sem("stacked"), sem("maxed"), sem("score_done")
        neg_ready, mt_done, mt_ready, row_loaded = sem("neg_ready"), sem("mt_done"), sem("mt_ready"), sem("row_loaded")
        st_done, exp_done, pv_done, norm_done = sem("st_done"), sem("exp_done"), sem("pv_done"), sem("norm_done")
        turned_out = sem("turned_out")
        y_high, y_low, dve_chain = sem("y_high"), sem("y_low"), sem("dve_chain")
        UNITS, SCORES, PAIRS = 10, 32, 32
        DVE_LINKS, POOL_LINKS = 9, 8

        with nc.Block() as block:
            @block.sync
            def _(sp):
                for f in range(2):
                    for j in range(8):
                        sp.dma_start(freq[j * XHD:(j + 1) * XHD, f, :], enc_dram[f]).then_inc(loads, 16)
                sp.dma_start(bqk[:, :], b_dram).then_inc(loads, 16)
                sp.dma_start(bm[:, :], bm_dram).then_inc(loads, 16)
                sp.dma_start(bv[:, :, :].rearrange("p h d -> p (h d)"), bv_dram).then_inc(loads, 16)
                sp.wait_ge(loads, 16 * 19)

            @block.gpsimd
            def _(pool):
                nc.gpsimd.memset(identh[:, :], 0.0).then_inc(made, 1)
                nc.gpsimd.memset(va[:, :, :, :], 1.0).then_inc(signed, 1)
                nc.gpsimd.memset(quot[:, :, :], 0.0).then_inc(signed, 1)
                pool.wait_ge(made, 1)
                nc.gpsimd.affine_select(out=identh[:, :], in_=identh[:, :], compare_op=ALU.not_equal, fill=1.0,
                                        base=0, pattern=[[-1, P]], channel_multiplier=1).then_inc(signed, 1)
                nc.gpsimd.iota(signi[:, :], pattern=[[0, 1]], base=0, channel_multiplier=1).then_inc(made, 1)

            @block.vector
            def _(dve):
                nc.vector.memset(qs[4 * XHD:PB, :, :], 0.0).then_inc(signed, 1)
                nc.vector.memset(ks[4 * XHD:PB, :, :], 0.0).then_inc(signed, 1)
                nc.vector.memset(ks[PB:PR, :, :], 1.0).then_inc(signed, 1)
                dve.wait_ge(made, 2)
                nc.vector.tensor_scalar(signi[:, :], signi[:, :], 1, None, ALU.bitwise_and).then_inc(made, 1)
                dve.wait_ge(made, 3)
                nc.vector.tensor_scalar(sign[:, :], signi[:, :], 2.0, -1.0, ALU.mult, ALU.add).then_inc(made, 1)
                dve.wait_ge(made, 4)
                dve.wait_ge(loads, 16 * 19)
                nc.vector.tensor_scalar(freq[:, 1, :], freq[:, 1, :], sign[:, 0:1], None, ALU.mult).then_inc(made, 1)

        block = ctx.enter_context(nc.Block())

        @block.tensor
        def _(pe):
            with pe.Fori(0, B) as b:
                def unit(out, lhs, rhs, chunks):
                    split_product(nc, out, lhs, rhs, chunks).then_inc(proj_done, 1)

                for u in range(4):
                    side, oc = u // 2, u % 2
                    if u < 2:
                        pe.wait_ge(res_done, 2 * b + u + 1)
                    else:
                        pe.wait_ge(qk_out, 4 * b + u - 1)
                    src = xn if side == 0 else cx
                    unit(proj[:, u % 2, :], lambda a, c: w[:, a, side, c, oc * P:(oc + 1) * P],
                         lambda p, c: src[:, p, 2 * b + c, :], CC)
                for kt in range(4):
                    if kt < 2:
                        pe.wait_ge(qk_out, 4 * b + kt + 3)
                    else:
                        pe.wait_ge(v_out, 4 * b + kt - 1)
                    unit(proj[:, kt % 2, 0:CH], lambda a, c: cx[:, a, 2 * b + c, kt * P:(kt + 1) * P],
                         lambda p, c: w[:, p, 2, c, :], CC)
                pe.wait_ge(stacked, 128 * b + 128)
                for n in range(SCORES):
                    qt, hp = n // 8, n % 8
                    if n >= 2:
                        pe.wait_ge(maxed, SCORES * b + n - 1)
                    for i in range(2):
                        last = nc.tensor.matmul(sc[:, 2 * (n % 2) + i, :], qs[0:QB, 2 * hp + i, qt * P:(qt + 1) * P],
                                                ks[0:QB, 2 * hp + i, :], start=True, stop=True)
                    last.then_inc(score_done, 1)
                pe.wait_ge(neg_ready, b + 1)
                pe.wait_ge(turned_out, 4 * b + 1)
                mtp = pv[0:H, 0, 0:G // 2].bitcast(F16)
                for t in range(4):
                    last = nc.tensor.transpose(mtp[:, t * P:(t + 1) * P], nm[:, t, :], identh[:, :])
                last.then_inc(mt_done, 1)

                def transposed_scores(p):
                    hq, kt, jj = p // 8, p // 2 % 4, p % 2
                    if p >= 2:
                        pe.wait_ge(exp_done, PAIRS * b + p - 1)
                    for i in range(2):
                        h = 4 * hq + 2 * jj + i
                        last = nc.tensor.matmul(sc[:, 2 * (p % 2) + i, :], ks[0:PR, h, kt * P:(kt + 1) * P],
                                                qs[0:PR, h, :], start=True, stop=True)
                    last.then_inc(st_done, 1)

                def values(qd):
                    hq, kt = qd // 4, qd % 4
                    pe.wait_ge(exp_done, PAIRS * b + 2 * qd + 2)
                    if kt == 0:
                        pe.wait_ge(turned_out, 4 * b + hq + 1)
                    for j in range(4):
                        last = nc.tensor.matmul(pv[j * 32:(j + 1) * 32, hq % 2, :], va[:, kt, 4 * hq + j, :],
                                                pt[:, (2 * qd + j // 2) % 4, j % 2, :], start=(kt == 0),
                                                stop=(kt == 3), skip_group_check=True, tile_position=(0, j * 32))
                    last.then_inc(pv_done, 1)

                pe.wait_ge(row_loaded, 16 * b + 16)
                pe.wait_ge(mt_ready, b + 1)
                for p in range(2):
                    transposed_scores(p)
                for qd in range(16):
                    for p in (2 * qd + 2, 2 * qd + 3):
                        if p < PAIRS:
                            transposed_scores(p)
                    values(qd)
                pe.wait_ge(y_low, 4 * b + 4)
                for oc in range(2):
                    pe.wait_ge(v_out, 4 * b + 3 + oc)
                    unit(proj[:, oc, :], lambda a, c: wm[:, a, c, oc * P:(oc + 1) * P],
                         lambda p, c: yt[:, p, c, :], 4)

        @block.vector
        def _(dve):
            dve.sem_inc(res_done, 2)
            dve.sem_inc(turned_out, 1)
            with dve.Fori(0, B) as b:
                link = Chain(dve, dve_chain, DVE_LINKS, b)
                for u in range(4):
                    dve.wait_ge(qk_out, 4 * b + u + 1)
                    if u >= 2:
                        dve.wait_ge(rotated, 4 * b + u - 1)
                    nc.vector.memset(waited[:, u:u + 1], 0.0)
                    nc.vector.stream_shuffle(rf[:, u % 2, :], tf[:, u, :], [i ^ 1 for i in range(32)]).then_inc(swapped, 1)
                for kt in range(4):
                    dve.wait_ge(proj_done, UNITS * b + 4 + kt + 1)
                    nc.vector.tensor_tensor(va[:, kt, :, 0:XHD],
                                            proj[:, kt % 2, 0:CH].rearrange("p (h d) -> p h d", h=H), bv[:, :, :],
                                            ALU.add).then_inc(v_out, 1)
                for u in range(4):
                    dve.wait_ge(high_ready, 4 * b + u + 1)
                    nc.vector.tensor_tensor(qk[:, 1, u, :], tf[:, u, :], qk[:, 0, u, :],
                                            ALU.subtract).then_inc(low_ready, 1)
                for n in range(SCORES):
                    qt, hp = n // 8, n % 8
                    dve.wait_ge(score_done, SCORES * b + n + 1)
                    nc.vector.reduce_max(mx[:, qt, 2 * hp:2 * hp + 2], sc[:, 2 * (n % 2):2 * (n % 2) + 2, :],
                                         AX.X).then_inc(maxed, 1)
                dve.wait_ge(maxed, SCORES * b + SCORES)
                link.then_wait(nc.vector.tensor_scalar(nmf[:, :, :], mx[:, :, :], -1.0, M_CLAMP, ALU.mult, ALU.min))
                nc.vector.tensor_scalar(nm[:, :, :], nmf[:, :, :], -M_CLAMP, None, ALU.max).then_inc(neg_ready, 1)
                for hq in range(4):
                    dve.wait_ge(pv_done, 16 * b + 4 * hq + 4)
                    nc.vector.transpose(turned[:, :, :].rearrange("p a b -> p (a b)"), pv[:, hq % 2, :]
                                        ).then_inc(turned_out, 1)
                    dve.wait_ge(turned_out, 4 * b + hq + 2)
                    link.then_wait(nc.vector.reciprocal(rden[:, :], turned[:, :, XHD]))
                    link.then_wait(nc.vector.tensor_tensor(
                        quot[:, :, 0:XHD], turned[:, :, 0:XHD],
                        rden[:, :].rearrange("p (a o) -> p a o", o=1).to_broadcast([P, G // 32, XHD]), ALU.mult))
                    if hq >= 2:
                        dve.wait_ge(y_low, 4 * b + hq - 1)
                    nc.vector.transpose(yf[:, hq % 2, :], quot[:, :, :].rearrange("p a b -> p (a b)")
                                        ).then_inc(norm_done, 1)
                    if hq < 3:
                        dve.wait_ge(norm_done, 4 * b + hq + 1)
                for oc in range(2):
                    dve.wait_ge(proj_done, UNITS * b + 8 + oc + 1)
                    nc.vector.scalar_tensor_tensor(x_sb[:, 2 * b + oc, :], proj[:, oc, :], bm[:, oc:oc + 1],
                                                   x_sb[:, 2 * b + oc, :], ALU.add, ALU.add).then_inc(res_done, 1)
                assert link.n == DVE_LINKS

        @block.scalar
        def _(act):
            with act.Fori(0, B) as b:
                for u in range(4):
                    act.wait_ge(proj_done, UNITS * b + u + 1)
                    nc.scalar.activation(tf[:, u, :], proj[:, u % 2, :], ACT.Identity,
                                         bias=bqk[:, u:u + 1]).then_inc(qk_out, 1)
                for u in range(4):
                    act.wait_ge(rotated, 4 * b + u + 1)
                    nc.scalar.activation(qk[:, 0, u, :], tf[:, u, :], ACT.Copy).then_inc(high_ready, 1)
                act.wait_ge(mt_done, b + 1)
                nc.scalar.activation(mt[:, :], pv[0:H, 0, 0:G // 2].bitcast(F16), ACT.Copy).then_inc(mt_ready, 1)

                def high(hq):
                    act.wait_ge(norm_done, 4 * b + hq + 1)
                    nc.scalar.activation(yt[:, 0, hq, :], yf[:, hq % 2, :], ACT.Copy).then_inc(y_high, 1)

                for p in range(PAIRS):
                    act.wait_ge(st_done, PAIRS * b + p + 1)
                    if p >= 4:
                        act.wait_ge(pv_done, 16 * b + p // 2 - 1)
                    nc.scalar.activation(pt[:, p % 4, :, :], sc[:, 2 * (p % 2):2 * (p % 2) + 2, :],
                                         ACT.Exp, scale=SCALE).then_inc(exp_done, 1)
                    if p % 8 == 5 and p > 8:
                        high(p // 8 - 1)
                high(3)

        @block.gpsimd
        def _(pool):
            with pool.Fori(0, B) as b:
                link = Chain(pool, pool_chain, POOL_LINKS, b)
                for u in range(4):
                    pool.wait_ge(swapped, 4 * b + u + 1)
                    link(nc.gpsimd.tensor_tensor(tf[:, u, :], tf[:, u, :], freq[:, 0, :], ALU.mult))
                    link.then_wait(nc.gpsimd.tensor_tensor(rf[:, u % 2, :], rf[:, u % 2, :], freq[:, 1, :], ALU.mult))
                    nc.gpsimd.tensor_tensor(tf[:, u, :], tf[:, u, :], rf[:, u % 2, :], ALU.add).then_inc(rotated, 1)
                for hq in range(4):
                    pool.wait_ge(y_high, 4 * b + hq + 1)
                    nc.gpsimd.tensor_tensor(yt[:, 1, hq, :], yf[:, hq % 2, :], yt[:, 0, hq, :],
                                            ALU.subtract).then_inc(y_low, 1)

        @block.sync
        def _(sp):
            with sp.Fori(0, B) as b:
                for side in range(2):
                    sp.wait_ge(low_ready, 4 * b + 2 * side + 2)
                    for part in range(2):
                        sp.dma_start(scratch[part, 2 * side:2 * side + 2].rearrange("u p n -> p u n"),
                                     qk[:, part, 2 * side:2 * side + 2, :]).then_inc(spilled, 16)
                sp.wait_ge(spilled, 64 * b + 64)
                for side, (tile, parts) in enumerate(((qs, (0, 0, 1, 1)), (ks, (0, 1, 0, 1)))):
                    for r, part in enumerate(parts):
                        sp.dma_start(tile[r * XHD:(r + 1) * XHD, :, :],
                                     scratch[part, 2 * side:2 * side + 2].rearrange("u (h d) n -> d (u h) n", d=XHD)
                                     ).then_inc(stacked, 16)
                sp.wait_ge(mt_ready, b + 1)
                sp.dma_start(qs[PB:PR, :, :], mt[:, :]).then_inc(row_loaded, 16)


def router(nc, xn, comb, wg_dram):
    with ExitStack() as ctx:
        sb = lambda n, s, d: ctx.enter_context(nc.sbuf_tensor(f"ro_{n}", s, d))
        sem = lambda n: ctx.enter_context(nc.semaphore(f"ro_{n}"))
        raw = sb("raw", [P, DC, E], F32)
        wg = sb("wg", [P, 2, DC, E], F16)
        split_weights(nc, "ro_split", [(wg_dram.rearrange("(c p) e -> p c e", p=P), raw[:, :, :],
                                        (wg[:, 0], wg[:, 1]))])
        logits = ctx.enter_context(nc.psum_tensor("ro_logits", [P, NT, E], F32))
        lg = sb("lg", [P, NT, E], F32)
        s = sb("s", [P, NT, E], F32)
        col = sb("col", [P, NT], F32)
        gs = sb("gs", [P, NT, GR], F32)
        cmp = sb("cmp", [P, NT, E, E], F32)
        eq = sb("eq", [P, NT, E, E], F32)
        rank = sb("rank", [P, NT, E], F32)
        before = sb("before", [P, E, E], F32)
        made, logits_ready, shifted, exped, chain = (
            sem("made"), sem("logits_ready"), sem("shifted"), sem("exped"), sem("chain"))
        block = ctx.enter_context(nc.Block())

        @block.gpsimd
        def _(pool):
            nc.gpsimd.memset(before[:, :, :], 1.0).then_inc(made, 1)
            pool.wait_ge(made, 1)
            nc.gpsimd.affine_select(out=before[:, :, :], in_=before[:, :, :], compare_op=ALU.is_gt, fill=0.0,
                                    base=0, pattern=[[1, E], [-1, E]], channel_multiplier=0).then_inc(made, 1)

        @block.tensor
        def _(pe):
            for t in range(NT):
                last = split_product(nc, logits[:, t, :], lambda a, c: xn[:, a, c, t * P:(t + 1) * P],
                                     lambda b, c: wg[:, b, c, :], DC)
            last.then_inc(logits_ready, 1)

        @block.vector
        def _(dve):
            link = Chain(dve, chain)
            over = lambda a, n: a.rearrange("p t (g o) -> p t g o", o=1).to_broadcast([P, NT, n, n])
            dve.wait_ge(logits_ready, 1)
            link.then_wait(nc.vector.reduce_max(col[:, :], logits[:, :, :], AX.X))
            bc = col[:, :].rearrange("p (t o) -> p t o", o=1).to_broadcast([P, NT, E])
            nc.vector.tensor_tensor(lg[:, :, :], logits[:, :, :], bc, ALU.subtract).then_inc(shifted, 1)
            dve.wait_ge(exped, 1)
            link.then_wait(nc.vector.reduce_sum(col[:, :], s[:, :, :], AX.X))
            link.then_wait(nc.vector.reciprocal(col[:, :], col[:, :]))
            link.then_wait(nc.vector.tensor_tensor(s[:, :, :], s[:, :, :], bc, ALU.mult))
            link.then_wait(nc.vector.reduce_max(gs[:, :, :], s[:, :, :].rearrange("p t (g e) -> p t g e", g=GR), AX.X))
            dve.wait_ge(made, 2)

            def ranks(v, n):
                c4 = cmp[:, :, 0:n, 0:n]
                e4 = eq[:, :, 0:n, 0:n]
                other = v.rearrange("p t (o g) -> p t o g", o=1).to_broadcast([P, NT, n, n])
                own = over(v, n)
                bf = before[:, 0:n, 0:n].rearrange("p (o a) b -> p o a b", o=1).to_broadcast([P, NT, n, n])
                link(nc.vector.tensor_tensor(c4, other, own, ALU.is_gt))
                link.then_wait(nc.vector.tensor_tensor(e4, other, own, ALU.is_equal))
                link.then_wait(nc.vector.tensor_tensor(e4, e4, bf, ALU.mult))
                link.then_wait(nc.vector.tensor_tensor(c4, c4, e4, ALU.add))
                link.then_wait(nc.vector.reduce_sum(rank[:, :, 0:n], c4, AX.X))

            ranks(gs[:, :, :], GR)
            link.then_wait(nc.vector.tensor_scalar(gs[:, :, :], rank[:, :, 0:GR], float(TOPK_G), None, ALU.is_lt))
            gb = gs[:, :, :].rearrange("p t (g o) -> p t g o", o=1).to_broadcast([P, NT, GR, EG])
            l4 = lg[:, :, :].rearrange("p t (g e) -> p t g e", g=GR)
            link.then_wait(nc.vector.tensor_tensor(l4, s[:, :, :].rearrange("p t (g e) -> p t g e", g=GR), gb, ALU.mult))
            link.then_wait(nc.vector.tensor_scalar(gs[:, :, :], gs[:, :, :], -1.0, None, ALU.add))
            link.then_wait(nc.vector.tensor_tensor(l4, l4, gb, ALU.add))
            ranks(lg[:, :, :], E)
            link.then_wait(nc.vector.tensor_scalar(rank[:, :, :], rank[:, :, :], float(TOPK), None, ALU.is_lt))
            link(nc.vector.tensor_tensor(comb[:, 0:E, :].rearrange("p e t -> p t e"), s[:, :, :], rank[:, :, :], ALU.mult))
            link(nc.vector.memset(comb[:, E:EA, :], 1.0))

        @block.scalar
        def _(act):
            act.wait_ge(shifted, 1)
            nc.scalar.activation(s[:, :, :], lg[:, :, :], ACT.Exp).then_inc(exped, 1)


def experts(nc, x_sb, xn, comb, w1_dram, w3_dram, w2_dram, out_dram):
    with ExitStack() as ctx:
        sb = lambda n, s, d: ctx.enter_context(nc.sbuf_tensor(f"ex_{n}", s, d))
        pb = lambda n, s, d: ctx.enter_context(nc.psum_tensor(f"ex_{n}", s, d))
        sem = lambda n: ctx.enter_context(nc.semaphore(f"ex_{n}"))
        raw_up = sb("raw_up", [P, 2, 2, DC, IP], F32)
        raw_down = sb("raw_down", [P, 2, IC, D], F32)
        up = sb("up", [P, 2, 2, 2, DC, IP], F16)
        down = sb("down", [P, 2, 2, IC, D], F16)
        gate = sb("gate", [P, 2, G], F32)
        hf = sb("hf", [P, 2, G], F32)
        ht = sb("ht", [P, 2, 2, IC, G], F16)
        ab = pb("ab", [P, 2, 2, G], F32)
        yp = pb("yp", [P, 4, D], F32)
        loaded = [sem("loaded0"), sem("loaded1")]
        w_high, w_low = sem("w_high"), sem("w_low")
        ab_done, gate_done, h_done, h_high, h_low = (
            sem("ab_done"), sem("gate_done"), sem("h_done"), sem("h_high"), sem("h_low"))
        y_done, added, stored = sem("y_done"), sem("added"), sem("stored")
        GT = T // G
        HC = GT * IC
        LOOPS = EA // 2
        block = ctx.enter_context(nc.Block())

        def each_round(engine, body):
            with engine.Fori(0, LOOPS - 1) as i:
                for k in range(2):
                    body(2 * i + k, k, False)
            for k in range(2):
                body(EA - 2 + k, k, k == 1)

        @block.sync
        def _(sp):
            sp.sem_inc(w_low, 6)
            def body(e, k, _last):
                sp.wait_ge(w_low, 3 * e + 3)
                sp.dma_start(raw_up[:, k, 0], w1_dram[e].rearrange("(c p) i -> p c i", p=P)).then_inc(loaded[k], 16)
                sp.dma_start(raw_up[:, k, 1], w3_dram[e].rearrange("(c p) i -> p c i", p=P)).then_inc(loaded[k], 16)
                sp.dma_start(raw_down[:, k], w2_dram[e].rearrange("(c p) d -> p c d", p=P)).then_inc(loaded[k], 16)
            each_round(sp, body)
            for t in range(0, NT, 4):
                sp.wait_ge(added, EA * NT - NT + t + 4 + 2 * NT)
                sp.dma_start(out_dram[t:t + 4].rearrange("t p d -> p t d"), x_sb[:, t:t + 4, :]).then_inc(stored, 16)
            sp.wait_ge(stored, 16 * (NT // 4))

        def raw_and_pair(k, j):
            if j < 2:
                return raw_up[:, k, j], up[:, k, j, 0], up[:, k, j, 1]
            return raw_down[:, k], down[:, k, 0], down[:, k, 1]

        @block.gpsimd
        def _(pool):
            def body(e, k, _last):
                for j in range(3):
                    pool.wait_ge(w_high, 3 * e + j + 1)
                    raw, high, low = raw_and_pair(k, j)
                    nc.gpsimd.tensor_tensor(low, raw, high, ALU.subtract).then_inc(w_low, 1)
            for j in range(3):
                raw, high, low = raw_and_pair(0, j)
                pool.wait_ge(w_high, j + 1)
                nc.gpsimd.tensor_tensor(low, raw, high, ALU.subtract).then_inc(w_low, 1)

            def turn(e, k, last):
                for n in range(HC):
                    pool.wait_ge(h_high, HC * e + n + 1)
                    g, c = n // IC, n % IC
                    nc.gpsimd.tensor_tensor(ht[:, g % 2, 1, c, :], hf[:, n % 2, :], ht[:, g % 2, 0, c, :],
                                            ALU.subtract).then_inc(h_low, 1)
                    if not last and n % 3 == 1 and n // 3 >= 1:
                        j = n // 3 - 1
                        pool.wait_ge(w_high, 3 * (e + 1) + j + 1)
                        raw, high, low = raw_and_pair(1 - k, j)
                        nc.gpsimd.tensor_tensor(low, raw, high, ALU.subtract).then_inc(w_low, 1)
            each_round(pool, turn)

        @block.scalar
        def _(act):
            def split(e, k, j):
                act.wait_ge(loaded[k], 24 * (e - k) + 48)
                raw, high, low = raw_and_pair(k, j)
                nc.scalar.activation(high, raw, ACT.Copy).then_inc(w_high, 1)
            for j in range(3):
                split(0, 0, j)

            def turn(e, k, last):
                for n in range(HC):
                    act.wait_ge(ab_done, HC * e + n + 1)
                    act.wait_ge(h_done, HC * e + n + 1)
                    nc.scalar.activation(gate[:, n % 2, :], ab[:, n % 2, 0, :], ACT.Silu).then_inc(gate_done, 1)
                    g, c = n // IC, n % IC
                    act.wait_ge(h_done, HC * e + n + 3)
                    act.wait_ge(y_done, 4 * GT * e + 4 * g + 4)
                    nc.scalar.activation(ht[:, g % 2, 0, c, :], hf[:, n % 2, :], ACT.Copy).then_inc(h_high, 1)
                    if not last and n % 3 == 0 and n // 3 >= 1:
                        if n // 3 == 1:
                            act.wait_ge(y_done, 4 * GT * e + 8)
                        split(e + 1, 1 - k, n // 3 - 1)
            each_round(act, turn)

        @block.vector
        def _(dve):
            dve.sem_inc(h_done, 2)
            dve.sem_inc(added, 2 * NT)

            def hidden(e, n):
                dve.wait_ge(gate_done, HC * e + n + 1)
                dve.wait_ge(h_low, HC * e + n + 1)
                nc.vector.tensor_tensor(hf[:, n % 2, :], ab[:, n % 2, 1, :], gate[:, n % 2, :],
                                        ALU.mult).then_inc(h_done, 1)

            def add(e, g):
                for t in range(4):
                    tile = 4 * g + t
                    dve.wait_ge(y_done, 4 * GT * e + tile + 1 + 8)
                    dve.wait_ge(added, NT * e + tile + 1 + NT)
                    nc.vector.scalar_tensor_tensor(x_sb[:, tile, :], yp[:, t, :], comb[:, e, tile:tile + 1],
                                                   x_sb[:, tile, :], ALU.mult, ALU.add).then_inc(added, 1)

            for n in range(IC):
                hidden(0, n)

            def turn(e, k, last):
                for g in range(GT):
                    if g < GT - 1:
                        for c in range(IC):
                            hidden(e, (g + 1) * IC + c)
                    elif not last:
                        for c in range(IC):
                            hidden(e + 1, c)
                    add(e, g)
            each_round(dve, turn)

        @block.tensor
        def _(pe):
            pe.sem_inc(h_low, 2)
            pe.sem_inc(y_done, 8)

            def hidden(e, k, g):
                for c in range(IC):
                    n = g * IC + c
                    pe.wait_ge(h_done, HC * e + n + 1)
                    for j in range(2):
                        last = split_product(nc, ab[:, n % 2, j, :],
                                             lambda a, d: up[:, k, j, a, d, c * P:(c + 1) * P],
                                             lambda b, d: xn[:, b, d, g * G:(g + 1) * G], DC)
                    last.then_inc(ab_done, 1)

            def outputs(e, k, g):
                pe.wait_ge(h_low, HC * e + (g + 1) * IC + 2)
                for t in range(4):
                    pe.wait_ge(added, NT * e + 4 * g + t + 1 + 2 * NT - 4)
                    split_product(nc, yp[:, t, :], lambda a, c: ht[:, g % 2, a, c, t * P:(t + 1) * P],
                                  lambda b, c: down[:, k, b, c, :], IC).then_inc(y_done, 1)

            pe.wait_ge(w_low, 6 + 3)
            hidden(0, 0, 0)

            def turn(e, k, last):
                for g in range(GT):
                    if g < GT - 1:
                        hidden(e, k, g + 1)
                    elif not last:
                        pe.wait_ge(w_low, 3 * e + 12)
                        hidden(e + 1, 1 - k, 0)
                    outputs(e, k, g)
            each_round(pe, turn)


def decoder_block(nc, a):
    with ExitStack() as ctx:
        x_sb = ctx.enter_context(nc.sbuf_tensor("x_sb", [P, NT, D], F32))
        ident = ctx.enter_context(nc.sbuf_tensor("ident", [P, P], F16))
        made = ctx.enter_context(nc.semaphore("ident_made"))
        with nc.Block() as block:
            @block.gpsimd
            def _(pool):
                nc.gpsimd.memset(ident[:, :], 0.0).then_inc(made, 1)
                pool.wait_ge(made, 1)
                nc.gpsimd.affine_select(out=ident[:, :], in_=ident[:, :], compare_op=ALU.not_equal, fill=1.0,
                                        base=0, pattern=[[-1, P]], channel_multiplier=1).then_inc(made, 1)
        self_attention(nc, x_sb, ident, a["x"], a["wqkv"], a["wout"])
        cross_attention(nc, x_sb, a["ctx"], a["enc"], a["wx"], a["bx"], a["bv"], a["wm"], a["bm"])
        with nc.sbuf_tensor("fx_xn", [P, 2, DC, T], F16) as xn, nc.sbuf_tensor("fx_comb", [P, EA, NT], F32) as comb:
            layer_norm(nc, "fx_ln", x_sb, xn, ident, True)
            router(nc, xn, comb, a["wg"])
            experts(nc, x_sb, xn, comb, a["w1"], a["w3"], a["w2"], a["out"])


def laid_out(inputs):
    import numpy as np

    get = lambda k: np.asarray(inputs[k])
    heads = lambda m: m.reshape(XHD, H, *m.shape[1:]).swapaxes(0, 1).reshape(CH, *m.shape[1:])
    pad = lambda m, axis: np.concatenate(
        [m, np.zeros([IP - I if n == axis else s for n, s in enumerate(m.shape)], m.dtype)], axis)
    wx = np.stack([heads(get(f"L0_xattn_W{s}")).T for s in "qkv"])
    bx = np.concatenate([heads(get(f"L0_xattn_b{s}")).reshape(CC, P) for s in "qk"]).T
    wm = np.zeros((4, P, CH), np.float32)
    wm.reshape(4, 4, 2, XHD, CH)[:, :, 0] = heads(get("L0_xattn_Wm").T).reshape(4, 4, XHD, CH)
    both = lambda routed, shared: np.concatenate([routed, shared.reshape(SH, I, D)])
    w2s = get("L0_ffn_Ws2").T.reshape(SH, I, D)
    out = {
        "x": get("x").reshape(NT, P, D),
        "ctx": get("ctx_2048").reshape(NT, P, D),
        "wqkv": get("L0_attn_w_qkv").T,
        "wout": get("L0_attn_w_out").T,
        "enc": get("L0_xattn_encoding").reshape(2, G, XHD).swapaxes(1, 2),
        "wx": wx,
        "bx": bx,
        "bv": np.repeat(heads(get("L0_xattn_bv"))[None], P, 0),
        "wm": wm,
        "bm": get("L0_xattn_bm").reshape(CC, P).T,
        "wg": get("L0_ffn_Wg").T,
        "w1": pad(both(get("L0_ffn_W1"), get("L0_ffn_Ws1")).swapaxes(1, 2), 2),
        "w3": pad(both(get("L0_ffn_W3"), get("L0_ffn_Ws3")).swapaxes(1, 2), 2),
        "w2": pad(np.concatenate([get("L0_ffn_W2").swapaxes(1, 2), w2s]), 1),
    }
    return {k: np.ascontiguousarray(v) for k, v in out.items()}


def kernel(**inputs):
    import concourse.bacc as bacc
    from concourse.bass_utils import run_bass_kernel_spmd

    nc = bacc.Bacc("TRN2", target_bir_lowering=False, num_devices=1)
    arrays = {f"in_{k}": v for k, v in laid_out(inputs).items()}
    args = {k[3:]: nc.dram_tensor(k, v.shape, mybir.dt.from_np(v.dtype), kind="ExternalInput").ap()
            for k, v in arrays.items()}
    args["out"] = nc.dram_tensor("out", (NT, P, D), F32, kind="ExternalOutput").ap()
    decoder_block(nc, args)
    r = run_bass_kernel_spmd(nc, [arrays], core_ids=[0])
    return r.results[0]["out"].reshape(B, S, D)
```

```python
import concourse.bass as bass
from concourse import mybir
from contextlib import ExitStack

P = 128
B, S, D = 8, 256, 512
T = B * S
NT = T // P
H = 16
G = 512
DC = D // P
HD = D // H
CH = S
CC = CH // P
XHD = CH // H
E, GR, EG = 16, 4, 4
TOPK, TOPK_G = 4, 2
SH = 2
EA = E + SH
I = 352
IC = (I + P - 1) // P
IP = IC * P
I_ROWS = [min(P, I - c * P) for c in range(IC)]
EW = 2 * DC * I
WC = EW + IC * D
PIECES = [(c * 2 * I, 2 * I) for c in range(DC)] + [(EW + n * IC * D // 2, IC * D // 2) for n in range(2)]
NP = len(PIECES)
MAX_TILES = (T * TOPK + E * (P - 1)) // P
TILES = 2 * ((MAX_TILES + 1) // 2) + 4
CLEARS = 6
assert TILES % CLEARS == 0
EPS = 1e-5
MASKED = -1e30
M_CLAMP = 60000.0
PRODUCTS = ((0, 0), (0, 1), (1, 0))
QB, PB, PR = 96, 96, 97

F32 = mybir.dt.float32
F16 = mybir.dt.float16
BF16 = mybir.dt.bfloat16
I32 = mybir.dt.int32
ALU = mybir.AluOpType
ACT = mybir.ActivationFunctionType
AX = mybir.AxisListType


class Chain:

    def __init__(self, engine, sem, per_round=0, turn=0):
        self.engine, self.sem, self.n = engine, sem, 0
        self.base = per_round * turn

    def __call__(self, instruction):
        instruction.then_inc(self.sem, 1)
        self.n += 1
        return self.base + self.n

    def then_wait(self, instruction):
        self.engine.wait_ge(self.sem, self(instruction))


def split_product(nc, out, lhs, rhs, chunks):
    last = None
    for c in range(chunks):
        for n, (a, b) in enumerate(PRODUCTS):
            last = nc.tensor.matmul(out, lhs(a, c), rhs(b, c), start=(c == 0 and n == 0),
                                    stop=(c == chunks - 1 and n == len(PRODUCTS) - 1))
    return last


def layer_norm(nc, name, x_sb, xn, ident, transposed, source=None, rows=None):
    with ExitStack() as ctx:
        sb = lambda n, s, d: ctx.enter_context(nc.sbuf_tensor(f"{name}_{n}", s, d))
        sem = lambda n: ctx.enter_context(nc.semaphore(f"{name}_{n}"))
        stats = sb("stats", [P, NT, 6], F32)
        moments = sb("moments", [P, NT, 2], F32)
        std = sb("std", [P, NT], F32)
        rstd = sb("rstd", [P, NT], F32)
        norm = sb("norm", [P, 2, D], F32)
        pair = sb("pair", [P, 2, 2, D], F16)
        turned = ctx.enter_context(nc.psum_tensor(f"{name}_turned", [P, 2, 2, DC, P], F16))
        loaded = [sem(f"loaded{q}") for q in range(4)]
        dve_chain, moments_ready, std_ready = sem("dve_chain"), sem("moments_ready"), sem("std_ready")
        norm_ready, high_ready, low_ready = sem("norm_ready"), sem("high_ready"), sem("low_ready")
        turn_ready, stored, row_chain = sem("turn_ready"), sem("stored"), sem("row_chain")
        block = ctx.enter_context(nc.Block())

        @block.sync
        def _(sp):
            if source is not None:
                for q in range(4):
                    sp.dma_start(x_sb[:, 4 * q:4 * q + 4, :],
                                 source[4 * q:4 * q + 4].rearrange("t p d -> p t d")).then_inc(loaded[q], 16)

        @block.vector
        def _(dve):
            link = Chain(dve, dve_chain)
            for t in range(NT):
                if source is not None and t % 4 == 0:
                    dve.wait_ge(loaded[t // 4], 16)
                link(nc.vector.bn_stats(stats[:, t, :], x_sb[:, t, :]))
            dve.wait_ge(dve_chain, NT)
            for t in range(NT):
                link(nc.vector.bn_aggr(moments[:, t, :], stats[:, t, :]))
            dve.wait_ge(dve_chain, 2 * NT)
            nc.vector.tensor_scalar(std[:, :], moments[:, :, 1], EPS, None, ALU.add).then_inc(moments_ready, 1)
            dve.wait_ge(std_ready, 1)
            link.then_wait(nc.vector.reciprocal(rstd[:, :], std[:, :]))
            with dve.Fori(0, NT // 2) as i:
                for s in range(2):
                    dve.wait_ge(low_ready, 2 * i + s + 1)
                    nc.vector.tensor_scalar(norm[:, s, :], x_sb[:, 2 * i + s, :],
                                            moments[:, 2 * i + s, 0:1], rstd[:, bass.ds(2 * i + s, 1)],
                                            ALU.subtract, ALU.mult).then_inc(norm_ready, 1)
                for s in range(2):
                    dve.wait_ge(high_ready, 2 * i + s + 1)
                    low = xn[:, 1, 2 * i + s, :] if not transposed else pair[:, s, 1, :]
                    lower = nc.vector.tensor_tensor(low, norm[:, s, :],
                                                    xn[:, 0, 2 * i + s, :] if not transposed else pair[:, s, 0, :],
                                                    ALU.subtract)
                    if rows is None:
                        lower.then_inc(low_ready, 1)
                    else:
                        lower.then_inc(row_chain, 1)
                        dve.wait_ge(row_chain, 2 * i + s + 1)
                        nc.vector.tensor_copy(rows[:, 2 * i + s, :, :], pair[:, s, :, :]).then_inc(low_ready, 1)

        @block.scalar
        def _(act):
            act.wait_ge(moments_ready, 1)
            nc.scalar.activation(std[:, :], std[:, :], ACT.Sqrt).then_inc(std_ready, 1)
            act.sem_inc(low_ready, 2)
            with act.Fori(0, NT // 2) as i:
                for s in range(2):
                    act.wait_ge(norm_ready, 2 * i + s + 1)
                    high = xn[:, 0, 2 * i + s, :] if not transposed else pair[:, s, 0, :]
                    if transposed:
                        act.wait_ge(turn_ready, 2 * i + s + 1)
                    nc.scalar.activation(high, norm[:, s, :], ACT.Copy).then_inc(high_ready, 1)
                if transposed:
                    for s in range(2):
                        act.wait_ge(turn_ready, 2 * i + s + 3)
                        nc.scalar.activation(
                            xn[:, :, :, bass.ds((2 * i + s) * P, P)].rearrange("p h c n -> p (h c) n"),
                            turned[:, s, :, :, :].rearrange("p h c n -> p (h c) n"),
                            ACT.Copy).then_inc(stored, 1)

        if transposed:
            @block.tensor
            def _(pe):
                pe.sem_inc(turn_ready, 2)
                with pe.Fori(0, NT // 2) as i:
                    for s in range(2):
                        pe.wait_ge(low_ready, 2 * i + s + 3)
                        if s == 0:
                            pe.wait_ge(high_ready, 2 * i + 1)
                        for h in range(2):
                            for c in range(DC):
                                last = nc.tensor.transpose(turned[:, s, h, c, :],
                                                           pair[:, s, h, c * P:(c + 1) * P], ident[:, :])
                        last.then_inc(turn_ready, 1)


class WeightSplit:

    def __init__(self, nc, ctx):
        self.nc = nc
        self.loaded = [ctx.enter_context(nc.semaphore(f"split_loaded{n}")) for n in range(DC + 1)]
        self.high_ready = ctx.enter_context(nc.semaphore("split_high_ready"))
        self.low_ready = ctx.enter_context(nc.semaphore("split_low_ready"))
        self.loads, self.done = [0] * (DC + 1), 0

    def __call__(self, jobs):
        for n in range(len(jobs)):
            self.loads[n] += 16
        with self.nc.Block() as block:
            self.programs(block, jobs, list(self.loads), self.done)
        self.done += len(jobs)

    def programs(self, block, jobs, arrived, done):
        nc, loaded, high_ready, low_ready = self.nc, self.loaded, self.high_ready, self.low_ready

        @block.sync
        def _(sp):
            for n, (dram, raw, _pair) in enumerate(jobs):
                sp.dma_start(raw, dram).then_inc(loaded[n], 16)

        @block.scalar
        def _(act):
            for n, (_dram, raw, pair) in enumerate(jobs):
                act.wait_ge(loaded[n], arrived[n])
                nc.scalar.activation(pair[0], raw, ACT.Copy).then_inc(high_ready, 1)

        @block.gpsimd
        def _(pool):
            for n, (_dram, raw, pair) in enumerate(jobs):
                pool.wait_ge(high_ready, done + n + 1)
                nc.gpsimd.tensor_tensor(pair[1], raw, pair[0], ALU.subtract).then_inc(low_ready, 1)


def self_attention(nc, split, x_sb, ident, x_dram, wqkv_dram, wout_dram, slot_rows, slot_outs, cleared):
    SCALE = float(HD) ** -0.5
    with ExitStack() as ctx:
        sb = lambda n, s, d: ctx.enter_context(nc.sbuf_tensor(f"sa_{n}", s, d))
        pb = lambda n, s, d: ctx.enter_context(nc.psum_tensor(f"sa_{n}", s, d))
        sem = lambda n: ctx.enter_context(nc.semaphore(f"sa_{n}"))
        w = sb("w", [P, 2, DC, 3 * D], F16)
        wo = sb("wo", [P, 2, DC, D], F16)
        xn = sb("xn", [P, 2, DC, T], F16)
        zeros = sb("zeros", [P, 2 * D], F16)
        identb = sb("identb", [P, P], BF16)
        mask4 = sb("mask4", [P, 4, P], BF16)
        mask2 = sb("mask2", [P, 2, 2, P], BF16)
        maskt = sb("maskt", [P, 3, P], BF16)
        with ExitStack() as raws:
            raw = raws.enter_context(nc.sbuf_tensor("sa_raw", [P, DC, 3 * D], F32))
            rawo = raws.enter_context(nc.sbuf_tensor("sa_rawo", [P, DC, D], F32))
            jobs = [(wqkv_dram.rearrange("(c p) e -> p c e", p=P)[:, c], raw[:, c, :],
                     (w[:, 0, c, :], w[:, 1, c, :])) for c in range(DC)]
            jobs.append((wout_dram.rearrange("(c p) e -> p c e", p=P), rawo[:, :, :],
                         (wo[:, 0], wo[:, 1])))
            split(jobs)
        layer_norm(nc, "sa_ln", x_sb, xn, ident, True, x_dram)

        qk = sb("qk", [P, 2, 2 * DC, G], F16)
        qs = sb("qs", [P, H, G], F16)
        ks = sb("ks", [P, H, G], F16)
        v = sb("v", [P, 4, D], F32)
        ones = sb("ones", [P, HD], F32)
        mx = sb("mx", [P, 4, H], F32)
        nm = sb("nm", [P, 4, H], F16)
        nmf = sb("nmf", [P, 4, H], F32)
        mt = sb("mt", [H, G], F16)
        pt = sb("pt", [P, 4, 2, G], F32)
        rden = sb("rden", [P, G], F32)
        yf = sb("yf", [P, 2, G], F32)
        yt = sb("yt", [P, 2, DC, G], F16)
        scratch = nc.dram_tensor("sa_scratch", (2, 2 * D, G), F16).ap()
        proj = pb("proj", [P, 2, G], F32)
        sc = pb("sc", [P, 4, G], F32)
        pv = pb("pv", [P, G], F32)
        den = pb("den", [P, G], F32)
        made, made_f = sem("made"), sem("made_f")
        proj_done, proj_free, high_ready = sem("proj_done"), sem("proj_free"), sem("high_ready")
        spilled, stacked, maxed, score_done = sem("spilled"), sem("stacked"), sem("maxed"), sem("score_done")
        neg_ready, mt_done, mt_ready, row_loaded = sem("neg_ready"), sem("mt_done"), sem("mt_ready"), sem("row_loaded")
        st_done, exp_done, pv_done, norm_done = sem("st_done"), sem("exp_done"), sem("pv_done"), sem("norm_done")
        y_high, y_low, dve_chain = sem("y_high"), sem("y_low"), sem("dve_chain")
        UNITS, SCORES, PAIRS = 16, 24, 16
        DVE_LINKS = 5

        with nc.Block() as block:
            @block.gpsimd
            def _(pool):
                nc.gpsimd.memset(mask4[:, :, :], 0.0).then_inc(made, 1)
                nc.gpsimd.memset(mask2[:, :, :, :], 0.0).then_inc(made, 1)
                nc.gpsimd.memset(maskt[:, :, :], 0.0).then_inc(made, 1)
                nc.gpsimd.memset(identb[:, :], 0.0).then_inc(made, 1)
                nc.gpsimd.memset(ones[:, :], 1.0).then_inc(made_f, 1)
                nc.gpsimd.memset(zeros[:, :], 0.0).then_inc(made_f, 1)
                pool.wait_ge(made, 4)
                nc.gpsimd.affine_select(out=mask4[:, :, :], in_=mask4[:, :, :], compare_op=ALU.is_ge, fill=MASKED,
                                        base=0, pattern=[[0, 4], [-1, P]], channel_multiplier=1).then_inc(made_f, 1)
                nc.gpsimd.affine_select(out=mask2[:, :, 1, :], in_=mask2[:, :, 1, :], compare_op=ALU.is_ge, fill=MASKED,
                                        base=0, pattern=[[0, 2], [-1, P]], channel_multiplier=1).then_inc(made_f, 1)
                nc.gpsimd.affine_select(out=maskt[:, 0:3:2, :], in_=maskt[:, 0:3:2, :], compare_op=ALU.is_ge, fill=MASKED,
                                        base=0, pattern=[[0, 2], [1, P]], channel_multiplier=-1).then_inc(made_f, 1)
                nc.gpsimd.affine_select(out=identb[:, :], in_=identb[:, :], compare_op=ALU.not_equal, fill=1.0,
                                        base=0, pattern=[[-1, P]], channel_multiplier=1).then_inc(made_f, 1)

            @block.vector
            def _(dve):
                nc.vector.memset(ks[PB:PR, :, :], 1.0).then_inc(made_f, 1)

        block = ctx.enter_context(nc.Block())

        @block.tensor
        def _(pe):
            with pe.Fori(0, T // G) as g:
                def unit(u, lhs, rhs):
                    pe.wait_ge(proj_free, UNITS * g + u + 1)
                    split_product(nc, proj[:, u % 2, :], lhs, rhs, DC).then_inc(proj_done, 1)

                for u in range(2 * DC):
                    unit(u, lambda a, c: w[:, a, c, u * P:(u + 1) * P], lambda b, c: xn[:, b, c, bass.ds(g * G, G)])
                for t in range(4):
                    unit(2 * DC + t, lambda a, c: xn[:, a, c, bass.ds(g * G + t * P, P)],
                         lambda b, c: w[:, b, c, 2 * D:3 * D])
                pe.wait_ge(stacked, 96 * g + 96)
                n = 0
                for bb in range(2):
                    for hq in range(4):
                        for part in range(3):
                            if n >= 4:
                                pe.wait_ge(maxed, SCORES * g + n - 3)
                            bank = sc[:, n % 4, :]
                            q0 = bb * S + (P if part else 0)
                            keys, heads = (S, 2) if part else (P, 4)
                            mask = mask2[:, :, :, :].rearrange("p a b c -> p (a b c)") if part \
                                else mask4[:, :, :].rearrange("p a c -> p (a c)")
                            nc.tensor.matmul(bank, identb[:, :], mask, start=True, stop=False, skip_group_check=True)
                            for k in range(heads):
                                h = 4 * hq + (2 * (part - 1) if part else 0) + k
                                last = nc.tensor.matmul(bank[:, k * keys:(k + 1) * keys],
                                                        qs[0:QB, h, q0:q0 + P],
                                                        ks[0:QB, h, bb * S:bb * S + keys],
                                                        start=False, stop=(k == heads - 1), skip_group_check=True)
                            last.then_inc(score_done, 1)
                            n += 1
                pe.wait_ge(neg_ready, g + 1)
                pe.wait_ge(norm_done, 4 * g + 1)
                mtp = pv[0:H, 0:G // 2].bitcast(F16)
                for t in range(4):
                    last = nc.tensor.transpose(mtp[:, t * P:(t + 1) * P], nm[:, t, :], ident[:, :])
                last.then_inc(mt_done, 1)

                def transposed_scores(p):
                    hq, bb, jj = p // 4, p // 2 % 2, p % 2
                    if p >= 2:
                        pe.wait_ge(exp_done, PAIRS * g + p - 1)
                    for i in range(2):
                        h, bank = 4 * hq + 2 * jj + i, sc[:, 2 * (p % 2) + i, :]
                        k0 = bb * S
                        nc.tensor.matmul(bank[:, 0:3 * P], identb[:, :], maskt[:, :, :].rearrange("p a c -> p (a c)"),
                                         start=True, stop=False, skip_group_check=True)
                        nc.tensor.matmul(bank[:, 0:S], ks[0:PR, h, k0:k0 + P], qs[0:PR, h, k0:k0 + S],
                                         start=False, stop=False, skip_group_check=True)
                        last = nc.tensor.matmul(bank[:, S:S + P], ks[0:PR, h, k0 + P:k0 + S],
                                                qs[0:PR, h, k0 + P:k0 + S], start=False, stop=True,
                                                skip_group_check=True)
                    last.then_inc(st_done, 1)

                def values(qd):
                    hq, bb = qd // 2, qd % 2
                    pe.wait_ge(exp_done, PAIRS * g + 2 * qd + 2)
                    if bb == 0:
                        pe.wait_ge(norm_done, 4 * g + hq + 1)
                    for out, values_of in ((pv, True), (den, False)):
                        for kt in range(2):
                            for j in range(4):
                                pr = pt[:, (2 * qd + j // 2) % 4, j % 2, :]
                                lhs = v[:, 2 * bb + kt, (4 * hq + j) * HD:(4 * hq + j + 1) * HD] if values_of \
                                    else ones[:, :]
                                cols = slice(bb * S, bb * S + S) if kt == 0 else slice(bb * S + P, bb * S + S)
                                last = nc.tensor.matmul(out[j * HD:(j + 1) * HD, cols], lhs,
                                                        pr[:, 0:S] if kt == 0 else pr[:, S:S + P],
                                                        start=(kt == 0), stop=(kt == 1), skip_group_check=True,
                                                        tile_position=(0, j * HD))
                    last.then_inc(pv_done, 1)

                pe.wait_ge(row_loaded, 16 * g + 16)
                for p in range(2):
                    transposed_scores(p)
                for qd in range(8):
                    for p in (2 * qd + 2, 2 * qd + 3):
                        if p < PAIRS:
                            transposed_scores(p)
                    values(qd)
                pe.wait_ge(y_low, 4 * g + 4)
                for t in range(4):
                    unit(12 + t, lambda a, c: yt[:, a, c, t * P:(t + 1) * P], lambda b, c: wo[:, b, c, :])

        @block.vector
        def _(dve):
            dve.sem_inc(proj_free, 2)
            dve.sem_inc(norm_done, 1)
            with dve.Fori(0, T // G) as g:
                link = Chain(dve, dve_chain, DVE_LINKS, g)
                for u in range(2 * DC):
                    dve.wait_ge(high_ready, 2 * DC * g + u + 1)
                    nc.vector.tensor_tensor(qk[:, 1, u, :], proj[:, u % 2, :], qk[:, 0, u, :],
                                            ALU.subtract).then_inc(proj_free, 1)
                for t in range(4):
                    dve.wait_ge(proj_done, UNITS * g + 2 * DC + t + 1)
                    nc.vector.tensor_copy(v[:, t, :], proj[:, t % 2, :]).then_inc(proj_free, 1)
                n = 0
                for bb in range(2):
                    for hq in range(4):
                        for part in range(3):
                            dve.wait_ge(score_done, SCORES * g + n + 1)
                            if part == 0:
                                out, heads = mx[:, 2 * bb, 4 * hq:4 * hq + 4], 4
                            else:
                                h0 = 4 * hq + 2 * (part - 1)
                                out, heads = mx[:, 2 * bb + 1, h0:h0 + 2], 2
                            nc.vector.reduce_max(out, sc[:, n % 4, :].rearrange("p (h k) -> p h k", h=heads),
                                                 AX.X).then_inc(maxed, 1)
                            n += 1
                dve.wait_ge(maxed, SCORES * g + SCORES)
                link.then_wait(nc.vector.tensor_scalar(nmf[:, :, :], mx[:, :, :], -1.0, M_CLAMP, ALU.mult, ALU.min))
                nc.vector.tensor_scalar(nm[:, :, :], nmf[:, :, :], -M_CLAMP, None, ALU.max).then_inc(neg_ready, 1)
                for hq in range(4):
                    dve.wait_ge(pv_done, 8 * g + 2 * hq + 2)
                    if hq >= 1:
                        dve.wait_ge(norm_done, 4 * g + hq + 1)
                    link.then_wait(nc.vector.reciprocal(rden[:, :], den[:, :]))
                    if hq >= 2:
                        dve.wait_ge(y_low, 4 * g + hq - 1)
                    nc.vector.tensor_tensor(yf[:, hq % 2, :], pv[:, :], rden[:, :], ALU.mult).then_inc(norm_done, 1)
                for t in range(4):
                    dve.wait_ge(proj_done, UNITS * g + 12 + t + 1)
                    nc.vector.tensor_tensor(x_sb[:, 4 * g + t, :], proj[:, t % 2, :], x_sb[:, 4 * g + t, :],
                                            ALU.add).then_inc(proj_free, 1)
                assert link.n == DVE_LINKS

        @block.scalar
        def _(act):
            with act.Fori(0, T // G) as g:
                for u in range(2 * DC):
                    act.wait_ge(proj_done, UNITS * g + u + 1)
                    nc.scalar.activation(qk[:, 0, u, :], proj[:, u % 2, :], ACT.Copy).then_inc(high_ready, 1)
                act.wait_ge(mt_done, g + 1)
                nc.scalar.activation(mt[:, :], pv[0:H, 0:G // 2].bitcast(F16), ACT.Copy).then_inc(mt_ready, 1)

                def high(hq):
                    act.wait_ge(norm_done, 4 * g + hq + 2)
                    nc.scalar.activation(yt[:, 0, hq, :], yf[:, hq % 2, :], ACT.Copy).then_inc(y_high, 1)

                for p in range(PAIRS):
                    act.wait_ge(st_done, PAIRS * g + p + 1)
                    if p >= 4:
                        act.wait_ge(pv_done, 8 * g + p // 2 - 1)
                    nc.scalar.activation(pt[:, p % 4, :, 0:3 * P], sc[:, 2 * (p % 2):2 * (p % 2) + 2, 0:3 * P],
                                         ACT.Exp, scale=SCALE).then_inc(exp_done, 1)
                    if p % 4 == 3 and p > 3:
                        high(p // 4 - 1)
                high(3)

        @block.gpsimd
        def _(pool):
            m = TILES // CLEARS
            for n in range(0, TILES, m):
                pool.dma_start(slot_rows[n * P:(n + m) * P].rearrange("(a p) n -> p a n", p=P),
                               zeros[:, :].rearrange("p (o n) -> p o n", o=1).to_broadcast([P, m, 2 * D])
                               ).then_inc(cleared, 16)
            spare = TILES - T * TOPK // P
            pool.dma_start(slot_outs[(TILES - spare) * P:].rearrange("(a p) n -> p a n", p=P),
                           zeros[:, :].bitcast(F32).rearrange("p (o n) -> p o n", o=1).to_broadcast([P, spare, D])
                           ).then_inc(cleared, 16)
            with pool.Fori(0, T // G) as g:
                for hq in range(4):
                    pool.wait_ge(y_high, 4 * g + hq + 1)
                    nc.gpsimd.tensor_tensor(yt[:, 1, hq, :], yf[:, hq % 2, :], yt[:, 0, hq, :],
                                            ALU.subtract).then_inc(y_low, 1)
            pool.wait_ge(cleared, 16 * CLEARS + 16)

        @block.sync
        def _(sp):
            with sp.Fori(0, T // G) as g:
                for side in range(2):
                    sp.wait_ge(proj_free, UNITS * g + 2 + DC * (side + 1))
                    for part in range(2):
                        sp.dma_start(scratch[part, side * D:(side + 1) * D].rearrange("(c p) n -> p c n", p=P),
                                     qk[:, part, side * DC:(side + 1) * DC, :]).then_inc(spilled, 16)
                sp.wait_ge(spilled, 64 * g + 64)
                for side, (tile, parts) in enumerate(((qs, (0, 0, 1)), (ks, (0, 1, 0)))):
                    for r, part in enumerate(parts):
                        sp.dma_start(tile[r * HD:(r + 1) * HD, :, :],
                                     scratch[part, side * D:(side + 1) * D].rearrange("(h d) n -> d h n", d=HD)
                                     ).then_inc(stacked, 16)
                sp.wait_ge(mt_ready, g + 1)
                sp.dma_start(qs[PB:PR, :, :], mt[:, :]).then_inc(row_loaded, 16)


def row_moments(nc, name, x_sb, mean, rstd):
    with ExitStack() as ctx:
        sb = lambda n, s, d: ctx.enter_context(nc.sbuf_tensor(f"{name}_{n}", s, d))
        sem = lambda n: ctx.enter_context(nc.semaphore(f"{name}_{n}"))
        stats = sb("stats", [P, NT, 6], F32)
        moments = sb("moments", [P, NT, 2], F32)
        std = sb("std", [P, NT], F32)
        dve_chain, moments_ready, std_ready = sem("dve_chain"), sem("moments_ready"), sem("std_ready")
        block = ctx.enter_context(nc.Block())

        @block.vector
        def _(dve):
            link = Chain(dve, dve_chain)
            for t in range(NT):
                link(nc.vector.bn_stats(stats[:, t, :], x_sb[:, t, :]))
            dve.wait_ge(dve_chain, NT)
            for t in range(NT):
                link(nc.vector.bn_aggr(moments[:, t, :], stats[:, t, :]))
            dve.wait_ge(dve_chain, 2 * NT)
            nc.vector.tensor_scalar(std[:, :], moments[:, :, 1], EPS, None, ALU.add).then_inc(moments_ready, 1)
            link(nc.vector.tensor_copy(mean[:, :], moments[:, :, 0]))
            dve.wait_ge(std_ready, 1)
            nc.vector.reciprocal(rstd[:, :], std[:, :])

        @block.scalar
        def _(act):
            act.wait_ge(moments_ready, 1)
            nc.scalar.activation(std[:, :], std[:, :], ACT.Sqrt).then_inc(std_ready, 1)


def cross_attention(nc, split, x_sb, ctx_dram, enc_dram, w_dram, b_dram, bv_dram, wm_dram, bm_dram, we_dram, we_pairs):
    SCALE = float(XHD) ** -0.5
    BANKS, QUADS = 4 * H, 16
    MADE, OUT, SWAP, ADD, HIGH, LOW = ({2 * u + k: u for u in range(4)} for k in range(1, 7))
    X_NORM, X_HIGH, X_LOW = 11, 12, 13
    FIRST_PIECE = 4
    WP = 2 * NP
    with ExitStack() as ctx:
        sb = lambda n, s, d: ctx.enter_context(nc.sbuf_tensor(f"ca_{n}", s, d))
        pb = lambda n, s, d: ctx.enter_context(nc.psum_tensor(f"ca_{n}", s, d))
        sem = lambda n: ctx.enter_context(nc.semaphore(f"ca_{n}"))
        w = sb("w", [P, 2, 3, CC, CH], F16)
        wm = sb("wm", [P, 2, 4, CH], F16)
        with ExitStack() as raws:
            raw = raws.enter_context(nc.sbuf_tensor("ca_raw", [P, 3, CC, CH], F32))
            rawm = raws.enter_context(nc.sbuf_tensor("ca_rawm", [P, 4, CH], F32))
            jobs = [(w_dram.rearrange("s (c p) e -> p s c e", p=P), raw[:, :, :, :], (w[:, 0], w[:, 1])),
                    (wm_dram.rearrange("q p e -> p q e"), rawm[:, :, :], (wm[:, 0], wm[:, 1]))]
            split(jobs)
        mean = sb("mean", [P, NT], F32)
        rstd = sb("rstd", [P, NT], F32)
        row_moments(nc, "ca_ln", x_sb, mean, rstd)

        norm = sb("norm", [P, CC, G], F32)
        xn = sb("xn", [P, 2, CC, G], F16)
        rawc = sb("rawc", [P, CC, G], F32)
        cx = sb("cx", [P, 2, 2, CC, G], F16)
        wraw = sb("wraw", [P, 3, IC * D // 2], F32)
        wpair = sb("wpair", [P, 2, 2, IC * D // 2], F16)
        freq = sb("freq", [P, 2, G], F32)
        sign = sb("sign", [P, 1], F32)
        signi = sb("signi", [P, 1], I32)
        bqk = sb("bqk", [P, 4], F32)
        bm = sb("bm", [P, CC], F32)
        bv = sb("bv", [P, H, XHD], F32)
        tf = sb("tf", [P, 4, G], F32)
        waited = sb("waited", [P, 4], F32)
        rf = sb("rf", [P, G], F32)
        qk = sb("qk", [P, 2, 4, G], F16)
        qs = sb("qs", [P, 2, H, G], F16)
        ks = sb("ks", [P, 2, H, G], F16)
        va = sb("va", [P, 4, H, 2 * XHD], F32)
        identh = sb("identh", [P, P], F16)
        mx = sb("mx", [P, 4, H], F32)
        nm = sb("nm", [P, 4, H], F16)
        nmf = sb("nmf", [P, 4, H], F32)
        mt = sb("mt", [H, G], F16)
        pt = sb("pt", [P, 8, G], F32)
        turned = sb("turned", [P, G // 32, 32], F32)
        rden = sb("rden", [P, G // 32], F32)
        quot = sb("quot", [P, G // 32, 32], F32)
        yf = sb("yf", [P, 2, G], F32)
        yt = sb("yt", [P, 2, 4, G], F16)
        scratch = nc.dram_tensor("ca_scratch", (2, 4, P, G), F16).ap()
        proj = pb("proj", [P, 2, G], F32)
        sc = pb("sc", [P, 2, G], F32)
        st = pb("st", [P, 2, G], F32)
        pv = pb("pv", [P, 2, G], F32)
        loads, made, signed = sem("loads"), sem("made"), sem("signed")
        proj_done, qk_out, v_done, v_out = sem("proj_done"), sem("qk_out"), sem("v_done"), sem("v_out")
        out_done, res_done, swapped, cosed, rotated = (
            sem("out_done"), sem("res_done"), sem("swapped"), sem("cosed"), sem("rotated"))
        high_ready, low_ready = sem("high_ready"), sem("low_ready")
        norm_ready, x_high, x_low = sem("norm_ready"), sem("x_high"), sem("x_low")
        spilled, stacked, maxed, score_done = sem("spilled"), sem("stacked"), sem("maxed"), sem("score_done")
        neg_ready, mt_done, mt_ready, row_loaded = sem("neg_ready"), sem("mt_done"), sem("mt_ready"), sem("row_loaded")
        st_done, exp_done, pv_done, norm_done = sem("st_done"), sem("exp_done"), sem("pv_done"), sem("norm_done")
        turned_out = sem("turned_out")
        y_high, y_low, dve_chain, pre_chain = sem("y_high"), sem("y_low"), sem("dve_chain"), sem("pre_chain")
        c_loaded, c_high, c_low = sem("c_loaded"), sem("c_high"), sem("c_low")
        w_loaded, w_stored = [sem(f"w_loaded{k}") for k in range(3)], [sem(f"w_stored{k}") for k in range(2)]
        w_high, w_low = sem("w_high"), sem("w_low")
        PRE_LINKS, DVE_LINKS = 1, 8

        with nc.Block() as block:
            @block.sync
            def _(sp):
                for f in range(2):
                    for j in range(8):
                        sp.dma_start(freq[j * XHD:(j + 1) * XHD, f, :], enc_dram[f]).then_inc(loads, 16)
                sp.dma_start(bqk[:, :], b_dram).then_inc(loads, 16)
                sp.dma_start(bm[:, :], bm_dram).then_inc(loads, 16)
                sp.dma_start(bv[:, :, :].rearrange("p h d -> p (h d)"), bv_dram).then_inc(loads, 16)
                sp.wait_ge(loads, 16 * 19)

            @block.gpsimd
            def _(pool):
                nc.gpsimd.memset(identh[:, :], 0.0).then_inc(made, 1)
                nc.gpsimd.memset(va[:, :, :, :], 1.0).then_inc(signed, 1)
                nc.gpsimd.memset(quot[:, :, :], 0.0).then_inc(signed, 1)
                pool.wait_ge(made, 1)
                nc.gpsimd.affine_select(out=identh[:, :], in_=identh[:, :], compare_op=ALU.not_equal, fill=1.0,
                                        base=0, pattern=[[-1, P]], channel_multiplier=1).then_inc(signed, 1)
                nc.gpsimd.iota(signi[:, :], pattern=[[0, 1]], base=0, channel_multiplier=1).then_inc(made, 1)

            @block.vector
            def _(dve):
                for tile in (qs, ks):
                    nc.vector.memset(tile[4 * XHD:PB, :, :, :].rearrange("p s h n -> p (s h n)").bitcast(F32), 0.0
                                     ).then_inc(signed, 1)
                nc.vector.memset(ks[PB:PR, :, :, :], 1.0).then_inc(signed, 1)
                dve.wait_ge(made, 2)
                nc.vector.tensor_scalar(signi[:, :], signi[:, :], 1, None, ALU.bitwise_and).then_inc(made, 1)
                dve.wait_ge(made, 3)
                nc.vector.tensor_scalar(sign[:, :], signi[:, :], 2.0, -1.0, ALU.mult, ALU.add).then_inc(made, 1)
                dve.wait_ge(made, 4)
                dve.wait_ge(loads, 16 * 19)
                nc.vector.tensor_scalar(freq[:, 1, :], freq[:, 1, :], sign[:, 0:1], None, ALU.mult).then_inc(made, 1)

        block = ctx.enter_context(nc.Block())

        def all_turns(engine, turn):
            turn(-2, 0, False, False, True, True)
            turn(-1, 1, False, True, True, True)
            with engine.Fori(0, (B - 4) // 2) as i:
                for s in range(2):
                    with engine.Fori(s, s + 1) as j:
                        turn(2 * i + j, s, True, True, True, True)
            turn(B - 4, 0, True, True, True, True)
            turn(B - 3, 1, True, True, True, False)
            turn(B - 2, 0, True, True, False, False)
            turn(B - 1, 1, True, False, False, False)

        @block.tensor
        def _(pe):
            def turn(b, s, attend, maxima, projects, _pairs):
                c, e, sn = b + 1, b + 2, 1 - s

                def project(u):
                    side, oc = u // 2, u % 2
                    if u == 0:
                        pe.wait_ge(x_low, 2 * e + 2)
                    if u == 2:
                        pe.wait_ge(c_low, e + 1)
                    if u >= 2 or maxima:
                        pe.wait_ge(qk_out, 4 * e + u - 1)
                    if u < 2 and attend:
                        pe.wait_ge(res_done, 2 * b + u + 1)
                        pe.wait_ge(v_out, 4 * b + u + 3)
                    split_product(nc, proj[:, oc, :], lambda a, k: w[:, a, side, k, oc * P:(oc + 1) * P],
                                  (lambda p, k: xn[:, p, k, :]) if side == 0 else (lambda p, k: cx[:, s, p, k, :]),
                                  CC).then_inc(proj_done, 1)

                def values(kt):
                    if kt >= 2:
                        pe.wait_ge(v_out, 4 * c + kt - 1)
                    elif projects:
                        pe.wait_ge(qk_out, 4 * e + kt + 3)
                    else:
                        pe.wait_ge(res_done, 2 * b + kt + 1)
                    split_product(nc, proj[:, kt % 2, 0:CH], lambda a, k: cx[:, sn, a, k, kt * P:(kt + 1) * P],
                                  lambda p, k: w[:, p, 2, k, :], CC).then_inc(v_done, 1)

                def scores(n):
                    qt, h = n // H, n % H
                    if n == 0:
                        pe.wait_ge(stacked, 128 * c + 128)
                        if attend:
                            pe.wait_ge(mt_ready, c)
                    if n >= 2:
                        pe.wait_ge(maxed, BANKS * c + n - 1)
                    nc.tensor.matmul(sc[:, n % 2, :], qs[0:QB, sn, h, qt * P:(qt + 1) * P], ks[0:QB, sn, h, :],
                                     start=True, stop=True).then_inc(score_done, 1)

                def turn_maxima():
                    pe.wait_ge(neg_ready, c + 1)
                    mtp = sc[0:H, 0, 0:G // 2].bitcast(F16)
                    for t in range(4):
                        last = nc.tensor.transpose(mtp[:, t * P:(t + 1) * P], nm[:, t, :], identh[:, :])
                    last.then_inc(mt_done, 1)

                def transposed_scores(p):
                    hq, kt, j = p // 16, p // 4 % 4, p % 4
                    if p == 0:
                        pe.wait_ge(row_loaded, 16 * b + 16)
                    if p >= 2:
                        pe.wait_ge(exp_done, BANKS * b + p - 1)
                    nc.tensor.matmul(st[:, p % 2, :], ks[0:PR, s, 4 * hq + j, kt * P:(kt + 1) * P],
                                     qs[0:PR, s, 4 * hq + j, :], start=True, stop=True).then_inc(st_done, 1)

                def weigh_values(qd):
                    hq, kt = qd // 4, qd % 4
                    if qd == 0:
                        pe.wait_ge(v_out, 4 * b + 4)
                    pe.wait_ge(exp_done, BANKS * b + 4 * qd + 4)
                    if kt == 0:
                        pe.wait_ge(turned_out, 4 * b + hq + 1)
                    for j in range(4):
                        last = nc.tensor.matmul(pv[j * 32:(j + 1) * 32, hq % 2, :], va[:, kt, 4 * hq + j, :],
                                                pt[:, (4 * qd + j) % 8, :], start=(kt == 0),
                                                stop=(kt == 3), skip_group_check=True, tile_position=(0, j * 32))
                    last.then_inc(pv_done, 1)

                if attend:
                    for p in range(4):
                        transposed_scores(p)
                for qd in range(QUADS):
                    for k in range(4):
                        if attend and qd + 1 < QUADS:
                            transposed_scores(4 * qd + 4 + k)
                        if maxima:
                            scores(4 * qd + k)
                    if projects and qd in MADE:
                        project(MADE[qd])
                    if attend:
                        weigh_values(qd)
                if maxima:
                    values(0)
                    values(1)
                    turn_maxima()
                    values(2)
                    values(3)
                if attend:
                    pe.wait_ge(y_low, 4 * b + 4)
                    for oc in range(2):
                        pe.wait_ge(*((v_out, 4 * c + 3 + oc) if maxima else (res_done, 2 * b + oc + 1)))
                        split_product(nc, proj[:, oc, :], lambda a, k: wm[:, a, k, oc * P:(oc + 1) * P],
                                      lambda p, k: yt[:, p, k, :], 4).then_inc(out_done, 1)
            all_turns(pe, turn)

        @block.vector
        def _(dve):
            dve.sem_inc(turned_out, 2)
            dve.sem_inc(res_done, 2)

            def normalise(j, c):
                nc.vector.tensor_scalar(norm[:, j, :], x_sb[:, 2 * c + j, :], mean[:, bass.ds(2 * c + j, 1)],
                                        rstd[:, bass.ds(2 * c + j, 1)], ALU.subtract, ALU.mult).then_inc(norm_ready, 1)

            def x_low_part(j, c):
                dve.wait_ge(x_high, 2 * c + j + 1)
                nc.vector.tensor_tensor(xn[:, 1, j, :], norm[:, j, :], xn[:, 0, j, :], ALU.subtract).then_inc(x_low, 1)

            for j in range(CC):
                normalise(j, 0)
            for j in range(CC):
                x_low_part(j, 0)

            def turn(b, s, attend, maxima, projects, pairs):
                c, e, f = b + 1, b + 2, b + 3
                link = Chain(dve, dve_chain, DVE_LINKS, b)

                def swap(u):
                    dve.wait_ge(qk_out, 4 * e + u + 1)
                    if u or maxima:
                        dve.wait_ge(rotated, 4 * e + u)
                    nc.vector.memset(waited[:, u:u + 1], 0.0)
                    nc.vector.stream_shuffle(rf[:, :], tf[:, u, :], [i ^ 1 for i in range(32)]).then_inc(swapped, 1)
                    dve.wait_ge(swapped, 8 * e + 2 * u + 1)
                    nc.vector.tensor_tensor(rf[:, :], rf[:, :], freq[:, 1, :], ALU.mult).then_inc(swapped, 1)

                def add(u):
                    dve.wait_ge(swapped, 8 * e + 2 * u + 2)
                    dve.wait_ge(cosed, 4 * e + u + 1)
                    nc.vector.tensor_tensor(tf[:, u, :], tf[:, u, :], rf[:, :], ALU.add).then_inc(rotated, 1)

                def low_part(u):
                    dve.wait_ge(high_ready, 4 * e + u + 1)
                    nc.vector.tensor_tensor(qk[:, 1, u, :], tf[:, u, :], qk[:, 0, u, :],
                                            ALU.subtract).then_inc(low_ready, 1)

                def maximum(n):
                    dve.wait_ge(score_done, BANKS * c + n + 1)
                    nc.vector.reduce_max(mx[:, n // H, n % H:n % H + 1], sc[:, n % 2, :], AX.X).then_inc(maxed, 1)

                def divide(hq):
                    dve.wait_ge(pv_done, 16 * b + 4 * hq + 4)
                    nc.vector.transpose(turned[:, :, :].rearrange("p a b -> p (a b)"), pv[:, hq % 2, :]
                                        ).then_inc(turned_out, 1)
                    dve.wait_ge(turned_out, 4 * b + hq + 3)
                    link.then_wait(nc.vector.reciprocal(rden[:, :], turned[:, :, XHD]))
                    link.then_wait(nc.vector.tensor_tensor(
                        quot[:, :, 0:XHD], turned[:, :, 0:XHD],
                        rden[:, :].rearrange("p (a o) -> p a o", o=1).to_broadcast([P, G // 32, XHD]), ALU.mult))
                    if hq >= 2:
                        dve.wait_ge(y_low, 4 * b + hq - 1)
                    nc.vector.transpose(yf[:, hq % 2, :], quot[:, :, :].rearrange("p a b -> p (a b)")
                                        ).then_inc(norm_done, 1)
                    dve.wait_ge(norm_done, 4 * b + hq + 1)

                for qd in range(QUADS):
                    if maxima:
                        for k in range(4):
                            maximum(4 * qd + k)
                    for step, at in ((add, ADD), (low_part, LOW), (swap, SWAP)):
                        if projects and qd in at:
                            step(at[qd])
                    for step, at in ((normalise, X_NORM), (x_low_part, X_LOW)):
                        if pairs and qd == at:
                            for j in range(CC):
                                step(j, f)
                    if maxima and qd == QUADS - 1:
                        dve.wait_ge(maxed, BANKS * c + BANKS)
                        nc.vector.tensor_scalar(nmf[:, :, :], mx[:, :, :], -1.0, M_CLAMP, ALU.mult, ALU.min
                                                ).then_inc(pre_chain, 1)
                        dve.wait_ge(pre_chain, c + 1)
                        nc.vector.tensor_scalar(nm[:, :, :], nmf[:, :, :], -M_CLAMP, None, ALU.max).then_inc(neg_ready, 1)
                    if attend and qd % 4 == 3:
                        divide(qd // 4)
                if maxima:
                    for kt in range(4):
                        dve.wait_ge(v_done, 4 * c + kt + 1)
                        nc.vector.tensor_tensor(va[:, kt, :, 0:XHD],
                                                proj[:, kt % 2, 0:CH].rearrange("p (h d) -> p h d", h=H), bv[:, :, :],
                                                ALU.add).then_inc(v_out, 1)
                if attend:
                    for oc in range(2):
                        dve.wait_ge(out_done, 2 * b + oc + 1)
                        nc.vector.scalar_tensor_tensor(x_sb[:, 2 * b + oc, :], proj[:, oc, :], bm[:, oc:oc + 1],
                                                       x_sb[:, 2 * b + oc, :], ALU.add, ALU.add).then_inc(res_done, 1)
                    assert link.n == DVE_LINKS
            all_turns(dve, turn)

        @block.scalar
        def _(act):
            def split_piece(b, m):
                n = PIECES[m % NP][1]
                act.wait_ge(w_loaded[m % 3], 16 * (WP // 3 * b + m // 3 + 1))
                act.wait_ge(w_stored[m % 2], 16 * (WP // 2 * b + m // 2 + 1))
                nc.scalar.activation(wpair[:, m % 2, 0, 0:n], wraw[:, m % 3, 0:n], ACT.Copy).then_inc(w_high, 1)

            def x_high_part(j, c):
                act.wait_ge(norm_ready, 2 * c + j + 1)
                nc.scalar.activation(xn[:, 0, j, :], norm[:, j, :], ACT.Copy).then_inc(x_high, 1)

            def c_high_part(f, parity, used):
                act.wait_ge(c_loaded, 16 * f + 16)
                if used:
                    act.wait_ge(v_done, 4 * (f - 1))
                nc.scalar.activation(cx[:, parity, 0, :, :], rawc[:, :, :], ACT.Copy).then_inc(c_high, 1)

            act.sem_inc(w_stored[0], 16)
            act.sem_inc(w_stored[1], 16)
            for j in range(CC):
                x_high_part(j, 0)
            c_high_part(0, 0, False)

            def turn(b, s, attend, maxima, projects, pairs):
                c, e, f = b + 1, b + 2, b + 3

                def out(u):
                    act.wait_ge(proj_done, 4 * e + u + 1)
                    if maxima:
                        act.wait_ge(low_ready, 4 * e + u - 3)
                    nc.scalar.activation(tf[:, u, :], proj[:, u % 2, :], ACT.Identity,
                                         bias=bqk[:, u:u + 1]).then_inc(qk_out, 1)

                def high_part(u):
                    act.wait_ge(rotated, 4 * e + u + 1)
                    if maxima and u == 0:
                        act.wait_ge(spilled, 64 * e)
                    nc.scalar.activation(qk[:, 0, u, :], tf[:, u, :], ACT.Copy).then_inc(high_ready, 1)

                def y_high_part(hq):
                    act.wait_ge(norm_done, 4 * b + hq + 1)
                    nc.scalar.activation(yt[:, 0, hq, :], yf[:, hq % 2, :], ACT.Copy).then_inc(y_high, 1)

                for qd in range(QUADS):
                    for p in range(4 * qd, 4 * qd + 4) if attend else ():
                        act.wait_ge(st_done, BANKS * b + p + 1)
                        if p >= 8:
                            act.wait_ge(pv_done, 16 * b + qd - 1)
                        nc.scalar.activation(pt[:, p % 8, :], st[:, p % 2, :], ACT.Exp, scale=SCALE).then_inc(exp_done, 1)
                    for step, at in ((out, OUT), (high_part, HIGH)):
                        if projects and qd in at:
                            step(at[qd])
                    if attend and qd % 4 == 1 and qd > 4:
                        y_high_part(qd // 4 - 1)
                    if pairs and qd == X_HIGH:
                        for j in range(CC):
                            x_high_part(j, f)
                    if attend and qd >= FIRST_PIECE:
                        split_piece(b, qd - FIRST_PIECE)
                if maxima:
                    act.wait_ge(mt_done, c + 1)
                    nc.scalar.activation(mt[:, :], sc[0:H, 0, 0:G // 2].bitcast(F16), ACT.Copy).then_inc(mt_ready, 1)
                if attend:
                    y_high_part(3)
                if pairs:
                    c_high_part(f, 1 - s, maxima)
            all_turns(act, turn)

        @block.gpsimd
        def _(pool):
            def c_low_part(f, parity):
                pool.wait_ge(c_high, f + 1)
                nc.gpsimd.tensor_tensor(cx[:, parity, 1, :, :], rawc[:, :, :], cx[:, parity, 0, :, :],
                                        ALU.subtract).then_inc(c_low, 1)

            pool.sem_inc(w_low, 1)
            c_low_part(0, 0)

            def turn(b, s, attend, maxima, projects, pairs):
                e, f = b + 2, b + 3

                def y_low_part(hq):
                    pool.wait_ge(y_high, 4 * b + hq + 1)
                    nc.gpsimd.tensor_tensor(yt[:, 1, hq, :], yf[:, hq % 2, :], yt[:, 0, hq, :],
                                            ALU.subtract).then_inc(y_low, 1)

                for qd in range(QUADS):
                    if attend and qd % 4 == 1 and qd > 4:
                        y_low_part(qd // 4 - 1)
                    if attend and qd >= FIRST_PIECE:
                        m = qd - FIRST_PIECE
                        n = PIECES[m % NP][1]
                        pool.wait_ge(w_high, WP * b + m + 1)
                        nc.gpsimd.tensor_tensor(wpair[:, m % 2, 1, 0:n], wraw[:, m % 3, 0:n],
                                                wpair[:, m % 2, 0, 0:n], ALU.subtract).then_inc(w_low, 1)
                    if projects and qd in SWAP:
                        u = SWAP[qd]
                        pool.wait_ge(swapped, 8 * e + 2 * u + 1)
                        nc.gpsimd.tensor_tensor(tf[:, u, :], tf[:, u, :], freq[:, 0, :], ALU.mult).then_inc(cosed, 1)
                if attend:
                    y_low_part(3)
                if pairs:
                    c_low_part(f, 1 - s)
            all_turns(pool, turn)

        @block.sync
        def _(sp):
            def load_context(f):
                sp.dma_start(rawc[:, :, :], ctx_dram[bass.ds(CC * f, CC)].rearrange("t p d -> p t d")
                             ).then_inc(c_loaded, 16)

            def load_piece(b, m):
                at, n = PIECES[m % NP]
                sp.dma_start(wraw[:, m % 3, 0:n], we_dram[2 * b + m // NP, :, at:at + n]).then_inc(w_loaded[m % 3], 16)

            def store_piece(b, m):
                at, n = PIECES[m % NP]
                sp.dma_start(we_pairs[2 * b + m // NP, :, :, at:at + n], wpair[:, m % 2, :, 0:n]
                              ).then_inc(w_stored[m % 2], 16)

            load_context(0)
            load_piece(0, 0)
            load_piece(0, 1)

            def turn(b, s, attend, maxima, projects, pairs):
                c, e, f, sn = b + 1, b + 2, b + 3, 1 - s
                if pairs:
                    sp.wait_ge(c_low, f)
                    load_context(f)
                if projects and maxima:
                    sp.wait_ge(stacked, 128 * e)
                for qd in range(QUADS):
                    if attend and qd >= FIRST_PIECE:
                        m = qd - FIRST_PIECE
                        sp.wait_ge(w_low, WP * b + m + 1)
                        if m:
                            store_piece(b, m - 1)
                        load_piece(b, m + 2)
                    if projects and LOW.get(qd) in (1, 3):
                        side = LOW[qd] // 2
                        sp.wait_ge(low_ready, 4 * e + 2 * side + 2)
                        for part in range(2):
                            sp.dma_start(scratch[part, 2 * side:2 * side + 2].rearrange("u p n -> p u n"),
                                         qk[:, part, 2 * side:2 * side + 2, :]).then_inc(spilled, 16)
                if projects:
                    sp.wait_ge(spilled, 64 * e + 64)
                    if attend:
                        sp.wait_ge(st_done, BANKS * c)
                    for side, (tile, parts) in enumerate(((qs, (0, 0, 1, 1)), (ks, (0, 1, 0, 1)))):
                        for r, part in enumerate(parts):
                            sp.dma_start(tile[r * XHD:(r + 1) * XHD, s, :, :],
                                         scratch[part, 2 * side:2 * side + 2].rearrange("u (h d) n -> d (u h) n", d=XHD)
                                         ).then_inc(stacked, 16)
                if maxima:
                    sp.wait_ge(mt_ready, c + 1)
                    sp.dma_start(qs[PB:PR, sn, :, :], mt[:, :]).then_inc(row_loaded, 16)
                if attend:
                    sp.wait_ge(w_low, WP * c + 1)
                    store_piece(b, WP - 1)
            all_turns(sp, turn)
            for k in range(2):
                sp.wait_ge(w_stored[k], 16 * (WP // 2 * B + 1))
                sp.wait_ge(w_loaded[k], 16 * (WP // 3 * B + 1))


class SharedExpert:

    ROUNDS = T // G
    HIDDEN = T // G * IC

    def __init__(self, nc, split, ctx, name, expert, xn, we_dram, sems, turn):
        self.nc, self.xn, self.turn = nc, xn, turn
        self.units, self.tiles = turn * self.HIDDEN, turn * NT
        sb = lambda n, s, d: ctx.enter_context(nc.sbuf_tensor(f"{name}_{n}", s, d))
        pb = lambda n, s, d: ctx.enter_context(nc.psum_tensor(f"{name}_{n}", s, d))
        pair = sb("pair", [P, 2, WC], F16)
        with nc.sbuf_tensor(f"{name}_raw", [P, WC], F32) as raw:
            halves = [(0, EW), (EW, WC)]
            split([(we_dram[expert, :, a:b], raw[:, a:b],
                                                 (pair[:, 0, a:b], pair[:, 1, a:b])) for a, b in halves])
        self.up = pair[:, :, 0:EW].rearrange("p h (c j i) -> p h c j i", c=DC, j=2)
        self.down = pair[:, :, EW:WC].rearrange("p h (c d) -> p h c d", c=IC)
        self.gate = sb("gate", [P, 2, G], F32)
        self.lin = sb("lin", [P, 2, G], F32)
        self.hf = sb("hf", [P, 2, G], F32)
        self.ht = sb("ht", [P, 2, 2, IC, G], F16)
        self.ab = pb("ab", [P, 2, 2, G], F32)
        self.yp = pb("yp", [P, 2, D], F32)
        self.ab_done, self.lin_done, self.h_done, self.h_high, self.h_low, self.y_done, self.added = sems

    @staticmethod
    def semaphores(nc, ctx):
        return [ctx.enter_context(nc.semaphore(f"sh_{n}"))
                for n in ("ab_done", "lin_done", "h_done", "h_high", "h_low", "y_done", "added")]

    def tensor(self, pe, between=lambda g: None):
        nc = self.nc
        if self.turn == 0:
            pe.sem_inc(self.lin_done, 2)

        def hidden(g):
            for c in range(IC):
                n, rows = g * IC + c, I_ROWS[c]
                pe.wait_ge(self.lin_done, self.units + n + 1)
                for j in range(2):
                    last = split_product(nc, self.ab[0:rows, n % 2, j, :],
                                         lambda a, d: self.up[:, a, d, j, c * P:c * P + rows],
                                         lambda b, d: self.xn[:, b, d, g * G:(g + 1) * G], DC)
                last.then_inc(self.ab_done, 1)

        hidden(0)
        for g in range(self.ROUNDS):
            if g + 1 < self.ROUNDS:
                hidden(g + 1)
            between(g)
            pe.wait_ge(self.h_low, self.units + (g + 1) * IC)
            for t in range(4):
                n = 4 * g + t
                if n >= 2:
                    pe.wait_ge(self.added, self.tiles + n - 1)
                split_product(nc, self.yp[:, n % 2, :],
                              lambda a, c: self.ht[0:I_ROWS[c], g % 2, a, c, t * P:(t + 1) * P],
                              lambda b, c: self.down[0:I_ROWS[c], b, c, :], IC).then_inc(self.y_done, 1)

    def scalar(self, act):
        nc = self.nc
        for n in range(self.HIDDEN):
            g, c, rows, k = n // IC, n % IC, I_ROWS[n % IC], n % 2
            act.wait_ge(self.ab_done, self.units + n + 1)
            if n >= 2:
                act.wait_ge(self.h_done, self.units + n - 1)
            nc.scalar.activation(self.gate[0:rows, k, :], self.ab[0:rows, k, 0, :], ACT.Silu)
            nc.scalar.activation(self.lin[0:rows, k, :], self.ab[0:rows, k, 1, :], ACT.Copy).then_inc(self.lin_done, 1)
            act.wait_ge(self.h_done, self.units + n + 1)
            if g >= 2:
                act.wait_ge(self.y_done, self.tiles + 4 * (g - 1))
            nc.scalar.activation(self.ht[0:rows, g % 2, 0, c, :], self.hf[0:rows, k, :], ACT.Copy
                                 ).then_inc(self.h_high, 1)

    def gpsimd(self, pool, between):
        nc = self.nc
        for n in range(self.HIDDEN):
            g, c, rows, k = n // IC, n % IC, I_ROWS[n % IC], n % 2
            pool.wait_ge(self.lin_done, self.units + n + 3)
            nc.gpsimd.tensor_tensor(self.hf[0:rows, k, :], self.gate[0:rows, k, :], self.lin[0:rows, k, :],
                                    ALU.mult).then_inc(self.h_done, 1)
            pool.wait_ge(self.h_high, self.units + n + 1)
            nc.gpsimd.tensor_tensor(self.ht[0:rows, g % 2, 1, c, :], self.hf[0:rows, k, :],
                                    self.ht[0:rows, g % 2, 0, c, :], ALU.subtract).then_inc(self.h_low, 1)
            between(n)

    def add(self, dve, x_sb, tile):
        dve.wait_ge(self.y_done, self.tiles + tile + 1)
        self.nc.vector.tensor_tensor(x_sb[:, tile, :], self.yp[:, tile % 2, :], x_sb[:, tile, :],
                                     ALU.add).then_inc(self.added, 1)


def route_and_share(nc, split, sems, x_sb, xn, rows, route, wg_dram, we_dram, slot_rows, cleared):
    with ExitStack() as ctx:
        sb = lambda n, s, d: ctx.enter_context(nc.sbuf_tensor(f"ro_{n}", s, d))
        pb = lambda n, s, d: ctx.enter_context(nc.psum_tensor(f"ro_{n}", s, d))
        sem = lambda n: ctx.enter_context(nc.semaphore(f"ro_{n}"))
        shared = SharedExpert(nc, split, ctx, "sh0", E, xn, we_dram, sems, 0)
        raw = sb("raw", [P, DC, E], F32)
        wg = sb("wg", [P, 2, DC, E], F16)
        split([(wg_dram.rearrange("(c p) e -> p c e", p=P), raw[:, :, :],
                                        (wg[:, 0], wg[:, 1]))])
        logits = pb("logits", [P, NT, E], F32)
        places = pb("places", [P, 2, NT, E], F32)
        lg = sb("lg", [P, NT, E], F32)
        s = sb("s", [P, NT, E], F32)
        col = sb("col", [P, NT], F32)
        gs = sb("gs", [P, NT, GR], F32)
        cmp = sb("cmp", [P, NT, E, E], BF16)
        eq = sb("eq", [P, NT, E, E], BF16)
        rank = sb("rank", [P, NT, E], F32)
        before = sb("before", [P, E, E], BF16)
        earlier = sb("earlier", [P, P], BF16)
        every = sb("every", [P, P], BF16)
        chosen = sb("chosen", [P, NT, E], F32)
        chosen16 = sb("chosen16", [P, NT, E], BF16)
        tile_base = sb("tile_base", [P, NT + 1, E], F32)
        totals = sb("totals", [P, NT, E], F32)
        counts = sb("counts", [P, E], I32)
        tiles = sb("tiles", [P, E], F32)
        ends = sb("ends", [P, E], F32)
        base = sb("base", [P, E], F32)
        ones = sb("ones", [P, E], F32)
        slot1 = sb("slot1", [P, NT, E], F32)
        top = sb("top", [P, NT, 8], F32)
        hit = sb("hit", [P, NT, E], F32)
        tile_no = sb("tile_no", [1, TILES], F32)
        passed = sb("passed", [1, TILES, E], F32)
        owner = sb("owner", [1, TILES], F32)
        owner_i = sb("owner_i", [1, TILES], I32)
        made, logits_ready, shifted, exped, chain = (
            sem("made"), sem("logits_ready"), sem("shifted"), sem("exped"), sem("chain"))
        masks_ready, placed, routed, sent = sem("masks_ready"), sem("placed"), sem("routed"), sem("sent")
        block = ctx.enter_context(nc.Block())

        @block.gpsimd
        def _(pool):
            nc.gpsimd.memset(before[:, :, :], 1.0).then_inc(made, 1)
            nc.gpsimd.memset(earlier[:, :], 1.0).then_inc(made, 1)
            nc.gpsimd.memset(every[:, :], 1.0).then_inc(made, 1)
            nc.gpsimd.iota(tile_no[:, :], pattern=[[1, TILES]], base=0, channel_multiplier=0,
                           allow_small_or_imprecise_dtypes=True).then_inc(made, 1)
            pool.wait_ge(made, 4)
            nc.gpsimd.affine_select(out=before[:, :, :], in_=before[:, :, :], compare_op=ALU.is_gt, fill=0.0,
                                    base=0, pattern=[[1, E], [-1, E]], channel_multiplier=0).then_inc(made, 1)
            nc.gpsimd.affine_select(out=earlier[:, :], in_=earlier[:, :], compare_op=ALU.is_gt, fill=0.0,
                                    base=0, pattern=[[1, P]], channel_multiplier=-1).then_inc(made, 1)
            sends = [(t, k) for t in range(NT) for k in range(TOPK)]
            FIRST = 5

            def between(n):
                if n < FIRST:
                    return
                if n == FIRST:
                    pool.wait_ge(routed, 1)
                    pool.wait_ge(cleared, 16 * CLEARS + 16)
                share = -(-len(sends) // (SharedExpert.HIDDEN - FIRST))
                for t, k in sends[(n - FIRST) * share:(n - FIRST + 1) * share]:
                    nc.gpsimd.indirect_dma_start(
                        out=slot_rows, out_offset=bass.IndirectOffsetOnAxis(ap=route["index"][:, t, k:k + 1], axis=0),
                        in_=rows[:, t, :, :].rearrange("p h d -> p (h d)"), in_offset=None).then_inc(sent, 16)

            shared.gpsimd(pool, between)
            pool.wait_ge(sent, 16 * len(sends))

        @block.tensor
        def _(pe):
            for t in range(NT):
                last = split_product(nc, logits[:, t, :], lambda a, c: xn[:, a, c, t * P:(t + 1) * P],
                                     lambda b, c: wg[:, b, c, :], DC)
            last.then_inc(logits_ready, 1)

            def between(g):
                if g != 0:
                    return
                pe.wait_ge(masks_ready, 1)
                flat = chosen16[:, :, :].rearrange("p t e -> p (t e)")
                nc.tensor.matmul(places[:, 0, :, :].rearrange("p t e -> p (t e)"), earlier[:, :], flat,
                                 start=True, stop=True)
                nc.tensor.matmul(places[:, 1, :, :].rearrange("p t e -> p (t e)"), every[:, :], flat,
                                 start=True, stop=True).then_inc(placed, 1)

            shared.tensor(pe, between)

        @block.vector
        def _(dve):
            link = Chain(dve, chain)
            step = link.then_wait
            over = lambda a, n: a.rearrange("p t (g o) -> p t g o", o=1).to_broadcast([P, NT, n, n])
            dve.wait_ge(logits_ready, 1)
            step(nc.vector.reduce_max(col[:, :], logits[:, :, :], AX.X))
            bc = col[:, :].rearrange("p (t o) -> p t o", o=1).to_broadcast([P, NT, E])
            nc.vector.tensor_tensor(lg[:, :, :], logits[:, :, :], bc, ALU.subtract).then_inc(shifted, 1)
            dve.wait_ge(exped, 1)
            step(nc.vector.reduce_sum(col[:, :], s[:, :, :], AX.X))
            step(nc.vector.reciprocal(col[:, :], col[:, :]))
            step(nc.vector.tensor_tensor(s[:, :, :], s[:, :, :], bc, ALU.mult))
            step(nc.vector.reduce_max(gs[:, :, :], s[:, :, :].rearrange("p t (g e) -> p t g e", g=GR), AX.X))
            dve.wait_ge(made, 6)

            def ranks(v, n):
                c4 = cmp[:, :, 0:n, 0:n]
                e4 = eq[:, :, 0:n, 0:n]
                other = v.rearrange("p t (o g) -> p t o g", o=1).to_broadcast([P, NT, n, n])
                own = over(v, n)
                bf = before[:, 0:n, 0:n].rearrange("p (o a) b -> p o a b", o=1).to_broadcast([P, NT, n, n])
                link(nc.vector.tensor_tensor(c4, other, own, ALU.is_gt))
                step(nc.vector.tensor_tensor(e4, other, own, ALU.is_equal))
                step(nc.vector.tensor_tensor(e4, e4, bf, ALU.mult))
                step(nc.vector.tensor_tensor(c4, c4, e4, ALU.add))
                step(nc.vector.reduce_sum(rank[:, :, 0:n], c4, AX.X))

            ranks(gs[:, :, :], GR)
            step(nc.vector.tensor_scalar(gs[:, :, :], rank[:, :, 0:GR], float(TOPK_G), None, ALU.is_lt))
            gb = gs[:, :, :].rearrange("p t (g o) -> p t g o", o=1).to_broadcast([P, NT, GR, EG])
            l4 = lg[:, :, :].rearrange("p t (g e) -> p t g e", g=GR)
            step(nc.vector.tensor_tensor(l4, s[:, :, :].rearrange("p t (g e) -> p t g e", g=GR), gb, ALU.mult))
            step(nc.vector.tensor_scalar(gs[:, :, :], gs[:, :, :], -1.0, None, ALU.add))
            step(nc.vector.tensor_tensor(l4, l4, gb, ALU.add))
            ranks(lg[:, :, :], E)
            step(nc.vector.tensor_scalar(chosen[:, :, :], rank[:, :, :], float(TOPK), None, ALU.is_lt))
            nc.vector.tensor_copy(chosen16[:, :, :], chosen[:, :, :]).then_inc(masks_ready, 1)
            link(nc.vector.memset(tile_base[:, 0, :], 0.0))
            step(nc.vector.memset(ones[:, :], 1.0))
            dve.wait_ge(placed, 1)
            step(nc.vector.tensor_copy(totals[:, :, :], places[:, 1, :, :]))
            for t in range(NT):
                step(nc.vector.tensor_tensor(tile_base[:, t + 1, :], tile_base[:, t, :], totals[:, t, :], ALU.add))
            step(nc.vector.tensor_scalar(counts[:, :], tile_base[:, NT, :], float(P - 1), None, ALU.add))
            step(nc.vector.tensor_scalar(counts[:, :], counts[:, :], 7, None, ALU.arith_shift_right))
            step(nc.vector.tensor_copy(tiles[:, :], counts[:, :]))
            step(nc.vector.tensor_tensor_scan(ends[:, :], ones[:, :], tiles[:, :], 0.0, ALU.mult, ALU.add))
            step(nc.vector.tensor_tensor(base[:, :], ends[:, :], tiles[:, :], ALU.subtract))
            step(nc.vector.tensor_scalar(base[:, :], base[:, :], float(P), 1.0, ALU.mult, ALU.add))
            step(nc.vector.tensor_tensor(slot1[:, :, :], places[:, 0, :, :], tile_base[:, 0:NT, :], ALU.add))
            step(nc.vector.tensor_tensor(slot1[:, :, :], slot1[:, :, :],
                                         base[:, :].rearrange("p (o e) -> p o e", o=1).to_broadcast([P, NT, E]), ALU.add))
            step(nc.vector.tensor_tensor(slot1[:, :, :], slot1[:, :, :], chosen[:, :, :], ALU.mult))
            for t in range(NT):
                link(nc.vector.max(top[:, t, :], slot1[:, t, :]))
            dve.wait_ge(chain, link.n)
            step(nc.vector.tensor_scalar(route["index"][:, :, :], top[:, :, 0:TOPK], -1.0, None, ALU.add))
            nc.vector.memset(hit[:, :, :], 0.0).then_inc(routed, 1)
            dve.wait_ge(routed, 1)
            for k in range(TOPK):
                tk = top[:, :, k:k + 1].to_broadcast([P, NT, E])
                step(nc.vector.tensor_tensor(hit[:, :, :], slot1[:, :, :], tk, ALU.is_equal))
                step(nc.vector.tensor_tensor(hit[:, :, :], hit[:, :, :], s[:, :, :], ALU.mult))
                step(nc.vector.reduce_sum(route["weight"][:, :, k], hit[:, :, :], AX.X))
            step(nc.vector.tensor_copy(route["ends"][:, :], ends[0:1, :]))
            step(nc.vector.tensor_tensor(
                passed[:, :, :], tile_no[:, :].rearrange("p (t o) -> p t o", o=1).to_broadcast([1, TILES, E]),
                ends[0:1, :].rearrange("p (o e) -> p o e", o=1).to_broadcast([1, TILES, E]), ALU.is_ge))
            step(nc.vector.reduce_sum(owner[:, :], passed[:, :, :], AX.X))
            step(nc.vector.tensor_scalar(owner[:, :], owner[:, :], float(E - 1), None, ALU.min))
            step(nc.vector.tensor_copy(owner_i[:, :], owner[:, :]))
            step(nc.vector.tensor_scalar(route["slots"][:, :], owner_i[:, :], 1, None, ALU.bitwise_and))
            step(nc.vector.tensor_scalar(route["arrivals"][:, :], owner[:, :], 16.0, 16.0, ALU.mult, ALU.add))
            step(nc.vector.tensor_scalar(route["pairs"][:, :], ends[0:1, E - 1:E], 1.0, None, ALU.add))
            step(nc.vector.tensor_scalar(route["pairs"][:, :], route["pairs"][:, :], 1, None, ALU.arith_shift_right))
            for t in range(NT):
                shared.add(dve, x_sb, t)

        @block.scalar
        def _(act):
            act.wait_ge(shifted, 1)
            nc.scalar.activation(s[:, :, :], lg[:, :, :], ACT.Exp).then_inc(exped, 1)
            shared.scalar(act)


def routed_experts(nc, ident, route, we_pairs, slot_rows, slot_outs):
    with ExitStack() as ctx:
        sb = lambda n, s, d: ctx.enter_context(nc.sbuf_tensor(f"re_{n}", s, d))
        pb = lambda n, s, d: ctx.enter_context(nc.psum_tensor(f"re_{n}", s, d))
        sem = lambda n: ctx.enter_context(nc.semaphore(f"re_{n}"))
        w = sb("w", [P, 2, 2, WC], F16)
        up = w[:, :, :, 0:EW].rearrange("p s h (c j i) -> p s h c j i", c=DC, j=2)
        down = w[:, :, :, EW:WC].rearrange("p s h (c d) -> p s h c d", c=IC)
        xr = sb("xr", [P, 2, 2 * D], F16)
        xt = sb("xt", [P, 2, 2 * DC, P], F16)
        gate = sb("gate", [P, 2, I], F32)
        hf = sb("hf", [P, 2, I], F32)
        hp = sb("hp", [P, 2, 2, I], F16)
        ht = sb("ht", [P, 2, 2 * IC, P], F16)
        ys = sb("ys", [P, 2, D], F32)
        waited = sb("waited", [P, 4], F32)
        ab = pb("ab", [P, 2, 2, G], F32)
        xt_ps = pb("xt_ps", [P, 2 * DC, P], F16)
        ht_ps = pb("ht_ps", [P, 2 * DC, P], F16)
        yp = pb("yp", [P, 2, D], F32)
        w_loaded = sem("w_loaded")
        x_loaded, y_stored = [sem("x_loaded0"), sem("x_loaded1")], [sem("y_stored0"), sem("y_stored1")]
        x_turned, xt_ready, ab_done, gate_ready, h_ready = (
            sem("x_turned"), sem("xt_ready"), sem("ab_done"), sem("gate_ready"), sem("h_ready"))
        h_high, h_low, h_turned, ht_ready, y_done, ys_ready, clean = (
            sem("h_high"), sem("h_low"), sem("h_turned"), sem("ht_ready"), sem("y_done"), sem("ys_ready"), sem("clean"))
        block = ctx.enter_context(nc.Block())

        def turns(engine):
            return engine.value_load(route["pairs"][0:1, 0:1], min_val=1, max_val=(TILES - 4) // 2)

        @block.sync
        def _(sp):
            def load(e, slot):
                sp.dma_start(w[:, slot, :, :], we_pairs[e]).then_inc(w_loaded, 16)

            load(0, 0)
            sp.wait_ge(w_loaded, 16)
            load(1, 1)
            with sp.Fori(1, E // 2) as i:
                for k in range(2):
                    sp.wait_ge(w_loaded, 32 * i + 16 * k)
                    done = sp.value_load(route["ends"][0:1, bass.ds(2 * i + k - 2, 1)], min_val=0, max_val=TILES)
                    sp.wait_ge(y_done, done + 2)
                    load(2 * i + k, k)
            sp.wait_ge(w_loaded, 16 * E)

        @block.tensor
        def _(pe):
            pe.sem_inc(y_done, 2)
            pe.sem_inc(h_ready, 1)

            def turn_rows(s, bank_free, arrived):
                pe.wait_ge(x_loaded[s], arrived)
                if bank_free is not None:
                    pe.wait_ge(xt_ready, bank_free)
                for c in range(2 * DC):
                    last = nc.tensor.transpose(xt_ps[:, c, :], xr[:, s, c * P:(c + 1) * P], ident[:, :])
                last.then_inc(x_turned, 1)

            def hidden(s, slot, arrived, tile):
                pe.wait_ge(w_loaded, arrived)
                pe.wait_ge(xt_ready, tile + 1)
                pe.wait_ge(h_ready, tile)
                for j in range(2):
                    last = split_product(
                        nc, ab[:, s, j, 0:I], lambda a, c: xt[:, s, a * DC + c, :],
                        lambda b, c: up[:, bass.ds(slot, 1), b, c, j, :].rearrange("p o i -> p (o i)"), DC)
                last.then_inc(ab_done, 1)

            def turn_hidden(s, tile):
                pe.wait_ge(h_low, tile + 1)
                pe.wait_ge(ht_ready, tile + 1)
                for h in range(2):
                    for c in range(IC):
                        last = nc.tensor.transpose(ht_ps[0:I_ROWS[c], h * IC + c, :],
                                                   hp[:, s, h, c * P:c * P + I_ROWS[c]], ident[:, :])
                last.then_inc(h_turned, 1)

            def output(s, slot, tile):
                pe.wait_ge(ht_ready, tile + 2)
                pe.wait_ge(ys_ready, tile + 1)
                split_product(
                    nc, yp[:, s, :], lambda a, c: ht[0:I_ROWS[c], s, a * IC + c, :],
                    lambda b, c: down[0:I_ROWS[c], bass.ds(slot, 1), b, c, :].rearrange("p o d -> p (o d)"), IC
                ).then_inc(y_done, 1)

            n = turns(pe)
            turn_rows(0, None, 16)
            pe.wait_ge(clean, 1)
            first = pe.value_load(route["slots"][0:1, 0:1], min_val=0, max_val=1)
            pe.wait_ge(w_loaded, pe.value_load(route["arrivals"][0:1, 0:1], min_val=16, max_val=16 * E))
            pe.wait_ge(xt_ready, 1)
            for j in range(2):
                last = split_product(
                    nc, ab[:, 0, j, 0:I], lambda a, c: xt[:, 0, a * DC + c, :],
                    lambda b, c: up[:, bass.ds(first, 1), b, c, j, :].rearrange("p o i -> p (o i)"), DC)
            last.then_inc(ab_done, 1)
            turn_rows(1, 1, 16)
            with pe.Fori(0, n) as i:
                at = [pe.value_load(route["slots"][0:1, bass.ds(2 * i + d, 1)], min_val=0, max_val=1) for d in range(3)]
                arrived = [pe.value_load(route["arrivals"][0:1, bass.ds(2 * i + d, 1)], min_val=16, max_val=16 * E)
                           for d in (1, 2)]
                for s in range(2):
                    tile = 2 * i + s
                    hidden(1 - s, at[s + 1], arrived[s], tile + 1)
                    turn_hidden(s, tile)
                    turn_rows(s, tile + 2, 16 * i + 32)
                    output(s, at[s], tile)

        @block.scalar
        def _(act):
            def load(s, tile):
                act.dma_start(xr[:, s, :], slot_rows.rearrange("(t p) n -> t p n", p=P)[tile]
                              ).then_inc(x_loaded[s], 16)

            def keep_rows(s, tile):
                act.wait_ge(x_turned, tile + 1)
                nc.scalar.activation(xt[:, s, :, :], xt_ps[:, :, :], ACT.Copy).then_inc(xt_ready, 1)

            load(0, 0)
            load(1, 1)
            n = turns(act)
            for s in range(2):
                keep_rows(s, s)
                load(s, s + 2)
            with act.Fori(0, n) as i:
                for s in range(2):
                    tile = 2 * i + s
                    act.wait_ge(ab_done, tile + 1)
                    nc.scalar.activation(gate[:, s, :], ab[:, s, 0, 0:I], ACT.Silu).then_inc(gate_ready, 1)
                    act.wait_ge(h_ready, tile + 2)
                    nc.scalar.activation(hp[:, s, 0, :], hf[:, s, :], ACT.Copy).then_inc(h_high, 1)
                    keep_rows(s, tile + 2)
                    load(s, tile + 4)
                    act.wait_ge(ys_ready, tile + 3)
                    act.dma_start(slot_outs.rearrange("(t p) n -> t p n", p=P)[tile], ys[:, s, :]
                                  ).then_inc(y_stored[s], 16)

        @block.vector
        def _(dve):
            dve.sem_inc(ht_ready, 1)
            dve.sem_inc(ys_ready, 2)
            for s in range(2):
                dve.sem_inc(y_stored[s], 16)
            nc.vector.memset(ht_ps[:, :, :].rearrange("p c n -> p (c n)").bitcast(F32), 0.0).then_inc(clean, 1)
            n = turns(dve)
            with dve.Fori(0, n) as i:
                for s in range(2):
                    tile = 2 * i + s
                    dve.wait_ge(gate_ready, tile + 1)
                    nc.vector.tensor_tensor(hf[:, s, :], ab[:, s, 1, 0:I], gate[:, s, :], ALU.mult).then_inc(h_ready, 1)
                    dve.wait_ge(h_high, tile + 1)
                    nc.vector.tensor_tensor(hp[:, s, 1, :], hf[:, s, :], hp[:, s, 0, :], ALU.subtract).then_inc(h_low, 1)
                    dve.wait_ge(h_turned, tile + 1)
                    dve.wait_ge(y_done, tile + 1)
                    nc.vector.tensor_copy(ht[:, s, :, :], ht_ps[:, 0:2 * IC, :]).then_inc(ht_ready, 1)
                    dve.wait_ge(y_done, tile + 3)
                    dve.wait_ge(y_stored[s], 16 * i + 16)
                    nc.vector.tensor_copy(ys[:, s, :], yp[:, s, :]).then_inc(ys_ready, 1)
            for s in range(2):
                dve.wait_ge(y_stored[s], 16 * n + 16)
                nc.vector.memset(waited[:, 2 * s:2 * s + 1], 0.0)
                dve.wait_ge(x_loaded[s], 16 * n + 32)
                nc.vector.memset(waited[:, 2 * s + 1:2 * s + 2], 0.0)


def combine_and_share(nc, split, sems, x_sb, xn, route, we_dram, slot_outs, out_dram):
    RING = 4
    with ExitStack() as ctx:
        sb = lambda n, s, d: ctx.enter_context(nc.sbuf_tensor(f"co_{n}", s, d))
        sem = lambda n: ctx.enter_context(nc.semaphore(f"co_{n}"))
        shared = SharedExpert(nc, split, ctx, "sh1", E + 1, xn, we_dram, sems, 1)
        yg = sb("yg", [P, RING, D], F32)
        fetched = [sem(f"fetched{r}") for r in range(RING)]
        used, ready, stored = sem("used"), sem("ready"), sem("stored")
        fetches = [(t, k) for t in range(NT) for k in range(TOPK)]
        block = ctx.enter_context(nc.Block())

        @block.gpsimd
        def _(pool):
            def fetch(m):
                t, k = fetches[m]
                if m >= RING:
                    pool.wait_ge(used, m - RING + 1)
                nc.gpsimd.indirect_dma_start(
                    out=yg[:, m % RING, :], out_offset=None, in_=slot_outs,
                    in_offset=bass.IndirectOffsetOnAxis(ap=route["index"][:, t, k:k + 1], axis=0)
                ).then_inc(fetched[m % RING], 16)

            def between(n):
                share = -(-len(fetches) // SharedExpert.HIDDEN)
                for m in range(n * share, min((n + 1) * share, len(fetches))):
                    fetch(m)
            shared.gpsimd(pool, between)

        @block.tensor
        def _(pe):
            shared.tensor(pe)

        @block.scalar
        def _(act):
            shared.scalar(act)

        @block.vector
        def _(dve):
            def combine(t):
                for k in range(TOPK):
                    m = TOPK * t + k
                    dve.wait_ge(fetched[m % RING], 16 * (m // RING + 1))
                    nc.vector.scalar_tensor_tensor(x_sb[:, t, :], yg[:, m % RING, :], route["weight"][:, t, k:k + 1],
                                                   x_sb[:, t, :], ALU.mult, ALU.add).then_inc(used, 1)
                    dve.wait_ge(used, m + 1)

            for t in range(4):
                combine(t)
            for t in range(NT):
                shared.add(dve, x_sb, t)
                if t + 4 < NT:
                    combine(t + 4)

        @block.sync
        def _(sp):
            for t in range(0, NT, 4):
                sp.wait_ge(used, TOPK * (t + 4))
                sp.wait_ge(shared.added, shared.tiles + t + 4)
                sp.dma_start(out_dram[t:t + 4].rearrange("t p d -> p t d"), x_sb[:, t:t + 4, :]).then_inc(stored, 16)
            sp.wait_ge(stored, 16 * (NT // 4))


def decoder_block(nc, a):
    with ExitStack() as ctx:
        sb = lambda n, s, d: ctx.enter_context(nc.sbuf_tensor(n, s, d))
        x_sb = sb("x_sb", [P, NT, D], F32)
        ident = sb("ident", [P, P], F16)
        made = ctx.enter_context(nc.semaphore("ident_made"))
        split = WeightSplit(nc, ctx)
        cleared = ctx.enter_context(nc.semaphore("cleared"))
        we_pairs = nc.dram_tensor("we_pairs", (E, P, 2, WC), F16).ap()
        slot_rows = nc.dram_tensor("slot_rows", (TILES * P, 2 * D), F16).ap()
        slot_outs = nc.dram_tensor("slot_outs", (TILES * P, D), F32).ap()
        with nc.Block() as block:
            @block.gpsimd
            def _(pool):
                nc.gpsimd.memset(ident[:, :], 0.0).then_inc(made, 1)
                pool.wait_ge(made, 1)
                nc.gpsimd.affine_select(out=ident[:, :], in_=ident[:, :], compare_op=ALU.not_equal, fill=1.0,
                                        base=0, pattern=[[-1, P]], channel_multiplier=1).then_inc(made, 1)
        self_attention(nc, split, x_sb, ident, a["x"], a["wqkv"], a["wout"], slot_rows, slot_outs, cleared)
        cross_attention(nc, split, x_sb, a["ctx"], a["enc"], a["wx"], a["bx"], a["bv"], a["wm"], a["bm"], a["we"], we_pairs)
        with ExitStack() as ffn:
            sf = lambda n, s, d: ffn.enter_context(nc.sbuf_tensor(n, s, d))
            xn = sf("fx_xn", [P, 2, DC, T], F16)
            sems = SharedExpert.semaphores(nc, ffn)
            route = {
                "index": sf("fx_index", [P, NT, TOPK], I32),
                "weight": sf("fx_weight", [P, NT, TOPK], F32),
                "slots": sf("fx_slots", [1, TILES], I32),
                "arrivals": sf("fx_arrivals", [1, TILES], I32),
                "ends": sf("fx_ends", [1, E], I32),
                "pairs": sf("fx_pairs", [1, 1], I32),
            }
            with nc.sbuf_tensor("fx_rows", [P, NT, 2, D], F16) as rows:
                layer_norm(nc, "fx_ln", x_sb, xn, ident, True, rows=rows)
                route_and_share(nc, split, sems, x_sb, xn, rows, route, a["wg"], a["we"], slot_rows, cleared)
            routed_experts(nc, ident, route, we_pairs, slot_rows, slot_outs)
            combine_and_share(nc, split, sems, x_sb, xn, route, a["we"], slot_outs, a["out"])


def laid_out(inputs):
    import numpy as np

    get = lambda k: np.asarray(inputs[k])
    heads = lambda m: m.reshape(XHD, H, *m.shape[1:]).swapaxes(0, 1).reshape(CH, *m.shape[1:])
    pad = lambda m, axis: np.concatenate(
        [m, np.zeros([IP - I if n == axis else s for n, s in enumerate(m.shape)], m.dtype)], axis)
    wx = np.stack([heads(get(f"L0_xattn_W{s}")).T for s in "qkv"])
    bx = np.concatenate([heads(get(f"L0_xattn_b{s}")).reshape(CC, P) for s in "qk"]).T
    wm = np.zeros((4, P, CH), np.float32)
    wm.reshape(4, 4, 2, XHD, CH)[:, :, 0] = heads(get("L0_xattn_Wm").T).reshape(4, 4, XHD, CH)
    both = lambda routed, shared: np.concatenate([routed, shared.reshape(SH, I, D)])
    up = np.stack([both(get(f"L0_ffn_W{n}"), get(f"L0_ffn_Ws{n}")) for n in (1, 3)], 1)
    up = up.reshape(EA, 2, I, DC, P).transpose(0, 4, 3, 1, 2).reshape(EA, P, EW)
    w2s = get("L0_ffn_Ws2").T.reshape(SH, I, D)
    down = pad(np.concatenate([get("L0_ffn_W2").swapaxes(1, 2), w2s]), 1)
    down = down.reshape(EA, IC, P, D).transpose(0, 2, 1, 3).reshape(EA, P, IC * D)
    out = {
        "x": get("x").reshape(NT, P, D),
        "ctx": get("ctx_2048").reshape(NT, P, D),
        "wqkv": get("L0_attn_w_qkv").T,
        "wout": get("L0_attn_w_out").T,
        "enc": get("L0_xattn_encoding").reshape(2, G, XHD).swapaxes(1, 2),
        "wx": wx,
        "bx": bx,
        "bv": np.repeat(heads(get("L0_xattn_bv"))[None], P, 0),
        "wm": wm,
        "bm": get("L0_xattn_bm").reshape(CC, P).T,
        "wg": get("L0_ffn_Wg").T,
        "we": np.concatenate([up, down], 2),
    }
    return {k: np.ascontiguousarray(v) for k, v in out.items()}


def kernel(**inputs):
    import concourse.bacc as bacc
    from concourse.bass_utils import run_bass_kernel_spmd

    nc = bacc.Bacc("TRN2", target_bir_lowering=False, num_devices=1)
    arrays = {f"in_{k}": v for k, v in laid_out(inputs).items()}
    args = {k[3:]: nc.dram_tensor(k, v.shape, mybir.dt.from_np(v.dtype), kind="ExternalInput").ap()
            for k, v in arrays.items()}
    args["out"] = nc.dram_tensor("out", (NT, P, D), F32, kind="ExternalOutput").ap()
    decoder_block(nc, args)
    r = run_bass_kernel_spmd(nc, [arrays], core_ids=[0])
    return r.results[0]["out"].reshape(B, S, D)
```

```python
import numpy as np

import concourse.bass as bass
from concourse import mybir
from contextlib import ExitStack

P = 128
B, S, D = 8, 256, 512
T = B * S
NT = T // P
H = 16
G = 512
DC = D // P
HD = D // H
CH = S
CC = CH // P
XHD = CH // H
E, GR, EG = 16, 4, 4
TOPK, TOPK_G = 4, 2
SH = 2
EA = E + SH
I = 352
IC = (I + P - 1) // P
IP = IC * P
I_ROWS = [min(P, I - c * P) for c in range(IC)]
EW = 2 * DC * I
WC = EW + IC * D
PIECES = [(c * 2 * I, 2 * I) for c in range(DC)] + [(EW + n * IC * D // 2, IC * D // 2) for n in range(2)]
NP = len(PIECES)
MAX_TILES = T * TOPK // P + E
TILES = 2 * ((MAX_TILES + 1) // 2) + 4
OWNER = 16
CLEARS = 3
CT = -(-TILES // (CLEARS * T // G))
SPARE = TILES - T * TOPK // P
assert CT * CLEARS * T // G == TILES and SPARE % (T // G) == 0
EPS = 1e-5
MASKED = -1e30
M_CLAMP = 60000.0
PRODUCTS = ((0, 0), (0, 1), (1, 0))
QB, PB, PR = 96, 96, 97

F32 = mybir.dt.float32
F16 = mybir.dt.float16
BF16 = mybir.dt.bfloat16
I32 = mybir.dt.int32
ALU = mybir.AluOpType
ACT = mybir.ActivationFunctionType
AX = mybir.AxisListType


class Chain:

    def __init__(self, engine, sem, per_round=0, turn=0):
        self.engine, self.sem, self.n = engine, sem, 0
        self.base = per_round * turn

    def __call__(self, instruction):
        instruction.then_inc(self.sem, 1)
        self.n += 1
        return self.base + self.n

    def then_wait(self, instruction):
        self.engine.wait_ge(self.sem, self(instruction))


def split_product(nc, out, lhs, rhs, chunks):
    last = None
    for c in range(chunks):
        for n, (a, b) in enumerate(PRODUCTS):
            last = nc.tensor.matmul(out, lhs(a, c), rhs(b, c), start=(c == 0 and n == 0),
                                    stop=(c == chunks - 1 and n == len(PRODUCTS) - 1))
    return last


def layer_norm(nc, name, x_sb, xn, ident, rows=None, source=None, before=lambda block: None, after=lambda block: None):
    with ExitStack() as ctx:
        sb = lambda n, s, d: ctx.enter_context(nc.sbuf_tensor(f"{name}_{n}", s, d))
        sem = lambda n: ctx.enter_context(nc.semaphore(f"{name}_{n}"))
        stats = sb("stats", [P, NT, 6], F32)
        moments = sb("moments", [P, NT, 2], F32)
        std = sb("std", [P, NT], F32)
        rstd = sb("rstd", [P, NT], F32)
        norm = sb("norm", [P, 4, D], F32)
        pair = sb("pair", [P, 4, 2, D], F16)
        turned = ctx.enter_context(nc.psum_tensor(f"{name}_turned", [P, 4, 2, DC, P], F16))
        loaded = [sem(f"loaded{q}") for q in range(4)]
        dve_chain, moments_ready, std_ready = sem("dve_chain"), sem("moments_ready"), sem("std_ready")
        norm_ready, high_ready, low_ready = sem("norm_ready"), sem("high_ready"), sem("low_ready")
        turn_ready, stored, row_kept = sem("turn_ready"), sem("stored"), sem("row_kept")
        block = ctx.enter_context(nc.Block())

        @block.sync
        def _(sp):
            if source is not None:
                for q in range(4):
                    sp.dma_start(x_sb[:, 4 * q:4 * q + 4, :],
                                 source[4 * q:4 * q + 4].rearrange("t p d -> p t d")).then_inc(loaded[q], 16)

        before(block)

        @block.vector
        def _(dve):
            link = Chain(dve, dve_chain)
            for t in range(NT):
                if source is not None and t % 4 == 0:
                    dve.wait_ge(loaded[t // 4], 16)
                link(nc.vector.bn_stats(stats[:, t, :], x_sb[:, t, :]))
            dve.wait_ge(dve_chain, NT)
            for t in range(NT):
                link(nc.vector.bn_aggr(moments[:, t, :], stats[:, t, :]))
            dve.wait_ge(dve_chain, 2 * NT)
            nc.vector.tensor_scalar(std[:, :], moments[:, :, 1], EPS, None, ALU.add).then_inc(moments_ready, 1)
            dve.wait_ge(std_ready, 1)
            link.then_wait(nc.vector.reciprocal(rstd[:, :], std[:, :]))

            def normalise(t):
                if t >= 4:
                    dve.wait_ge(low_ready, t - 3)
                nc.vector.tensor_scalar(norm[:, t % 4, :], x_sb[:, t, :], moments[:, t, 0:1], rstd[:, t:t + 1],
                                        ALU.subtract, ALU.mult).then_inc(norm_ready, 1)

            def keep_rows(t):
                dve.wait_ge(low_ready, t + 1)
                nc.vector.tensor_copy(rows[:, t, :, :], pair[:, t % 4, :, :]).then_inc(row_kept, 1)

            normalise(0)
            normalise(1)
            for t in range(NT):
                if t + 2 < NT:
                    normalise(t + 2)
                dve.wait_ge(high_ready, t + 1)
                nc.vector.tensor_tensor(pair[:, t % 4, 1, :], norm[:, t % 4, :], pair[:, t % 4, 0, :],
                                        ALU.subtract).then_inc(low_ready, 1)
                if rows is not None and t:
                    keep_rows(t - 1)
            if rows is not None:
                keep_rows(NT - 1)

        @block.scalar
        def _(act):
            act.wait_ge(moments_ready, 1)
            nc.scalar.activation(std[:, :], std[:, :], ACT.Sqrt).then_inc(std_ready, 1)

            def keep(t):
                act.wait_ge(turn_ready, t + 1)
                nc.scalar.activation(
                    xn[:, :, :, t * P:(t + 1) * P].rearrange("p h c n -> p (h c) n"),
                    turned[:, t % 4, :, :, :].rearrange("p h c n -> p (h c) n"), ACT.Copy).then_inc(stored, 1)

            for t in range(NT):
                act.wait_ge(norm_ready, t + 1)
                if t >= 4:
                    act.wait_ge(turn_ready, t - 3)
                    if rows is not None:
                        act.wait_ge(row_kept, t - 3)
                nc.scalar.activation(pair[:, t % 4, 0, :], norm[:, t % 4, :], ACT.Copy).then_inc(high_ready, 1)
                if t >= 2:
                    keep(t - 2)
            keep(NT - 2)
            keep(NT - 1)

        @block.tensor
        def _(pe):
            for t in range(NT):
                pe.wait_ge(low_ready, t + 1)
                if t >= 4:
                    pe.wait_ge(stored, t - 3)
                for h in range(2):
                    for c in range(DC):
                        last = nc.tensor.transpose(turned[:, t % 4, h, c, :],
                                                   pair[:, t % 4, h, c * P:(c + 1) * P], ident[:, :])
                last.then_inc(turn_ready, 1)

        after(block)


class WeightSplit:

    def __init__(self, nc, ctx):
        self.nc = nc
        self.loaded = [ctx.enter_context(nc.semaphore(f"split_loaded{n}")) for n in range(DC + 1)]
        self.high_ready = ctx.enter_context(nc.semaphore("split_high_ready"))
        self.low_ready = ctx.enter_context(nc.semaphore("split_low_ready"))
        self.loads, self.done = [0] * (DC + 1), 0

    def __call__(self, jobs, block=None):
        if block is None:
            with self.nc.Block() as block:
                return self(jobs, block)
        for n in range(len(jobs)):
            self.loads[n] += 16
        self.programs(block, jobs, list(self.loads), self.done)
        self.done += len(jobs)

    def programs(self, block, jobs, arrived, done):
        nc, loaded, high_ready, low_ready = self.nc, self.loaded, self.high_ready, self.low_ready

        @block.sync
        def _(sp):
            for n, (dram, raw, _pair) in enumerate(jobs):
                sp.dma_start(raw, dram).then_inc(loaded[n], 16)

        @block.scalar
        def _(act):
            for n, (_dram, raw, pair) in enumerate(jobs):
                act.wait_ge(loaded[n], arrived[n])
                nc.scalar.activation(pair[0], raw, ACT.Copy).then_inc(high_ready, 1)

        @block.gpsimd
        def _(pool):
            for n, (_dram, raw, pair) in enumerate(jobs):
                pool.wait_ge(high_ready, done + n + 1)
                nc.gpsimd.tensor_tensor(pair[1], raw, pair[0], ALU.subtract).then_inc(low_ready, 1)


def self_attention(nc, split, x_sb, ident, x_dram, wqkv_dram, wout_dram, slot_rows, slot_outs, cleared):
    SCALE = float(HD) ** -0.5
    with ExitStack() as ctx:
        sb = lambda n, s, d: ctx.enter_context(nc.sbuf_tensor(f"sa_{n}", s, d))
        pb = lambda n, s, d: ctx.enter_context(nc.psum_tensor(f"sa_{n}", s, d))
        sem = lambda n: ctx.enter_context(nc.semaphore(f"sa_{n}"))
        w = sb("w", [P, 2, DC, 3 * D], F16)
        wo = sb("wo", [P, 2, DC, D], F16)
        xn = sb("xn", [P, 2, DC, T], F16)
        zeros = sb("zeros", [P, 2 * D], F16)
        identb = sb("identb", [P, P], BF16)
        mask4 = sb("mask4", [P, 4, P], BF16)
        mask2 = sb("mask2", [P, 2, 2, P], BF16)
        maskt = sb("maskt", [P, 3, P], BF16)
        with ExitStack() as raws:
            raw = raws.enter_context(nc.sbuf_tensor("sa_raw", [P, DC, 3 * D], F32))
            rawo = raws.enter_context(nc.sbuf_tensor("sa_rawo", [P, DC, D], F32))
            jobs = [(wqkv_dram.rearrange("(c p) e -> p c e", p=P)[:, c], raw[:, c, :],
                     (w[:, 0, c, :], w[:, 1, c, :])) for c in range(DC)]
            jobs.append((wout_dram.rearrange("(c p) e -> p c e", p=P), rawo[:, :, :],
                         (wo[:, 0], wo[:, 1])))
            layer_norm(nc, "sa_ln", x_sb, xn, ident, source=x_dram, before=lambda block: split(jobs, block))

        qk = sb("qk", [P, 2, 2 * DC, G], F16)
        qs = sb("qs", [P, H, G], F16)
        ks = sb("ks", [P, H, G], F16)
        v = sb("v", [P, 4, D], F32)
        ones = sb("ones", [P, HD], F32)
        mx = sb("mx", [P, 4, H], F32)
        nm = sb("nm", [P, 4, H], F16)
        nmf = sb("nmf", [P, 4, H], F32)
        mt = sb("mt", [H, G], F16)
        pt = sb("pt", [P, 4, 2, G], F32)
        rden = sb("rden", [P, G], F32)
        yf = sb("yf", [P, 2, G], F32)
        yt = sb("yt", [P, 2, DC, G], F16)
        scratch = nc.dram_tensor("sa_scratch", (2, 2 * D, G), F16).ap()
        proj = pb("proj", [P, 2, G], F32)
        sc = pb("sc", [P, 4, G], F32)
        pv = pb("pv", [P, G], F32)
        den = pb("den", [P, G], F32)
        made, made_f = sem("made"), sem("made_f")
        proj_done, proj_free, high_ready = sem("proj_done"), sem("proj_free"), sem("high_ready")
        spilled, stacked, maxed, score_done = sem("spilled"), sem("stacked"), sem("maxed"), sem("score_done")
        neg_ready, mt_done, mt_ready, row_loaded = sem("neg_ready"), sem("mt_done"), sem("mt_ready"), sem("row_loaded")
        st_done, exp_done, pv_done, norm_done = sem("st_done"), sem("exp_done"), sem("pv_done"), sem("norm_done")
        y_high, y_low, dve_chain = sem("y_high"), sem("y_low"), sem("dve_chain")
        UNITS, SCORES, PAIRS = 16, 24, 16

        def weighed(hq):
            return (proj[:, 0, :], proj[:, 1, :]) if hq % 2 else (pv[:, :], den[:, :])

        DVE_LINKS = 5

        with nc.Block() as block:
            @block.gpsimd
            def _(pool):
                nc.gpsimd.memset(mask4[:, :, :], 0.0).then_inc(made, 1)
                nc.gpsimd.memset(mask2[:, :, :, :], 0.0).then_inc(made, 1)
                nc.gpsimd.memset(maskt[:, :, :], 0.0).then_inc(made, 1)
                nc.gpsimd.memset(identb[:, :], 0.0).then_inc(made, 1)
                nc.gpsimd.memset(ones[:, :], 1.0).then_inc(made_f, 1)
                nc.gpsimd.memset(zeros[:, :], 0.0).then_inc(made_f, 1)
                pool.wait_ge(made, 4)
                nc.gpsimd.affine_select(out=mask4[:, :, :], in_=mask4[:, :, :], compare_op=ALU.is_ge, fill=MASKED,
                                        base=0, pattern=[[0, 4], [-1, P]], channel_multiplier=1).then_inc(made_f, 1)
                nc.gpsimd.affine_select(out=mask2[:, :, 1, :], in_=mask2[:, :, 1, :], compare_op=ALU.is_ge, fill=MASKED,
                                        base=0, pattern=[[0, 2], [-1, P]], channel_multiplier=1).then_inc(made_f, 1)
                nc.gpsimd.affine_select(out=maskt[:, 0:3:2, :], in_=maskt[:, 0:3:2, :], compare_op=ALU.is_ge, fill=MASKED,
                                        base=0, pattern=[[0, 2], [1, P]], channel_multiplier=-1).then_inc(made_f, 1)
                nc.gpsimd.affine_select(out=identb[:, :], in_=identb[:, :], compare_op=ALU.not_equal, fill=1.0,
                                        base=0, pattern=[[-1, P]], channel_multiplier=1).then_inc(made_f, 1)

            @block.vector
            def _(dve):
                nc.vector.memset(ks[PB:PR, :, :], 1.0).then_inc(made_f, 1)

        block = ctx.enter_context(nc.Block())

        @block.tensor
        def _(pe):
            with pe.Fori(0, T // G) as g:
                def unit(u, lhs, rhs):
                    pe.wait_ge(proj_free, UNITS * g + u + 1)
                    split_product(nc, proj[:, u % 2, :], lhs, rhs, DC).then_inc(proj_done, 1)

                for u in range(2 * DC):
                    unit(u, lambda a, c: w[:, a, c, u * P:(u + 1) * P], lambda b, c: xn[:, b, c, bass.ds(g * G, G)])
                for t in range(4):
                    unit(2 * DC + t, lambda a, c: xn[:, a, c, bass.ds(g * G + t * P, P)],
                         lambda b, c: w[:, b, c, 2 * D:3 * D])
                pe.wait_ge(stacked, 96 * g + 96)
                n = 0
                for bb in range(2):
                    for hq in range(4):
                        for part in range(3):
                            if n >= 4:
                                pe.wait_ge(maxed, SCORES * g + n - 3)
                            bank = sc[:, n % 4, :]
                            q0 = bb * S + (P if part else 0)
                            keys, heads = (S, 2) if part else (P, 4)
                            mask = mask2[:, :, :, :].rearrange("p a b c -> p (a b c)") if part \
                                else mask4[:, :, :].rearrange("p a c -> p (a c)")
                            nc.tensor.matmul(bank, identb[:, :], mask, start=True, stop=False, skip_group_check=True)
                            for k in range(heads):
                                h = 4 * hq + (2 * (part - 1) if part else 0) + k
                                last = nc.tensor.matmul(bank[:, k * keys:(k + 1) * keys],
                                                        qs[0:QB, h, q0:q0 + P],
                                                        ks[0:QB, h, bb * S:bb * S + keys],
                                                        start=False, stop=(k == heads - 1), skip_group_check=True)
                            last.then_inc(score_done, 1)
                            n += 1
                pe.wait_ge(neg_ready, g + 1)
                pe.wait_ge(norm_done, 4 * g + 1)
                mtp = pv[0:H, 0:G // 2].bitcast(F16)
                for t in range(4):
                    last = nc.tensor.transpose(mtp[:, t * P:(t + 1) * P], nm[:, t, :], ident[:, :])
                last.then_inc(mt_done, 1)

                def transposed_scores(p):
                    hq, bb, jj = p // 4, p // 2 % 2, p % 2
                    if p >= 2:
                        pe.wait_ge(exp_done, PAIRS * g + p - 1)
                    for i in range(2):
                        h, bank = 4 * hq + 2 * jj + i, sc[:, 2 * (p % 2) + i, :]
                        k0 = bb * S
                        nc.tensor.matmul(bank[:, 0:3 * P], identb[:, :], maskt[:, :, :].rearrange("p a c -> p (a c)"),
                                         start=True, stop=False, skip_group_check=True)
                        nc.tensor.matmul(bank[:, 0:S], ks[0:PR, h, k0:k0 + P], qs[0:PR, h, k0:k0 + S],
                                         start=False, stop=False, skip_group_check=True)
                        last = nc.tensor.matmul(bank[:, S:S + P], ks[0:PR, h, k0 + P:k0 + S],
                                                qs[0:PR, h, k0 + P:k0 + S], start=False, stop=True,
                                                skip_group_check=True)
                    last.then_inc(st_done, 1)

                def values(qd):
                    hq, bb = qd // 2, qd % 2
                    pe.wait_ge(exp_done, PAIRS * g + 2 * qd + 2)
                    if bb == 0 and hq == 1:
                        pe.wait_ge(proj_free, UNITS * g + 14)
                    elif bb == 0 and hq:
                        pe.wait_ge(norm_done, 4 * g + hq)
                    for out, values_of in zip(weighed(hq), (True, False)):
                        for kt in range(2):
                            for j in range(4):
                                pr = pt[:, (2 * qd + j // 2) % 4, j % 2, :]
                                lhs = v[:, 2 * bb + kt, (4 * hq + j) * HD:(4 * hq + j + 1) * HD] if values_of \
                                    else ones[:, :]
                                cols = slice(bb * S, bb * S + S) if kt == 0 else slice(bb * S + P, bb * S + S)
                                last = nc.tensor.matmul(out[j * HD:(j + 1) * HD, cols], lhs,
                                                        pr[:, 0:S] if kt == 0 else pr[:, S:S + P],
                                                        start=(kt == 0), stop=(kt == 1), skip_group_check=True,
                                                        tile_position=(0, j * HD))
                    last.then_inc(pv_done, 1)

                pe.wait_ge(row_loaded, 16 * g + 16)
                for p in range(2):
                    transposed_scores(p)
                for qd in range(8):
                    for p in (2 * qd + 2, 2 * qd + 3):
                        if p < PAIRS:
                            transposed_scores(p)
                    values(qd)
                pe.wait_ge(y_low, 4 * g + 4)
                for t in range(4):
                    unit(12 + t, lambda a, c: yt[:, a, c, t * P:(t + 1) * P], lambda b, c: wo[:, b, c, :])

        @block.vector
        def _(dve):
            dve.sem_inc(proj_free, 2)
            dve.sem_inc(norm_done, 1)
            with dve.Fori(0, T // G) as g:
                link = Chain(dve, dve_chain, DVE_LINKS, g)
                for u in range(2 * DC):
                    dve.wait_ge(high_ready, 2 * DC * g + u + 1)
                    nc.vector.tensor_tensor(qk[:, 1, u, :], proj[:, u % 2, :], qk[:, 0, u, :],
                                            ALU.subtract).then_inc(proj_free, 1)
                for t in range(4):
                    dve.wait_ge(proj_done, UNITS * g + 2 * DC + t + 1)
                    nc.vector.tensor_copy(v[:, t, :], proj[:, t % 2, :]).then_inc(proj_free, 1)
                n = 0
                for bb in range(2):
                    for hq in range(4):
                        for part in range(3):
                            dve.wait_ge(score_done, SCORES * g + n + 1)
                            if part == 0:
                                out, heads = mx[:, 2 * bb, 4 * hq:4 * hq + 4], 4
                            else:
                                h0 = 4 * hq + 2 * (part - 1)
                                out, heads = mx[:, 2 * bb + 1, h0:h0 + 2], 2
                            nc.vector.reduce_max(out, sc[:, n % 4, :].rearrange("p (h k) -> p h k", h=heads),
                                                 AX.X).then_inc(maxed, 1)
                            n += 1
                dve.wait_ge(maxed, SCORES * g + SCORES)
                link.then_wait(nc.vector.tensor_scalar(nmf[:, :, :], mx[:, :, :], -1.0, M_CLAMP, ALU.mult, ALU.min))
                nc.vector.tensor_scalar(nm[:, :, :], nmf[:, :, :], -M_CLAMP, None, ALU.max).then_inc(neg_ready, 1)
                for hq in range(4):
                    dve.wait_ge(pv_done, 8 * g + 2 * hq + 2)
                    if hq >= 1:
                        dve.wait_ge(norm_done, 4 * g + hq + 1)
                    values, sums = weighed(hq)
                    link.then_wait(nc.vector.reciprocal(rden[:, :], sums))
                    if hq >= 2:
                        dve.wait_ge(y_low, 4 * g + hq - 1)
                    nc.vector.tensor_tensor(yf[:, hq % 2, :], values, rden[:, :], ALU.mult).then_inc(norm_done, 1)
                for t in range(4):
                    dve.wait_ge(proj_done, UNITS * g + 12 + t + 1)
                    nc.vector.tensor_tensor(x_sb[:, 4 * g + t, :], proj[:, t % 2, :], x_sb[:, 4 * g + t, :],
                                            ALU.add).then_inc(proj_free, 1)
                assert link.n == DVE_LINKS

        @block.scalar
        def _(act):
            with act.Fori(0, T // G) as g:
                for u in range(2 * DC):
                    act.wait_ge(proj_done, UNITS * g + u + 1)
                    nc.scalar.activation(qk[:, 0, u, :], proj[:, u % 2, :], ACT.Copy).then_inc(high_ready, 1)
                act.wait_ge(mt_done, g + 1)
                nc.scalar.activation(mt[:, :], pv[0:H, 0:G // 2].bitcast(F16), ACT.Copy).then_inc(mt_ready, 1)

                def high(hq):
                    act.wait_ge(norm_done, 4 * g + hq + 2)
                    nc.scalar.activation(yt[:, 0, hq, :], yf[:, hq % 2, :], ACT.Copy).then_inc(y_high, 1)

                for p in range(PAIRS):
                    act.wait_ge(st_done, PAIRS * g + p + 1)
                    if p >= 4:
                        act.wait_ge(pv_done, 8 * g + p // 2 - 1)
                    nc.scalar.activation(pt[:, p % 4, :, 0:3 * P], sc[:, 2 * (p % 2):2 * (p % 2) + 2, 0:3 * P],
                                         ACT.Exp, scale=SCALE).then_inc(exp_done, 1)
                    if p % 4 == 3 and p > 3:
                        high(p // 4 - 1)
                high(3)

        @block.gpsimd
        def _(pool):
            with pool.Fori(0, T // G) as g:
                for hq in range(4):
                    pool.wait_ge(y_high, 4 * g + hq + 1)
                    nc.gpsimd.tensor_tensor(yt[:, 1, hq, :], yf[:, hq % 2, :], yt[:, 0, hq, :],
                                            ALU.subtract).then_inc(y_low, 1)
            pool.wait_ge(cleared, 16 * (CLEARS + 1) * T // G)

        @block.sync
        def _(sp):
            with sp.Fori(0, T // G) as g:
                for side in range(2):
                    sp.wait_ge(proj_free, UNITS * g + 2 + DC * (side + 1))
                    for part in range(2):
                        sp.dma_start(scratch[part, side * D:(side + 1) * D].rearrange("(c p) n -> p c n", p=P),
                                     qk[:, part, side * DC:(side + 1) * DC, :]).then_inc(spilled, 16)
                    sp.wait_ge(spilled, 64 * g + 32 * side + 32)
                    tile, parts = (ks, (0, 1, 0)) if side else (qs, (0, 0, 1))
                    for r, part in enumerate(parts):
                        sp.dma_start(tile[r * HD:(r + 1) * HD, :, :],
                                     scratch[part, side * D:(side + 1) * D].rearrange("(h d) n -> d h n", d=HD)
                                     ).then_inc(stacked, 16)
                zero = lambda rows, z: sp.dma_start(
                    rows.rearrange("(a p) n -> p a n", p=P),
                    z.rearrange("p (o n) -> p o n", o=1).to_broadcast([P, rows.shape[0] // P, z.shape[1]])
                ).then_inc(cleared, 16)
                for k in range(CLEARS):
                    zero(slot_rows[bass.ds((g * CLEARS + k) * CT * P, CT * P)], zeros[:, :])
                share = SPARE // (T // G)
                zero(slot_outs[bass.ds(T * TOPK + g * share * P, share * P)], zeros[:, :].bitcast(F32))
                sp.wait_ge(mt_ready, g + 1)
                sp.dma_start(qs[PB:PR, :, :], mt[:, :]).then_inc(row_loaded, 16)


def row_moments(nc, name, x_sb, mean, rstd, beside):
    with ExitStack() as ctx:
        sb = lambda n, s, d: ctx.enter_context(nc.sbuf_tensor(f"{name}_{n}", s, d))
        sem = lambda n: ctx.enter_context(nc.semaphore(f"{name}_{n}"))
        stats = sb("stats", [P, NT, 6], F32)
        moments = sb("moments", [P, NT, 2], F32)
        std = sb("std", [P, NT], F32)
        dve_chain, moments_ready, std_ready = sem("dve_chain"), sem("moments_ready"), sem("std_ready")
        block = ctx.enter_context(nc.Block())
        beside(block)

        @block.vector
        def _(dve):
            link = Chain(dve, dve_chain)
            for t in range(NT):
                link(nc.vector.bn_stats(stats[:, t, :], x_sb[:, t, :]))
            dve.wait_ge(dve_chain, NT)
            for t in range(NT):
                link(nc.vector.bn_aggr(moments[:, t, :], stats[:, t, :]))
            dve.wait_ge(dve_chain, 2 * NT)
            nc.vector.tensor_scalar(std[:, :], moments[:, :, 1], EPS, None, ALU.add).then_inc(moments_ready, 1)
            link(nc.vector.tensor_copy(mean[:, :], moments[:, :, 0]))
            dve.wait_ge(std_ready, 1)
            nc.vector.reciprocal(rstd[:, :], std[:, :])

        @block.scalar
        def _(act):
            act.wait_ge(moments_ready, 1)
            nc.scalar.activation(std[:, :], std[:, :], ACT.Sqrt).then_inc(std_ready, 1)


def cross_attention(nc, split, x_sb, ctx_dram, enc_dram, w_dram, b_dram, bv_dram, wm_dram, bm_dram, we_dram, we_pairs):
    SCALE = float(XHD) ** -0.5
    BANKS, QUADS = 4 * H, 16
    SR, TR, VR = 2, 3, 1
    MADE, OUT, SWAP, ADD, HIGH, LOW = ({2 * u + k: u for u in range(4)} for k in range(1, 7))
    X_NORM, X_HIGH, X_LOW = 11, 12, 13
    FIRST_PIECE = 4
    WP = 2 * NP
    with ExitStack() as ctx:
        sb = lambda n, s, d: ctx.enter_context(nc.sbuf_tensor(f"ca_{n}", s, d))
        pb = lambda n, s, d: ctx.enter_context(nc.psum_tensor(f"ca_{n}", s, d))
        sem = lambda n: ctx.enter_context(nc.semaphore(f"ca_{n}"))
        w = sb("w", [P, 2, 3, CC, CH], F16)
        wm = sb("wm", [P, 2, 4, CH], F16)
        mean = sb("mean", [P, NT], F32)
        rstd = sb("rstd", [P, NT], F32)
        with ExitStack() as raws:
            raw = raws.enter_context(nc.sbuf_tensor("ca_raw", [P, 3, CC, CH], F32))
            rawm = raws.enter_context(nc.sbuf_tensor("ca_rawm", [P, 4, CH], F32))
            jobs = [(w_dram.rearrange("s (c p) e -> p s c e", p=P), raw[:, :, :, :], (w[:, 0], w[:, 1])),
                    (wm_dram.rearrange("q p e -> p q e"), rawm[:, :, :], (wm[:, 0], wm[:, 1]))]
            row_moments(nc, "ca_ln", x_sb, mean, rstd, beside=lambda block: split(jobs, block))

        norm = sb("norm", [P, CC, G], F32)
        xn = sb("xn", [P, 2, CC, G], F16)
        rawc = sb("rawc", [P, CC, G], F32)
        cx = sb("cx", [P, 2, 2, CC, G], F16)
        wraw = sb("wraw", [P, 3, IC * D // 2], F32)
        wpair = sb("wpair", [P, 2, 2, IC * D // 2], F16)
        freq = sb("freq", [P, 2, G], F32)
        sign = sb("sign", [P, 1], F32)
        signi = sb("signi", [P, 1], I32)
        bqk = sb("bqk", [P, 4], F32)
        bm = sb("bm", [P, CC], F32)
        bv = sb("bv", [P, H, XHD], F32)
        tf = sb("tf", [P, 4, G], F32)
        waited = sb("waited", [P, 4], F32)
        rf = sb("rf", [P, G], F32)
        qk = sb("qk", [P, 2, 4, G], F16)
        qs = sb("qs", [P, 2, H, G], F16)
        ks = sb("ks", [P, 2, H, G], F16)
        va = sb("va", [P, 4, H, 2 * XHD], F32)
        identh = sb("identh", [P, P], F16)
        mx = sb("mx", [P, 4, H], F32)
        nm = sb("nm", [P, 4, H], F16)
        nmf = sb("nmf", [P, 4, H], F32)
        mt = sb("mt", [H, G], F16)
        pt = sb("pt", [P, 8, G], F32)
        turned = sb("turned", [P, G // 32, 32], F32)
        rden = sb("rden", [P, G // 32], F32)
        quot = sb("quot", [P, G // 32, 32], F32)
        yf = sb("yf", [P, 2, G], F32)
        yt = sb("yt", [P, 2, 4, G], F16)
        scratch = nc.dram_tensor("ca_scratch", (2, 4, P, G), F16).ap()
        proj = pb("proj", [P, 2, G], F32)
        sc = pb("sc", [P, SR, G], F32)
        st = pb("st", [P, TR, G], F32)
        pv = pb("pv", [P, VR, G], F32)
        loads, made, signed = sem("loads"), sem("made"), sem("signed")
        proj_done, qk_out, v_done, v_out = sem("proj_done"), sem("qk_out"), sem("v_done"), sem("v_out")
        out_done, res_done, swapped, cosed, rotated = (
            sem("out_done"), sem("res_done"), sem("swapped"), sem("cosed"), sem("rotated"))
        high_ready, low_ready = sem("high_ready"), sem("low_ready")
        norm_ready, x_high, x_low = sem("norm_ready"), sem("x_high"), sem("x_low")
        spilled, stacked, maxed, score_done = sem("spilled"), sem("stacked"), sem("maxed"), sem("score_done")
        neg_ready, mt_done, mt_ready, row_loaded = sem("neg_ready"), sem("mt_done"), sem("mt_ready"), sem("row_loaded")
        st_done, exp_done, pv_done, norm_done = sem("st_done"), sem("exp_done"), sem("pv_done"), sem("norm_done")
        turned_out = sem("turned_out")
        y_high, y_low, dve_chain, pre_chain = sem("y_high"), sem("y_low"), sem("dve_chain"), sem("pre_chain")
        c_loaded, c_high, c_low = sem("c_loaded"), sem("c_high"), sem("c_low")
        w_loaded, w_stored = [sem(f"w_loaded{k}") for k in range(3)], [sem(f"w_stored{k}") for k in range(2)]
        w_high, w_low = sem("w_high"), sem("w_low")
        PRE_LINKS, DVE_LINKS = 1, 8

        with nc.Block() as block:
            @block.sync
            def _(sp):
                for f in range(2):
                    for j in range(8):
                        sp.dma_start(freq[j * XHD:(j + 1) * XHD, f, :], enc_dram[f]).then_inc(loads, 16)
                sp.dma_start(bqk[:, :], b_dram).then_inc(loads, 16)
                sp.dma_start(bm[:, :], bm_dram).then_inc(loads, 16)
                sp.dma_start(bv[:, :, :].rearrange("p h d -> p (h d)"), bv_dram).then_inc(loads, 16)
                sp.wait_ge(loads, 16 * 19)

            @block.gpsimd
            def _(pool):
                nc.gpsimd.memset(identh[:, :], 0.0).then_inc(made, 1)
                nc.gpsimd.memset(va[:, :, :, :], 1.0).then_inc(signed, 1)
                nc.gpsimd.memset(quot[:, :, :], 0.0).then_inc(signed, 1)
                pool.wait_ge(made, 1)
                nc.gpsimd.affine_select(out=identh[:, :], in_=identh[:, :], compare_op=ALU.not_equal, fill=1.0,
                                        base=0, pattern=[[-1, P]], channel_multiplier=1).then_inc(signed, 1)
                nc.gpsimd.iota(signi[:, :], pattern=[[0, 1]], base=0, channel_multiplier=1).then_inc(made, 1)

            @block.vector
            def _(dve):
                one_pair = float(np.array([1, 1], np.float16).view(np.float32)[0])
                for tile, rows, value in ((qs, PB, 0.0), (ks, PR, one_pair)):
                    nc.vector.memset(tile[4 * XHD:rows, :, :, :].rearrange("p s h n -> p (s h n)").bitcast(F32), value
                                     ).then_inc(signed, 1)
                dve.wait_ge(made, 2)
                nc.vector.tensor_scalar(signi[:, :], signi[:, :], 1, None, ALU.bitwise_and).then_inc(made, 1)
                dve.wait_ge(made, 3)
                nc.vector.tensor_scalar(sign[:, :], signi[:, :], 2.0, -1.0, ALU.mult, ALU.add).then_inc(made, 1)
                dve.wait_ge(made, 4)
                dve.wait_ge(loads, 16 * 19)
                nc.vector.tensor_scalar(freq[:, 1, :], freq[:, 1, :], sign[:, 0:1], None, ALU.mult).then_inc(made, 1)

        block = ctx.enter_context(nc.Block())

        def all_turns(engine, turn):
            turn(-2, 0, False, False, True, True)
            turn(-1, 1, False, True, True, True)
            with engine.Fori(0, (B - 4) // 2) as i:
                for s in range(2):
                    with engine.Fori(s, s + 1) as j:
                        turn(2 * i + j, s, True, True, True, True)
            turn(B - 4, 0, True, True, True, True)
            turn(B - 3, 1, True, True, True, False)
            turn(B - 2, 0, True, True, False, False)
            turn(B - 1, 1, True, False, False, False)

        @block.tensor
        def _(pe):
            def turn(b, s, attend, maxima, projects, _pairs):
                c, e, sn = b + 1, b + 2, 1 - s

                def project(u):
                    side, oc = u // 2, u % 2
                    if u == 0:
                        pe.wait_ge(x_low, 2 * e + 2)
                    if u == 2:
                        pe.wait_ge(c_low, e + 1)
                    if u >= 2 or maxima:
                        pe.wait_ge(qk_out, 4 * e + u - 1)
                    if u < 2 and attend:
                        pe.wait_ge(res_done, 2 * b + u + 1)
                        pe.wait_ge(v_out, 4 * b + u + 3)
                    split_product(nc, proj[:, oc, :], lambda a, k: w[:, a, side, k, oc * P:(oc + 1) * P],
                                  (lambda p, k: xn[:, p, k, :]) if side == 0 else (lambda p, k: cx[:, s, p, k, :]),
                                  CC).then_inc(proj_done, 1)

                def values(kt):
                    if kt >= 2:
                        pe.wait_ge(v_out, 4 * c + kt - 1)
                    elif projects:
                        pe.wait_ge(qk_out, 4 * e + kt + 3)
                    else:
                        pe.wait_ge(res_done, 2 * b + kt + 1)
                    split_product(nc, proj[:, kt % 2, 0:CH], lambda a, k: cx[:, sn, a, k, kt * P:(kt + 1) * P],
                                  lambda p, k: w[:, p, 2, k, :], CC).then_inc(v_done, 1)

                def scores(n):
                    qt, h = n // H, n % H
                    if n == 0:
                        pe.wait_ge(stacked, 128 * c + 128)
                        if attend:
                            pe.wait_ge(mt_ready, c)
                    if n >= SR:
                        pe.wait_ge(maxed, BANKS * c + n - SR + 1)
                    nc.tensor.matmul(sc[:, n % SR, :], qs[0:QB, sn, h, qt * P:(qt + 1) * P], ks[0:QB, sn, h, :],
                                     start=True, stop=True).then_inc(score_done, 1)

                def turn_maxima():
                    pe.wait_ge(neg_ready, c + 1)
                    mtp = sc[0:H, 0, 0:G // 2].bitcast(F16)
                    for t in range(4):
                        last = nc.tensor.transpose(mtp[:, t * P:(t + 1) * P], nm[:, t, :], identh[:, :])
                    last.then_inc(mt_done, 1)

                def transposed_scores(p):
                    hq, kt, j = p // 16, p // 4 % 4, p % 4
                    if p == 0:
                        pe.wait_ge(row_loaded, 16 * b + 16)
                    if p >= TR:
                        pe.wait_ge(exp_done, BANKS * b + p - TR + 1)
                    nc.tensor.matmul(st[:, p % TR, :], ks[0:PR, s, 4 * hq + j, kt * P:(kt + 1) * P],
                                     qs[0:PR, s, 4 * hq + j, :], start=True, stop=True).then_inc(st_done, 1)

                def weigh_values(qd):
                    hq, kt = qd // 4, qd % 4
                    if qd == 0:
                        pe.wait_ge(v_out, 4 * b + 4)
                    pe.wait_ge(exp_done, BANKS * b + 4 * qd + 4)
                    if kt == 0:
                        pe.wait_ge(turned_out, 4 * b + hq + 1)
                    for j in range(4):
                        last = nc.tensor.matmul(pv[j * 32:(j + 1) * 32, hq % VR, :], va[:, kt, 4 * hq + j, :],
                                                pt[:, (4 * qd + j) % 8, :], start=(kt == 0),
                                                stop=(kt == 3), skip_group_check=True, tile_position=(0, j * 32))
                    last.then_inc(pv_done, 1)

                if attend:
                    for p in range(4):
                        transposed_scores(p)
                for qd in range(QUADS):
                    for k in range(4):
                        if attend and qd + 1 < QUADS:
                            transposed_scores(4 * qd + 4 + k)
                        if maxima:
                            scores(4 * qd + k)
                    if projects and qd in MADE:
                        project(MADE[qd])
                    if attend:
                        weigh_values(qd)
                if maxima:
                    values(0)
                    values(1)
                    turn_maxima()
                    values(2)
                    values(3)
                if attend:
                    pe.wait_ge(y_low, 4 * b + 4)
                    for oc in range(2):
                        pe.wait_ge(*((v_out, 4 * c + 3 + oc) if maxima else (res_done, 2 * b + oc + 1)))
                        split_product(nc, proj[:, oc, :], lambda a, k: wm[:, a, k, oc * P:(oc + 1) * P],
                                      lambda p, k: yt[:, p, k, :], 4).then_inc(out_done, 1)
            all_turns(pe, turn)

        @block.vector
        def _(dve):
            dve.sem_inc(turned_out, VR)
            dve.sem_inc(res_done, 2)

            def normalise(j, c):
                nc.vector.tensor_scalar(norm[:, j, :], x_sb[:, 2 * c + j, :], mean[:, bass.ds(2 * c + j, 1)],
                                        rstd[:, bass.ds(2 * c + j, 1)], ALU.subtract, ALU.mult).then_inc(norm_ready, 1)

            for j in range(CC):
                normalise(j, 0)

            def turn(b, s, attend, maxima, projects, pairs):
                c, e, f = b + 1, b + 2, b + 3
                link = Chain(dve, dve_chain, DVE_LINKS, b)

                def swap(u):
                    dve.wait_ge(qk_out, 4 * e + u + 1)
                    if u or maxima:
                        dve.wait_ge(rotated, 4 * e + u)
                    nc.vector.memset(waited[:, u:u + 1], 0.0)
                    nc.vector.stream_shuffle(rf[:, :], tf[:, u, :], [i ^ 1 for i in range(32)]).then_inc(swapped, 1)
                    dve.wait_ge(swapped, 8 * e + 2 * u + 1)
                    nc.vector.tensor_tensor(rf[:, :], rf[:, :], freq[:, 1, :], ALU.mult).then_inc(swapped, 1)

                def add(u):
                    dve.wait_ge(swapped, 8 * e + 2 * u + 2)
                    dve.wait_ge(cosed, 4 * e + u + 1)
                    nc.vector.tensor_tensor(tf[:, u, :], tf[:, u, :], rf[:, :], ALU.add).then_inc(rotated, 1)

                def maximum(n):
                    dve.wait_ge(score_done, BANKS * c + n + 1)
                    nc.vector.reduce_max(mx[:, n // H, n % H:n % H + 1], sc[:, n % SR, :], AX.X).then_inc(maxed, 1)

                def divide(hq):
                    dve.wait_ge(pv_done, 16 * b + 4 * hq + 4)
                    nc.vector.transpose(turned[:, :, :].rearrange("p a b -> p (a b)"), pv[:, hq % VR, :]
                                        ).then_inc(turned_out, 1)
                    dve.wait_ge(turned_out, 4 * b + hq + 1 + VR)
                    link.then_wait(nc.vector.reciprocal(rden[:, :], turned[:, :, XHD]))
                    link.then_wait(nc.vector.tensor_tensor(
                        quot[:, :, 0:XHD], turned[:, :, 0:XHD],
                        rden[:, :].rearrange("p (a o) -> p a o", o=1).to_broadcast([P, G // 32, XHD]), ALU.mult))
                    if hq >= 2:
                        dve.wait_ge(y_low, 4 * b + hq - 1)
                    nc.vector.transpose(yf[:, hq % 2, :], quot[:, :, :].rearrange("p a b -> p (a b)")
                                        ).then_inc(norm_done, 1)
                    dve.wait_ge(norm_done, 4 * b + hq + 1)

                for qd in range(QUADS):
                    if maxima:
                        maximum(4 * qd)
                        maximum(4 * qd + 1)
                    if projects and qd in ADD:
                        add(ADD[qd])
                    if maxima:
                        maximum(4 * qd + 2)
                        maximum(4 * qd + 3)
                    if projects and qd in SWAP:
                        swap(SWAP[qd])
                    if pairs and qd == X_NORM:
                        dve.wait_ge(x_low, 2 * f)
                        for j in range(CC):
                            normalise(j, f)
                    if maxima and qd == QUADS - 1:
                        dve.wait_ge(maxed, BANKS * c + BANKS)
                        nc.vector.tensor_scalar(nmf[:, :, :], mx[:, :, :], -1.0, M_CLAMP, ALU.mult, ALU.min
                                                ).then_inc(pre_chain, 1)
                        dve.wait_ge(pre_chain, c + 1)
                        nc.vector.tensor_scalar(nm[:, :, :], nmf[:, :, :], -M_CLAMP, None, ALU.max).then_inc(neg_ready, 1)
                    if attend and qd % 4 == 3:
                        divide(qd // 4)
                if maxima:
                    for kt in range(4):
                        dve.wait_ge(v_done, 4 * c + kt + 1)
                        nc.vector.tensor_tensor(va[:, kt, :, 0:XHD],
                                                proj[:, kt % 2, 0:CH].rearrange("p (h d) -> p h d", h=H), bv[:, :, :],
                                                ALU.add).then_inc(v_out, 1)
                if attend:
                    for oc in range(2):
                        dve.wait_ge(out_done, 2 * b + oc + 1)
                        nc.vector.scalar_tensor_tensor(x_sb[:, 2 * b + oc, :], proj[:, oc, :], bm[:, oc:oc + 1],
                                                       x_sb[:, 2 * b + oc, :], ALU.add, ALU.add).then_inc(res_done, 1)
                    assert link.n == DVE_LINKS
            all_turns(dve, turn)

        @block.scalar
        def _(act):
            def split_piece(b, m):
                n = PIECES[m % NP][1]
                act.wait_ge(w_loaded[m % 3], 16 * (WP // 3 * b + m // 3 + 1))
                act.wait_ge(w_stored[m % 2], 16 * (WP // 2 * b + m // 2 + 1))
                nc.scalar.activation(wpair[:, m % 2, 0, 0:n], wraw[:, m % 3, 0:n], ACT.Copy).then_inc(w_high, 1)

            def x_high_part(j, c):
                act.wait_ge(norm_ready, 2 * c + j + 1)
                nc.scalar.activation(xn[:, 0, j, :], norm[:, j, :], ACT.Copy).then_inc(x_high, 1)

            def c_high_part(f, parity, used):
                act.wait_ge(c_loaded, 16 * f + 16)
                if used:
                    act.wait_ge(v_done, 4 * (f - 1))
                nc.scalar.activation(cx[:, parity, 0, :, :], rawc[:, :, :], ACT.Copy).then_inc(c_high, 1)

            act.sem_inc(w_stored[0], 16)
            act.sem_inc(w_stored[1], 16)
            for j in range(CC):
                x_high_part(j, 0)
            c_high_part(0, 0, False)

            def turn(b, s, attend, maxima, projects, pairs):
                c, e, f = b + 1, b + 2, b + 3

                def out(u):
                    act.wait_ge(proj_done, 4 * e + u + 1)
                    if maxima:
                        act.wait_ge(low_ready, 4 * e + u - 3)
                    nc.scalar.activation(tf[:, u, :], proj[:, u % 2, :], ACT.Identity,
                                         bias=bqk[:, u:u + 1]).then_inc(qk_out, 1)

                def high_part(u):
                    act.wait_ge(rotated, 4 * e + u + 1)
                    if maxima and u == 0:
                        act.wait_ge(spilled, 64 * e)
                    nc.scalar.activation(qk[:, 0, u, :], tf[:, u, :], ACT.Copy).then_inc(high_ready, 1)

                def y_high_part(hq):
                    act.wait_ge(norm_done, 4 * b + hq + 1)
                    nc.scalar.activation(yt[:, 0, hq, :], yf[:, hq % 2, :], ACT.Copy).then_inc(y_high, 1)

                for qd in range(QUADS):
                    for p in range(4 * qd, 4 * qd + 4) if attend else ():
                        act.wait_ge(st_done, BANKS * b + p + 1)
                        if p >= 8:
                            act.wait_ge(pv_done, 16 * b + qd - 1)
                        nc.scalar.activation(pt[:, p % 8, :], st[:, p % TR, :], ACT.Exp, scale=SCALE).then_inc(exp_done, 1)
                    for step, at in ((out, OUT), (high_part, HIGH)):
                        if projects and qd in at:
                            step(at[qd])
                    if attend and qd % 4 == 1 and qd > 4:
                        y_high_part(qd // 4 - 1)
                    if pairs and qd == X_HIGH:
                        for j in range(CC):
                            x_high_part(j, f)
                    if attend and qd >= FIRST_PIECE:
                        split_piece(b, qd - FIRST_PIECE)
                if maxima:
                    act.wait_ge(mt_done, c + 1)
                    nc.scalar.activation(mt[:, :], sc[0:H, 0, 0:G // 2].bitcast(F16), ACT.Copy).then_inc(mt_ready, 1)
                if attend:
                    y_high_part(3)
                if pairs:
                    c_high_part(f, 1 - s, maxima)
            all_turns(act, turn)

        @block.gpsimd
        def _(pool):
            def c_low_part(f, parity):
                pool.wait_ge(c_high, f + 1)
                nc.gpsimd.tensor_tensor(cx[:, parity, 1, :, :], rawc[:, :, :], cx[:, parity, 0, :, :],
                                        ALU.subtract).then_inc(c_low, 1)

            def x_low_part(j, f):
                pool.wait_ge(x_high, 2 * f + j + 1)
                nc.gpsimd.tensor_tensor(xn[:, 1, j, :], norm[:, j, :], xn[:, 0, j, :], ALU.subtract).then_inc(x_low, 1)

            pool.sem_inc(w_low, 1)
            for j in range(CC):
                x_low_part(j, 0)
            c_low_part(0, 0)

            def turn(b, s, attend, maxima, projects, pairs):
                e, f = b + 2, b + 3

                def y_low_part(hq):
                    pool.wait_ge(y_high, 4 * b + hq + 1)
                    nc.gpsimd.tensor_tensor(yt[:, 1, hq, :], yf[:, hq % 2, :], yt[:, 0, hq, :],
                                            ALU.subtract).then_inc(y_low, 1)

                for qd in range(QUADS):
                    if attend and qd % 4 == 1 and qd > 4:
                        y_low_part(qd // 4 - 1)
                    if attend and qd >= FIRST_PIECE:
                        m = qd - FIRST_PIECE
                        n = PIECES[m % NP][1]
                        pool.wait_ge(w_high, WP * b + m + 1)
                        nc.gpsimd.tensor_tensor(wpair[:, m % 2, 1, 0:n], wraw[:, m % 3, 0:n],
                                                wpair[:, m % 2, 0, 0:n], ALU.subtract).then_inc(w_low, 1)
                    if projects and qd in SWAP:
                        u = SWAP[qd]
                        pool.wait_ge(swapped, 8 * e + 2 * u + 1)
                        nc.gpsimd.tensor_tensor(tf[:, u, :], tf[:, u, :], freq[:, 0, :], ALU.mult).then_inc(cosed, 1)
                    if projects and qd in LOW:
                        u = LOW[qd]
                        pool.wait_ge(high_ready, 4 * e + u + 1)
                        nc.gpsimd.tensor_tensor(qk[:, 1, u, :], tf[:, u, :], qk[:, 0, u, :],
                                                ALU.subtract).then_inc(low_ready, 1)
                    if pairs and qd == X_LOW:
                        for j in range(CC):
                            x_low_part(j, f)
                if attend:
                    y_low_part(3)
                if pairs:
                    c_low_part(f, 1 - s)
            all_turns(pool, turn)

        @block.sync
        def _(sp):
            def load_context(f):
                sp.dma_start(rawc[:, :, :], ctx_dram[bass.ds(CC * f, CC)].rearrange("t p d -> p t d")
                             ).then_inc(c_loaded, 16)

            def load_piece(b, m):
                at, n = PIECES[m % NP]
                sp.dma_start(wraw[:, m % 3, 0:n], we_dram[2 * b + m // NP, :, at:at + n]).then_inc(w_loaded[m % 3], 16)

            def store_piece(b, m):
                at, n = PIECES[m % NP]
                sp.dma_start(we_pairs[2 * b + m // NP, :, :, at:at + n], wpair[:, m % 2, :, 0:n]
                              ).then_inc(w_stored[m % 2], 16)

            load_context(0)
            load_piece(0, 0)
            load_piece(0, 1)

            def turn(b, s, attend, maxima, projects, pairs):
                c, e, f, sn = b + 1, b + 2, b + 3, 1 - s
                if pairs:
                    sp.wait_ge(c_low, f)
                    load_context(f)
                if projects and maxima:
                    sp.wait_ge(stacked, 128 * e)
                for qd in range(QUADS):
                    if attend and qd >= FIRST_PIECE:
                        m = qd - FIRST_PIECE
                        sp.wait_ge(w_low, WP * b + m + 1)
                        if m:
                            store_piece(b, m - 1)
                        load_piece(b, m + 2)
                    if projects and LOW.get(qd) in (1, 3):
                        side = LOW[qd] // 2
                        sp.wait_ge(low_ready, 4 * e + 2 * side + 2)
                        for part in range(2):
                            sp.dma_start(scratch[part, 2 * side:2 * side + 2].rearrange("u p n -> p u n"),
                                         qk[:, part, 2 * side:2 * side + 2, :]).then_inc(spilled, 16)
                if projects:
                    sp.wait_ge(spilled, 64 * e + 64)
                    if attend:
                        sp.wait_ge(st_done, BANKS * c)
                    for side, (tile, parts) in enumerate(((qs, (0, 0, 1, 1)), (ks, (0, 1, 0, 1)))):
                        for r, part in enumerate(parts):
                            sp.dma_start(tile[r * XHD:(r + 1) * XHD, s, :, :],
                                         scratch[part, 2 * side:2 * side + 2].rearrange("u (h d) n -> d (u h) n", d=XHD)
                                         ).then_inc(stacked, 16)
                if maxima:
                    sp.wait_ge(mt_ready, c + 1)
                    sp.dma_start(qs[PB:PR, sn, :, :], mt[:, :]).then_inc(row_loaded, 16)
                if attend:
                    sp.wait_ge(w_low, WP * c + 1)
                    store_piece(b, WP - 1)
            all_turns(sp, turn)
            for k in range(2):
                sp.wait_ge(w_stored[k], 16 * (WP // 2 * B + 1))
                sp.wait_ge(w_loaded[k], 16 * (WP // 3 * B + 1))


class SharedExpert:

    ROUNDS = T // G
    HIDDEN = T // G * IC
    BY_POOL = 2 * IC

    def __init__(self, nc, ctx, name, expert, xn, we_dram, sems, turn, beside):
        self.nc, self.xn, self.turn = nc, xn, turn
        self.units, self.tiles = turn * self.HIDDEN, turn * NT
        sb = lambda n, s, d: ctx.enter_context(nc.sbuf_tensor(f"{name}_{n}", s, d))
        pb = lambda n, s, d: ctx.enter_context(nc.psum_tensor(f"{name}_{n}", s, d))
        pair = sb("pair", [P, 2, WC], F16)
        halves = [(0, EW), (EW, WC)]
        with nc.sbuf_tensor(f"{name}_raw", [P, WC], F32) as raw:
            beside([(we_dram[expert, :, a:b], raw[:, a:b], (pair[:, 0, a:b], pair[:, 1, a:b])) for a, b in halves])
        self.up = pair[:, :, 0:EW].rearrange("p h (c j i) -> p h c j i", c=DC, j=2)
        self.down = pair[:, :, EW:WC].rearrange("p h (c d) -> p h c d", c=IC)
        self.gate = sb("gate", [P, 2, G], F32)
        self.lin = sb("lin", [P, 2, G], F32)
        self.hf = sb("hf", [P, 2, G], F32)
        self.ht = sb("ht", [P, 2, 2, IC, G], F16)
        self.ab = pb("ab", [P, 2, 2, G], F32)
        self.yp = pb("yp", [P, 2, D], F32)
        (self.ab_done, self.lin_done, self.h_high, self.y_done, self.added, self.pool_product, self.pool_low,
         self.dve_product, self.dve_low) = sems
        self.by_pool = 0 if turn else self.BY_POOL

    @staticmethod
    def semaphores(nc, ctx):
        return [ctx.enter_context(nc.semaphore(f"sh_{n}"))
                for n in ("ab_done", "lin_done", "h_high", "y_done", "added", "pool_product", "pool_low",
                          "dve_product", "dve_low")]

    def wait_product(self, engine, n):
        if n < self.by_pool:
            engine.wait_ge(self.pool_product, n + 1)
        else:
            engine.wait_ge(self.dve_product, self.units + n + 1 - self.BY_POOL)

    def wait_low(self, engine, n):
        if n < self.by_pool:
            engine.wait_ge(self.pool_low, n + 1)
        else:
            engine.wait_ge(self.dve_low, self.units + n + 1 - self.BY_POOL)

    def tensor(self, pe, between=lambda g: None):
        nc = self.nc
        if self.turn == 0:
            pe.sem_inc(self.lin_done, 2)

        def hidden(g):
            for c in range(IC):
                n, rows = g * IC + c, I_ROWS[c]
                pe.wait_ge(self.lin_done, self.units + n + 1)
                for j in range(2):
                    last = split_product(nc, self.ab[0:rows, n % 2, j, :],
                                         lambda a, d: self.up[:, a, d, j, c * P:c * P + rows],
                                         lambda b, d: self.xn[:, b, d, g * G:(g + 1) * G], DC)
                last.then_inc(self.ab_done, 1)

        hidden(0)
        for g in range(self.ROUNDS):
            if g + 1 < self.ROUNDS:
                hidden(g + 1)
            between(g)
            self.wait_low(pe, g * IC + IC - 1)
            for t in range(4):
                n = 4 * g + t
                if n >= 2:
                    pe.wait_ge(self.added, self.tiles + n - 1)
                split_product(nc, self.yp[:, n % 2, :],
                              lambda a, c: self.ht[0:I_ROWS[c], g % 2, a, c, t * P:(t + 1) * P],
                              lambda b, c: self.down[0:I_ROWS[c], b, c, :], IC).then_inc(self.y_done, 1)

    def scalar(self, act):
        nc = self.nc
        for n in range(self.HIDDEN):
            g, c, rows, k = n // IC, n % IC, I_ROWS[n % IC], n % 2
            act.wait_ge(self.ab_done, self.units + n + 1)
            if n >= 2:
                self.wait_product(act, n - 2)
            nc.scalar.activation(self.gate[0:rows, k, :], self.ab[0:rows, k, 0, :], ACT.Silu)
            nc.scalar.activation(self.lin[0:rows, k, :], self.ab[0:rows, k, 1, :], ACT.Copy).then_inc(self.lin_done, 1)
            self.wait_product(act, n)
            if g >= 2:
                act.wait_ge(self.y_done, self.tiles + 4 * (g - 1))
            nc.scalar.activation(self.ht[0:rows, g % 2, 0, c, :], self.hf[0:rows, k, :], ACT.Copy
                                 ).then_inc(self.h_high, 1)

    def product(self, engine, compute, n):
        rows, k = I_ROWS[n % IC], n % 2
        engine.wait_ge(self.lin_done, self.units + n + 3)
        if n >= 2:
            self.wait_low(engine, n - 2)
        compute.tensor_tensor(self.hf[0:rows, k, :], self.gate[0:rows, k, :], self.lin[0:rows, k, :],
                              ALU.mult).then_inc(self.pool_product if n < self.by_pool else self.dve_product, 1)

    def low_part(self, engine, compute, n):
        g, c, rows, k = n // IC, n % IC, I_ROWS[n % IC], n % 2
        engine.wait_ge(self.h_high, self.units + n + 1)
        compute.tensor_tensor(self.ht[0:rows, g % 2, 1, c, :], self.hf[0:rows, k, :],
                              self.ht[0:rows, g % 2, 0, c, :], ALU.subtract).then_inc(self.pool_low if n < self.by_pool else self.dve_low, 1)

    def add(self, dve, x_sb, tile):
        dve.wait_ge(self.y_done, self.tiles + tile + 1)
        self.nc.vector.tensor_tensor(x_sb[:, tile, :], self.yp[:, tile % 2, :], x_sb[:, tile, :],
                                     ALU.add).then_inc(self.added, 1)


def route_and_share(nc, split, sems, ident, x_sb, xn, rows, route, wg_dram, we_dram, slot_rows, cleared):
    with ExitStack() as ctx:
        sb = lambda n, s, d: ctx.enter_context(nc.sbuf_tensor(f"ro_{n}", s, d))
        pb = lambda n, s, d: ctx.enter_context(nc.psum_tensor(f"ro_{n}", s, d))
        sem = lambda n: ctx.enter_context(nc.semaphore(f"ro_{n}"))
        raw = sb("raw", [P, DC, E], F32)
        wg = sb("wg", [P, 2, DC, E], F16)
        router = (wg_dram.rearrange("(c p) e -> p c e", p=P), raw[:, :, :], (wg[:, 0], wg[:, 1]))
        normalise = lambda jobs: layer_norm(nc, "fx_ln", x_sb, xn, ident, rows=rows,
                                            before=lambda block: split([router] + jobs, block))
        shared = SharedExpert(nc, ctx, "sh0", E, xn, we_dram, sems, 0, normalise)
        logits = pb("logits", [P, NT, E], F32)
        places = pb("places", [P, 2, NT, E], F32)
        lg = sb("lg", [P, NT, E], F32)
        s = sb("s", [P, NT, E], F32)
        col = sb("col", [P, NT], F32)
        gs = sb("gs", [P, NT, GR], F32)
        cmp = sb("cmp", [P, NT, E, E], BF16)
        eq = sb("eq", [P, NT, E, E], BF16)
        rank = sb("rank", [P, NT, E], F32)
        before = sb("before", [P, E, E], BF16)
        earlier = sb("earlier", [P, P], BF16)
        every = sb("every", [P, P], BF16)
        chosen = sb("chosen", [P, NT, E], F32)
        chosen16 = sb("chosen16", [P, NT, E], BF16)
        tile_base = sb("tile_base", [P, NT + 1, E], F32)
        totals = sb("totals", [P, NT, E], F32)
        counts = sb("counts", [P, E], I32)
        tiles = sb("tiles", [P, E], F32)
        ends = sb("ends", [P, E], F32)
        base = sb("base", [P, E], F32)
        ones = sb("ones", [P, E], F32)
        slot1 = sb("slot1", [P, NT, E], F32)
        top = sb("top", [P, NT, 8], F32)
        hit = sb("hit", [P, NT, E], F32)
        tile_no = sb("tile_no", [1, TILES], F32)
        passed = sb("passed", [1, TILES, E], F32)
        owner = sb("owner", [1, TILES], F32)
        packed = sb("packed", [1, TILES], F32)
        made, logits_ready, shifted, exped, chain = (
            sem("made"), sem("logits_ready"), sem("shifted"), sem("exped"), sem("chain"))
        masks_ready, placed, routed, sent = sem("masks_ready"), sem("placed"), sem("routed"), sem("sent")
        block = ctx.enter_context(nc.Block())

        @block.gpsimd
        def _(pool):
            nc.gpsimd.memset(before[:, :, :], 1.0).then_inc(made, 1)
            nc.gpsimd.memset(earlier[:, :], 1.0).then_inc(made, 1)
            nc.gpsimd.memset(every[:, :], 1.0).then_inc(made, 1)
            nc.gpsimd.iota(tile_no[:, :], pattern=[[1, TILES]], base=0, channel_multiplier=0,
                           allow_small_or_imprecise_dtypes=True).then_inc(made, 1)
            pool.wait_ge(made, 4)
            nc.gpsimd.affine_select(out=before[:, :, :], in_=before[:, :, :], compare_op=ALU.is_gt, fill=0.0,
                                    base=0, pattern=[[1, E], [-1, E]], channel_multiplier=0).then_inc(made, 1)
            nc.gpsimd.affine_select(out=earlier[:, :], in_=earlier[:, :], compare_op=ALU.is_gt, fill=0.0,
                                    base=0, pattern=[[1, P]], channel_multiplier=-1).then_inc(made, 1)
            sends = [(t, k) for t in range(NT) for k in range(TOPK)]
            for n in range(shared.by_pool):
                shared.product(pool, nc.gpsimd, n)
                shared.low_part(pool, nc.gpsimd, n)
            pool.wait_ge(routed, 1)
            for t, k in sends:
                nc.gpsimd.indirect_dma_start(
                    out=slot_rows, out_offset=bass.IndirectOffsetOnAxis(ap=route["index"][:, t, k:k + 1], axis=0),
                    in_=rows[:, t, :, :].rearrange("p h d -> p (h d)"), in_offset=None).then_inc(sent, 16)
            pool.wait_ge(sent, 16 * len(sends))

        @block.tensor
        def _(pe):
            for t in range(NT):
                last = split_product(nc, logits[:, t, :], lambda a, c: xn[:, a, c, t * P:(t + 1) * P],
                                     lambda b, c: wg[:, b, c, :], DC)
            last.then_inc(logits_ready, 1)

            def between(g):
                if g != 0:
                    return
                pe.wait_ge(masks_ready, 1)
                flat = chosen16[:, :, :].rearrange("p t e -> p (t e)")
                nc.tensor.matmul(places[:, 0, :, :].rearrange("p t e -> p (t e)"), earlier[:, :], flat,
                                 start=True, stop=True)
                nc.tensor.matmul(places[:, 1, :, :].rearrange("p t e -> p (t e)"), every[:, :], flat,
                                 start=True, stop=True).then_inc(placed, 1)

            shared.tensor(pe, between)

        @block.vector
        def _(dve):
            link = Chain(dve, chain)
            step = link.then_wait
            over = lambda a, n: a.rearrange("p t (g o) -> p t g o", o=1).to_broadcast([P, NT, n, n])
            dve.wait_ge(logits_ready, 1)
            step(nc.vector.reduce_max(col[:, :], logits[:, :, :], AX.X))
            bc = col[:, :].rearrange("p (t o) -> p t o", o=1).to_broadcast([P, NT, E])
            nc.vector.tensor_tensor(lg[:, :, :], logits[:, :, :], bc, ALU.subtract).then_inc(shifted, 1)
            dve.wait_ge(exped, 1)
            step(nc.vector.reduce_sum(col[:, :], s[:, :, :], AX.X))
            step(nc.vector.reciprocal(col[:, :], col[:, :]))
            step(nc.vector.tensor_tensor(s[:, :, :], s[:, :, :], bc, ALU.mult))
            step(nc.vector.reduce_max(gs[:, :, :], s[:, :, :].rearrange("p t (g e) -> p t g e", g=GR), AX.X))
            dve.wait_ge(made, 6)

            def ranks(v, n):
                c4 = cmp[:, :, 0:n, 0:n]
                e4 = eq[:, :, 0:n, 0:n]
                other = v.rearrange("p t (o g) -> p t o g", o=1).to_broadcast([P, NT, n, n])
                own = over(v, n)
                bf = before[:, 0:n, 0:n].rearrange("p (o a) b -> p o a b", o=1).to_broadcast([P, NT, n, n])
                link(nc.vector.tensor_tensor(c4, other, own, ALU.is_gt))
                step(nc.vector.tensor_tensor(e4, other, own, ALU.is_equal))
                step(nc.vector.tensor_tensor(e4, e4, bf, ALU.mult))
                step(nc.vector.tensor_tensor(c4, c4, e4, ALU.add))
                step(nc.vector.reduce_sum(rank[:, :, 0:n], c4, AX.X))

            ranks(gs[:, :, :], GR)
            step(nc.vector.tensor_scalar(gs[:, :, :], rank[:, :, 0:GR], float(TOPK_G), None, ALU.is_lt))
            gb = gs[:, :, :].rearrange("p t (g o) -> p t g o", o=1).to_broadcast([P, NT, GR, EG])
            l4 = lg[:, :, :].rearrange("p t (g e) -> p t g e", g=GR)
            step(nc.vector.tensor_tensor(l4, s[:, :, :].rearrange("p t (g e) -> p t g e", g=GR), gb, ALU.mult))
            step(nc.vector.tensor_scalar(gs[:, :, :], gs[:, :, :], -1.0, None, ALU.add))
            step(nc.vector.tensor_tensor(l4, l4, gb, ALU.add))
            ranks(lg[:, :, :], E)
            step(nc.vector.tensor_scalar(chosen[:, :, :], rank[:, :, :], float(TOPK), None, ALU.is_lt))
            nc.vector.tensor_copy(chosen16[:, :, :], chosen[:, :, :]).then_inc(masks_ready, 1)
            link(nc.vector.memset(tile_base[:, 0, :], 0.0))
            step(nc.vector.memset(ones[:, :], 1.0))
            dve.wait_ge(placed, 1)
            step(nc.vector.tensor_copy(totals[:, :, :], places[:, 1, :, :]))
            for t in range(NT):
                step(nc.vector.tensor_tensor(tile_base[:, t + 1, :], tile_base[:, t, :], totals[:, t, :], ALU.add))
            step(nc.vector.tensor_scalar(counts[:, :], tile_base[:, NT, :], float(P - 1), None, ALU.add))
            step(nc.vector.tensor_scalar(counts[:, :], counts[:, :], 7, None, ALU.arith_shift_right))
            step(nc.vector.tensor_copy(tiles[:, :], counts[:, :]))
            step(nc.vector.tensor_scalar(tiles[:, :], tiles[:, :], 1.0, None, ALU.max))
            step(nc.vector.tensor_tensor_scan(ends[:, :], ones[:, :], tiles[:, :], 0.0, ALU.mult, ALU.add))
            step(nc.vector.tensor_tensor(base[:, :], ends[:, :], tiles[:, :], ALU.subtract))
            step(nc.vector.tensor_scalar(base[:, :], base[:, :], float(P), 1.0, ALU.mult, ALU.add))
            step(nc.vector.tensor_tensor(slot1[:, :, :], places[:, 0, :, :], tile_base[:, 0:NT, :], ALU.add))
            step(nc.vector.tensor_tensor(slot1[:, :, :], slot1[:, :, :],
                                         base[:, :].rearrange("p (o e) -> p o e", o=1).to_broadcast([P, NT, E]), ALU.add))
            step(nc.vector.tensor_tensor(slot1[:, :, :], slot1[:, :, :], chosen[:, :, :], ALU.mult))
            for t in range(NT):
                link(nc.vector.max(top[:, t, :], slot1[:, t, :]))
            dve.wait_ge(chain, link.n)
            step(nc.vector.tensor_scalar(route["index"][:, :, :], top[:, :, 0:TOPK], -1.0, None, ALU.add))
            nc.vector.memset(hit[:, :, :], 0.0).then_inc(routed, 1)
            for t in range(4):
                shared.add(dve, x_sb, t)
            dve.wait_ge(routed, 1)
            for k in range(TOPK):
                tk = top[:, :, k:k + 1].to_broadcast([P, NT, E])
                step(nc.vector.tensor_tensor(hit[:, :, :], slot1[:, :, :], tk, ALU.is_equal))
                step(nc.vector.tensor_tensor(hit[:, :, :], hit[:, :, :], s[:, :, :], ALU.mult))
                step(nc.vector.reduce_sum(route["weight"][:, :, k], hit[:, :, :], AX.X))
            step(nc.vector.tensor_copy(route["ends"][:, :], ends[0:1, :]))
            step(nc.vector.tensor_tensor(
                passed[:, :, :], tile_no[:, :].rearrange("p (t o) -> p t o", o=1).to_broadcast([1, TILES, E]),
                ends[0:1, :].rearrange("p (o e) -> p o e", o=1).to_broadcast([1, TILES, E]), ALU.is_ge))
            step(nc.vector.reduce_sum(owner[:, :], passed[:, :, :], AX.X))
            step(nc.vector.tensor_scalar(owner[:, :], owner[:, :], float(E - 1), None, ALU.min))
            step(nc.vector.scalar_tensor_tensor(packed[:, 0:TILES - 2], owner[:, 2:TILES], float(OWNER),
                                                owner[:, 1:TILES - 1], ALU.mult, ALU.add))
            step(nc.vector.scalar_tensor_tensor(packed[:, 0:TILES - 2], packed[:, 0:TILES - 2], float(OWNER),
                                                owner[:, 0:TILES - 2], ALU.mult, ALU.add))
            step(nc.vector.tensor_copy(route["owners"][:, 0:TILES - 2], packed[:, 0:TILES - 2]))
            step(nc.vector.tensor_scalar(route["pairs"][:, :], ends[0:1, E - 1:E], 1.0, None, ALU.add))
            step(nc.vector.tensor_scalar(route["pairs"][:, :], route["pairs"][:, :], 1, None, ALU.arith_shift_right))
            for g in range(1, shared.ROUNDS):
                for n in range(g * IC + IC, min(g * IC + 2 * IC, shared.HIDDEN)):
                    shared.product(dve, nc.vector, n)
                    shared.low_part(dve, nc.vector, n)
                for t in range(4 * g, 4 * g + 4):
                    shared.add(dve, x_sb, t)

        @block.scalar
        def _(act):
            act.wait_ge(shifted, 1)
            nc.scalar.activation(s[:, :, :], lg[:, :, :], ACT.Exp).then_inc(exped, 1)
            shared.scalar(act)


def routed_experts(nc, ident, route, we_pairs, slot_rows, slot_outs, jobs):
    with ExitStack() as ctx:
        sb = lambda n, s, d: ctx.enter_context(nc.sbuf_tensor(f"re_{n}", s, d))
        pb = lambda n, s, d: ctx.enter_context(nc.psum_tensor(f"re_{n}", s, d))
        sem = lambda n: ctx.enter_context(nc.semaphore(f"re_{n}"))
        w = sb("w", [P, 2, 2, WC], F16)
        up = w[:, :, :, 0:EW].rearrange("p s h (c j i) -> p s h c j i", c=DC, j=2)
        down = w[:, :, :, EW:WC].rearrange("p s h (c d) -> p s h c d", c=IC)
        xr = sb("xr", [P, 2, 2 * D], F16)
        xt = sb("xt", [P, 2, 2 * DC, P], F16)
        gate = sb("gate", [P, 2, I], F32)
        hf = sb("hf", [P, 2, I], F32)
        hp = sb("hp", [P, 2, 2, I], F16)
        ht = sb("ht", [P, 2, 2 * IC, P], F16)
        ys = sb("ys", [P, 2, D], F32)
        waited = sb("waited", [P, 4], F32)
        ab = pb("ab", [P, 2, 2, G], F32)
        xt_ps = pb("xt_ps", [P, 2 * DC, P], F16)
        ht_ps = pb("ht_ps", [P, 2 * DC, P], F16)
        yp = pb("yp", [P, 2, D], F32)
        w_loaded, jobs_loaded, jobs_done = sem("w_loaded"), sem("jobs_loaded"), sem("jobs_done")
        x_loaded, y_stored = [sem("x_loaded0"), sem("x_loaded1")], [sem("y_stored0"), sem("y_stored1")]
        x_turned, xt_ready, ab_done, gate_ready, h_ready = (
            sem("x_turned"), sem("xt_ready"), sem("ab_done"), sem("gate_ready"), sem("h_ready"))
        h_high, h_low, h_turned, ht_ready, y_done, ys_ready, clean = (
            sem("h_high"), sem("h_low"), sem("h_turned"), sem("ht_ready"), sem("y_done"), sem("ys_ready"), sem("clean"))
        block = ctx.enter_context(nc.Block())

        def turns(engine):
            return engine.value_load(route["pairs"][0:1, 0:1], min_val=1, max_val=(TILES - 4) // 2)

        @block.sync
        def _(sp):
            def load(e, slot):
                sp.dma_start(w[:, slot, :, :], we_pairs[e]).then_inc(w_loaded, 16)

            load(0, 0)
            sp.wait_ge(w_loaded, 16)
            load(1, 1)
            for dram, raw, _pair in jobs:
                sp.dma_start(raw, dram).then_inc(jobs_loaded, 16)
            with sp.Fori(1, E // 2) as i:
                for k in range(2):
                    sp.wait_ge(w_loaded, 32 * i + 16 * k)
                    done = sp.value_load(route["ends"][0:1, bass.ds(2 * i + k - 2, 1)], min_val=0, max_val=TILES)
                    sp.wait_ge(y_done, done + 2)
                    load(2 * i + k, k)
            sp.wait_ge(w_loaded, 16 * E)

        @block.gpsimd
        def _(pool):
            pool.wait_ge(jobs_loaded, 16 * len(jobs))
            for n, (_dram, raw, pair) in enumerate(jobs):
                nc.gpsimd.tensor_copy(pair[0], raw).then_inc(jobs_done, 1)
                pool.wait_ge(jobs_done, n + 1)
                nc.gpsimd.tensor_tensor(pair[1], raw, pair[0], ALU.subtract)

        @block.tensor
        def _(pe):
            pe.sem_inc(y_done, 2)
            pe.sem_inc(h_ready, 1)

            def turn_rows(s, bank_free, arrived):
                pe.wait_ge(x_loaded[s], arrived)
                if bank_free is not None:
                    pe.wait_ge(xt_ready, bank_free)
                for c in range(2 * DC):
                    last = nc.tensor.transpose(xt_ps[:, c, :], xr[:, s, c * P:(c + 1) * P], ident[:, :])
                last.then_inc(x_turned, 1)

            def hidden(s, slot, arrived, tile):
                pe.wait_ge(w_loaded, arrived)
                pe.wait_ge(xt_ready, tile + 1)
                pe.wait_ge(h_ready, tile)
                for j in range(2):
                    last = split_product(
                        nc, ab[:, s, j, 0:I], lambda a, c: xt[:, s, a * DC + c, :],
                        lambda b, c: up[:, bass.ds(slot, 1), b, c, j, :].rearrange("p o i -> p (o i)"), DC)
                last.then_inc(ab_done, 1)

            def turn_hidden(s, tile):
                pe.wait_ge(h_low, tile + 1)
                pe.wait_ge(ht_ready, tile + 1)
                for h in range(2):
                    for c in range(IC):
                        last = nc.tensor.transpose(ht_ps[0:I_ROWS[c], h * IC + c, :],
                                                   hp[:, s, h, c * P:c * P + I_ROWS[c]], ident[:, :])
                last.then_inc(h_turned, 1)

            def output(s, slot, tile):
                pe.wait_ge(ht_ready, tile + 2)
                pe.wait_ge(ys_ready, tile + 1)
                split_product(
                    nc, yp[:, s, :], lambda a, c: ht[0:I_ROWS[c], s, a * IC + c, :],
                    lambda b, c: down[0:I_ROWS[c], bass.ds(slot, 1), b, c, :].rearrange("p o d -> p (o d)"), IC
                ).then_inc(y_done, 1)

            slot_of = lambda owners, d: (owners >> (4 * d)) & 1
            arrival_of = lambda owners, d: ((owners >> (4 * d)) & (OWNER - 1)) * 16 + 16

            n = turns(pe)
            turn_rows(0, None, 16)
            pe.wait_ge(clean, 1)
            owners = pe.value_load(route["owners"][0:1, 0:1], min_val=0, max_val=OWNER ** 3 - 1)
            first = slot_of(owners, 0)
            pe.wait_ge(w_loaded, arrival_of(owners, 0))
            pe.wait_ge(xt_ready, 1)
            for j in range(2):
                last = split_product(
                    nc, ab[:, 0, j, 0:I], lambda a, c: xt[:, 0, a * DC + c, :],
                    lambda b, c: up[:, bass.ds(first, 1), b, c, j, :].rearrange("p o i -> p (o i)"), DC)
            last.then_inc(ab_done, 1)
            turn_rows(1, 1, 16)
            with pe.Fori(0, n) as i:
                owners = pe.value_load(route["owners"][0:1, bass.ds(2 * i, 1)], min_val=0, max_val=OWNER ** 3 - 1)
                at = [slot_of(owners, d) for d in range(3)]
                arrived = [arrival_of(owners, d) for d in (1, 2)]
                for s in range(2):
                    tile = 2 * i + s
                    hidden(1 - s, at[s + 1], arrived[s], tile + 1)
                    turn_hidden(s, tile)
                    turn_rows(s, tile + 2, 16 * i + 32)
                    output(s, at[s], tile)

        @block.scalar
        def _(act):
            def load(s, tile):
                act.dma_start(xr[:, s, :], slot_rows.rearrange("(t p) n -> t p n", p=P)[tile]
                              ).then_inc(x_loaded[s], 16)

            def keep_rows(s, tile):
                act.wait_ge(x_turned, tile + 1)
                nc.scalar.activation(xt[:, s, :, :], xt_ps[:, :, :], ACT.Copy).then_inc(xt_ready, 1)

            load(0, 0)
            load(1, 1)
            n = turns(act)
            for s in range(2):
                keep_rows(s, s)
                load(s, s + 2)
            with act.Fori(0, n) as i:
                for s in range(2):
                    tile = 2 * i + s
                    act.wait_ge(ab_done, tile + 1)
                    nc.scalar.activation(gate[:, s, :], ab[:, s, 0, 0:I], ACT.Silu).then_inc(gate_ready, 1)
                    act.wait_ge(h_ready, tile + 2)
                    nc.scalar.activation(hp[:, s, 0, :], hf[:, s, :], ACT.Copy).then_inc(h_high, 1)
                    keep_rows(s, tile + 2)
                    load(s, tile + 4)
                    act.wait_ge(ys_ready, tile + 3)
                    act.dma_start(slot_outs.rearrange("(t p) n -> t p n", p=P)[tile], ys[:, s, :]
                                  ).then_inc(y_stored[s], 16)

        @block.vector
        def _(dve):
            dve.sem_inc(ht_ready, 1)
            dve.sem_inc(ys_ready, 2)
            for s in range(2):
                dve.sem_inc(y_stored[s], 16)
            nc.vector.memset(ht_ps[:, :, :].rearrange("p c n -> p (c n)").bitcast(F32), 0.0).then_inc(clean, 1)
            n = turns(dve)
            with dve.Fori(0, n) as i:
                for s in range(2):
                    tile = 2 * i + s
                    dve.wait_ge(gate_ready, tile + 1)
                    nc.vector.tensor_tensor(hf[:, s, :], ab[:, s, 1, 0:I], gate[:, s, :], ALU.mult).then_inc(h_ready, 1)
                    dve.wait_ge(h_high, tile + 1)
                    nc.vector.tensor_tensor(hp[:, s, 1, :], hf[:, s, :], hp[:, s, 0, :], ALU.subtract).then_inc(h_low, 1)
                    dve.wait_ge(h_turned, tile + 1)
                    dve.wait_ge(y_done, tile + 1)
                    nc.vector.tensor_copy(ht[:, s, :, :], ht_ps[:, 0:2 * IC, :]).then_inc(ht_ready, 1)
                    dve.wait_ge(y_done, tile + 3)
                    dve.wait_ge(y_stored[s], 16 * i + 16)
                    nc.vector.tensor_copy(ys[:, s, :], yp[:, s, :]).then_inc(ys_ready, 1)
            for s in range(2):
                dve.wait_ge(y_stored[s], 16 * n + 16)
                nc.vector.memset(waited[:, 2 * s:2 * s + 1], 0.0)
                dve.wait_ge(x_loaded[s], 16 * n + 32)
                nc.vector.memset(waited[:, 2 * s + 1:2 * s + 2], 0.0)


def combine_and_share(nc, sems, x_sb, xn, route, we_dram, slot_outs, out_dram, routed):
    RING = 8
    with ExitStack() as ctx:
        sb = lambda n, s, d: ctx.enter_context(nc.sbuf_tensor(f"co_{n}", s, d))
        sem = lambda n: ctx.enter_context(nc.semaphore(f"co_{n}"))
        shared = SharedExpert(nc, ctx, "sh1", E + 1, xn, we_dram, sems, 1, routed)
        yg = sb("yg", [P, RING, D], F32)
        fetched = [sem(f"fetched{r}") for r in range(RING)]
        used, ready, stored = sem("used"), sem("ready"), sem("stored")
        fetches = [(t, k) for t in range(NT) for k in range(TOPK)]
        block = ctx.enter_context(nc.Block())

        @block.gpsimd
        def _(pool):
            for m, (t, k) in enumerate(fetches):
                if m >= RING:
                    pool.wait_ge(used, m - RING + 1)
                nc.gpsimd.indirect_dma_start(
                    out=yg[:, m % RING, :], out_offset=None, in_=slot_outs,
                    in_offset=bass.IndirectOffsetOnAxis(ap=route["index"][:, t, k:k + 1], axis=0)
                ).then_inc(fetched[m % RING], 16)

        @block.tensor
        def _(pe):
            shared.tensor(pe)

        @block.scalar
        def _(act):
            shared.scalar(act)

        @block.vector
        def _(dve):
            def combine(count):
                for m in order[:count]:
                    t, k = fetches[m]
                    dve.wait_ge(fetched[m % RING], 16 * (m // RING + 1))
                    nc.vector.scalar_tensor_tensor(x_sb[:, t, :], yg[:, m % RING, :], route["weight"][:, t, k:k + 1],
                                                   x_sb[:, t, :], ALU.mult, ALU.add).then_inc(used, 1)
                    dve.wait_ge(used, m + 1)
                del order[:count]

            order = list(range(len(fetches)))
            for g in range(shared.ROUNDS + 1):
                for n in range(g * IC, min(g * IC + IC, shared.HIDDEN)):
                    shared.product(dve, nc.vector, n)
                    combine(3)
                    shared.low_part(dve, nc.vector, n)
                    combine(3)
                if g >= 1:
                    for t in range(4 * g - 4, 4 * g):
                        dve.wait_ge(used, len(fetches) - len(order))
                        shared.add(dve, x_sb, t)
                        dve.wait_ge(shared.added, shared.tiles + t + 1)
            combine(len(order))

        @block.sync
        def _(sp):
            for t in range(0, NT, 4):
                sp.wait_ge(used, TOPK * (t + 4))
                sp.wait_ge(shared.added, shared.tiles + t + 4)
                sp.dma_start(out_dram[t:t + 4].rearrange("t p d -> p t d"), x_sb[:, t:t + 4, :]).then_inc(stored, 16)
            sp.wait_ge(stored, 16 * (NT // 4))


def decoder_block(nc, a):
    with ExitStack() as ctx:
        sb = lambda n, s, d: ctx.enter_context(nc.sbuf_tensor(n, s, d))
        x_sb = sb("x_sb", [P, NT, D], F32)
        ident = sb("ident", [P, P], F16)
        made = ctx.enter_context(nc.semaphore("ident_made"))
        split = WeightSplit(nc, ctx)
        cleared = ctx.enter_context(nc.semaphore("cleared"))
        we_pairs = nc.dram_tensor("we_pairs", (E, P, 2, WC), F16).ap()
        slot_rows = nc.dram_tensor("slot_rows", (TILES * P, 2 * D), F16).ap()
        slot_outs = nc.dram_tensor("slot_outs", (TILES * P, D), F32).ap()
        with nc.Block() as block:
            @block.gpsimd
            def _(pool):
                nc.gpsimd.memset(ident[:, :], 0.0).then_inc(made, 1)
                pool.wait_ge(made, 1)
                nc.gpsimd.affine_select(out=ident[:, :], in_=ident[:, :], compare_op=ALU.not_equal, fill=1.0,
                                        base=0, pattern=[[-1, P]], channel_multiplier=1).then_inc(made, 1)
        self_attention(nc, split, x_sb, ident, a["x"], a["wqkv"], a["wout"], slot_rows, slot_outs, cleared)
        cross_attention(nc, split, x_sb, a["ctx"], a["enc"], a["wx"], a["bx"], a["bv"], a["wm"], a["bm"], a["we"], we_pairs)
        with ExitStack() as ffn:
            sf = lambda n, s, d: ffn.enter_context(nc.sbuf_tensor(n, s, d))
            xn = sf("fx_xn", [P, 2, DC, T], F16)
            sems = SharedExpert.semaphores(nc, ffn)
            route = {
                "index": sf("fx_index", [P, NT, TOPK], I32),
                "weight": sf("fx_weight", [P, NT, TOPK], F32),
                "owners": sf("fx_owners", [1, TILES], I32),
                "ends": sf("fx_ends", [1, E], I32),
                "pairs": sf("fx_pairs", [1, 1], I32),
            }
            with nc.sbuf_tensor("fx_rows", [P, NT, 2, D], F16) as rows:
                route_and_share(nc, split, sems, ident, x_sb, xn, rows, route, a["wg"], a["we"], slot_rows, cleared)
            combine_and_share(nc, sems, x_sb, xn, route, a["we"], slot_outs, a["out"],
                              lambda jobs: routed_experts(nc, ident, route, we_pairs, slot_rows, slot_outs, jobs))


def laid_out(inputs):
    get = lambda k: np.asarray(inputs[k])
    heads = lambda m: m.reshape(XHD, H, *m.shape[1:]).swapaxes(0, 1).reshape(CH, *m.shape[1:])
    pad = lambda m, axis: np.concatenate(
        [m, np.zeros([IP - I if n == axis else s for n, s in enumerate(m.shape)], m.dtype)], axis)
    wx = np.stack([heads(get(f"L0_xattn_W{s}")).T for s in "qkv"])
    bx = np.concatenate([heads(get(f"L0_xattn_b{s}")).reshape(CC, P) for s in "qk"]).T
    wm = np.zeros((4, P, CH), np.float32)
    wm.reshape(4, 4, 2, XHD, CH)[:, :, 0] = heads(get("L0_xattn_Wm").T).reshape(4, 4, XHD, CH)
    both = lambda routed, shared: np.concatenate([routed, shared.reshape(SH, I, D)])
    up = np.stack([both(get(f"L0_ffn_W{n}"), get(f"L0_ffn_Ws{n}")) for n in (1, 3)], 1)
    up = up.reshape(EA, 2, I, DC, P).transpose(0, 4, 3, 1, 2).reshape(EA, P, EW)
    w2s = get("L0_ffn_Ws2").T.reshape(SH, I, D)
    down = pad(np.concatenate([get("L0_ffn_W2").swapaxes(1, 2), w2s]), 1)
    down = down.reshape(EA, IC, P, D).transpose(0, 2, 1, 3).reshape(EA, P, IC * D)
    out = {
        "x": get("x").reshape(NT, P, D),
        "ctx": get("ctx_2048").reshape(NT, P, D),
        "wqkv": get("L0_attn_w_qkv").T,
        "wout": get("L0_attn_w_out").T,
        "enc": get("L0_xattn_encoding").reshape(2, G, XHD).swapaxes(1, 2),
        "wx": wx,
        "bx": bx,
        "bv": np.repeat(heads(get("L0_xattn_bv"))[None], P, 0),
        "wm": wm,
        "bm": get("L0_xattn_bm").reshape(CC, P).T,
        "wg": get("L0_ffn_Wg").T,
        "we": np.concatenate([up, down], 2),
    }
    return {k: np.ascontiguousarray(v) for k, v in out.items()}


def kernel(**inputs):
    import concourse.bacc as bacc
    from concourse.bass_utils import run_bass_kernel_spmd

    nc = bacc.Bacc("TRN2", target_bir_lowering=False, num_devices=1)
    arrays = {f"in_{k}": v for k, v in laid_out(inputs).items()}
    args = {k[3:]: nc.dram_tensor(k, v.shape, mybir.dt.from_np(v.dtype), kind="ExternalInput").ap()
            for k, v in arrays.items()}
    args["out"] = nc.dram_tensor("out", (NT, P, D), F32, kind="ExternalOutput").ap()
    decoder_block(nc, args)
    r = run_bass_kernel_spmd(nc, [arrays], core_ids=[0])
    return r.results[0]["out"].reshape(B, S, D)
```
